# Optimizing a Trainium2 kernel written in Bass

```python
import numpy as np
import jax
import jax.numpy as jnp

def _softmax(x, axis=-1):
    return jax.nn.softmax(x, axis=axis)

def _gelu(x):
    return jax.nn.gelu(x, approximate=True)

def _silu(x):
    return jax.nn.silu(x)

def _sigmoid(x):
    return jax.nn.sigmoid(x)

def _layernorm(x, axis=-1, eps=1e-05):
    m = jnp.mean(x, axis=axis, keepdims=True)
    v = jnp.var(x, axis=axis, keepdims=True)
    return (x - m) / jnp.sqrt(v + eps)

def _scatter_add(tgt, idx, src, axis=0):
    return tgt.at[idx].add(src)

def _segment_sum(src, seg, n):
    return jax.ops.segment_sum(src, seg, n)
kernel_name = 'mk_gnn_preln_d2_gnn_r32_5f8c25'

def setup_inputs(seed: int=0):
    np.random.seed(seed)
    _w = jnp.asarray

    def _rec_inputs():
        import jax
        import jax.numpy as jnp
        _gk = jax.random.key(seed)
        x = -0.0003713 + 1 * jax.random.normal(jax.random.fold_in(_gk, 1), (50000, 256), jnp.float32)
        _s = jax.random.randint(jax.random.fold_in(_gk, 2), (12500,), 0, 50000, jnp.int32)
        _d = jax.random.randint(jax.random.fold_in(_gk, 3), (12500,), 0, 50000, jnp.int32)
        _loop = jnp.arange(50000, dtype=jnp.int32)
        src = jnp.concatenate([_s, _d, _loop])
        dst = jnp.concatenate([_d, _s, _loop])
        _o = jnp.argsort(dst, stable=True)
        src = src[_o]
        dst = dst[_o]
        return (x, src, dst)
    x, src, dst = _rec_inputs()

    def _L0_gnn_setup():
        import jax, jax.numpy as jnp
        import numpy as np
        N_NODES = 50000
        N_EDGES = 25000
        FEATURES = 256
        HEADS = 8
        HEAD_DIM = FEATURES // HEADS
        LAYERS = 3
        NEG_SLOPE_ATTN = 0.2
        NEG_SLOPE_ACT = 0.01

        def _gat_layer(x, W, al, ar, b, src, dst, apply_act):
            h = (x @ W).reshape(N_NODES, HEADS, HEAD_DIM)
            el = jnp.einsum('nhd,hd->nh', h, al)
            er = jnp.einsum('nhd,hd->nh', h, ar)
            e = jax.nn.leaky_relu(el[src] + er[dst], negative_slope=NEG_SLOPE_ATTN)
            m = jax.ops.segment_max(e, dst, num_segments=N_NODES)
            ex = jnp.exp(e - m[dst])
            s = jax.ops.segment_sum(ex, dst, num_segments=N_NODES)
            a = ex / s[dst]
            msg = h[src] * a[:, :, None]
            out = jax.ops.segment_sum(msg, dst, num_segments=N_NODES)
            out = out + b.reshape(1, HEADS, HEAD_DIM)
            out = out.reshape(N_NODES, FEATURES)
            if apply_act:
                out = jax.nn.leaky_relu(out, negative_slope=NEG_SLOPE_ACT)
            return out
        key = jax.random.key(seed)
        ks = jax.random.split(key, 7)
        x = jax.random.normal(ks[0], (N_NODES, FEATURES), dtype=jnp.float32)
        src = jax.random.randint(ks[1], (N_EDGES,), 0, N_NODES, dtype=jnp.int32)
        dst = jax.random.randint(ks[2], (N_EDGES,), 0, N_NODES, dtype=jnp.int32)
        W = jax.random.normal(ks[3], (LAYERS, FEATURES, FEATURES), dtype=jnp.float32) / np.sqrt(FEATURES)
        al = jax.random.normal(ks[4], (LAYERS, HEADS, HEAD_DIM), dtype=jnp.float32) * 0.1
        ar = jax.random.normal(ks[5], (LAYERS, HEADS, HEAD_DIM), dtype=jnp.float32) * 0.1
        b = jnp.zeros((LAYERS, FEATURES), dtype=jnp.float32)
        return {'x': x, 'src': src, 'dst': dst, 'W': W, 'al': al, 'ar': ar, 'b': b}
    _L0_gnn_all = _L0_gnn_setup()
    _L0_gnn_in = {k: v for k, v in _L0_gnn_all.items() if k in ('W', 'al', 'ar', 'b')}
    del _L0_gnn_all

    def _L1_gnn_setup():
        import jax, jax.numpy as jnp
        import numpy as np
        HIDDEN = 256
        HEADS = 8
        HEAD_DIM = HIDDEN // HEADS
        N_NODES = 50000
        N_EDGES = 25000
        key = jax.random.key(seed)
        ks = jax.random.split(key, 12)
        h = jax.random.normal(ks[0], (N_NODES, HIDDEN), dtype=jnp.float32)
        row = jax.random.randint(ks[1], (N_EDGES,), 0, N_NODES, dtype=jnp.int64 if jax.config.jax_enable_x64 else jnp.int32)
        col = jax.random.randint(ks[2], (N_EDGES,), 0, N_NODES, dtype=jnp.int64 if jax.config.jax_enable_x64 else jnp.int32)

        def lin(kw, kb):
            W = jax.random.normal(kw, (HIDDEN, HIDDEN), dtype=jnp.float32) * 0.02
            b = jax.random.normal(kb, (HIDDEN,), dtype=jnp.float32) * 0.02
            return (W, b)
        Wq, bq = lin(ks[3], ks[4])
        Wk, bk = lin(ks[5], ks[6])
        Wv, bv = lin(ks[7], ks[8])
        Wo, bo = lin(ks[9], ks[10])
        return {'h': h, 'row': row, 'col': col, 'Wq': Wq, 'bq': bq, 'Wk': Wk, 'bk': bk, 'Wv': Wv, 'bv': bv, 'Wo': Wo, 'bo': bo}
    _L1_gnn_all = _L1_gnn_setup()
    _L1_gnn_in = {k: v for k, v in _L1_gnn_all.items() if k in ('Wq', 'bq', 'Wk', 'bk', 'Wv', 'bv', 'Wo', 'bo')}
    del _L1_gnn_all
    return {'x': x, 'src': src, 'dst': dst, 'L0_gnn_W': _L0_gnn_in['W'], 'L0_gnn_al': _L0_gnn_in['al'], 'L0_gnn_ar': _L0_gnn_in['ar'], 'L0_gnn_b': _L0_gnn_in['b'], 'L1_gnn_Wq': _L1_gnn_in['Wq'], 'L1_gnn_bq': _L1_gnn_in['bq'], 'L1_gnn_Wk': _L1_gnn_in['Wk'], 'L1_gnn_bk': _L1_gnn_in['bk'], 'L1_gnn_Wv': _L1_gnn_in['Wv'], 'L1_gnn_bv': _L1_gnn_in['bv'], 'L1_gnn_Wo': _L1_gnn_in['Wo'], 'L1_gnn_bo': _L1_gnn_in['bo']}

def reference(x, src, dst, L0_gnn_W, L0_gnn_al, L0_gnn_ar, L0_gnn_b, L1_gnn_Wq, L1_gnn_bq, L1_gnn_Wk, L1_gnn_bk, L1_gnn_Wv, L1_gnn_bv, L1_gnn_Wo, L1_gnn_bo):
    import jax
    import jax.numpy as jnp

    def _L0_gnn_ref(x, src, dst, W, al, ar, b):
        import jax, jax.numpy as jnp
        import numpy as np
        N_NODES = 50000
        N_EDGES = 25000
        FEATURES = 256
        HEADS = 8
        HEAD_DIM = FEATURES // HEADS
        LAYERS = 3
        NEG_SLOPE_ATTN = 0.2
        NEG_SLOPE_ACT = 0.01

        def _gat_layer(x, W, al, ar, b, src, dst, apply_act):
            h = (x @ W).reshape(N_NODES, HEADS, HEAD_DIM)
            el = jnp.einsum('nhd,hd->nh', h, al)
            er = jnp.einsum('nhd,hd->nh', h, ar)
            e = jax.nn.leaky_relu(el[src] + er[dst], negative_slope=NEG_SLOPE_ATTN)
            m = jax.ops.segment_max(e, dst, num_segments=N_NODES)
            ex = jnp.exp(e - m[dst])
            s = jax.ops.segment_sum(ex, dst, num_segments=N_NODES)
            a = ex / s[dst]
            msg = h[src] * a[:, :, None]
            out = jax.ops.segment_sum(msg, dst, num_segments=N_NODES)
            out = out + b.reshape(1, HEADS, HEAD_DIM)
            out = out.reshape(N_NODES, FEATURES)
            if apply_act:
                out = jax.nn.leaky_relu(out, negative_slope=NEG_SLOPE_ACT)
            return out
        for i in range(LAYERS):
            x = _gat_layer(x, W[i], al[i], ar[i], b[i], src, dst, apply_act=i + 1 < LAYERS)
        return x

    def _L1_gnn_ref(h, row, col, Wq, bq, Wk, bk, Wv, bv, Wo, bo):
        import jax, jax.numpy as jnp
        import numpy as np
        HIDDEN = 256
        HEADS = 8
        HEAD_DIM = HIDDEN // HEADS
        N_NODES = 50000
        N_EDGES = 25000
        N = h.shape[0]
        scaling = HEAD_DIM ** (-0.5)
        q = (h @ Wq.T + bq).reshape(N, HEAD_DIM, HEADS) * scaling
        k = (h @ Wk.T + bk).reshape(N, HEAD_DIM, HEADS)
        v = (h @ Wv.T + bv).reshape(N, HEAD_DIM, HEADS)
        s = jnp.einsum('edh,edh->eh', q[row], k[col])
        m = jax.ops.segment_max(s, row, num_segments=N)
        e = jnp.exp(s - m[row])
        z = jax.ops.segment_sum(e, row, num_segments=N)
        attn = e / z[row]
        out = jax.ops.segment_sum(attn[:, None, :] * v[col], row, num_segments=N)
        return out.reshape(N, -1) @ Wo.T + bo
    h = jnp.maximum(_layernorm(x, axis=-1), 0.0)
    x = x + _L0_gnn_ref(h, src, dst, L0_gnn_W, L0_gnn_al, L0_gnn_ar, L0_gnn_b)
    h = jnp.maximum(_layernorm(x, axis=-1), 0.0)
    x = x + _L1_gnn_ref(h, src, dst, L1_gnn_Wq, L1_gnn_bq, L1_gnn_Wk, L1_gnn_bk, L1_gnn_Wv, L1_gnn_bv, L1_gnn_Wo, L1_gnn_bo)
    return x

_drawn_inputs = setup_inputs


def setup_inputs(seed=0):
    import zlib

    import numpy as np

    out = dict(_drawn_inputs(seed))
    spreads = {'L0_gnn_b': (0.0, 0.1)}
    factors = {'L0_gnn_al': 3.532,
     'L0_gnn_ar': 31.626,
     'L1_gnn_Wq': 23.54,
     'L1_gnn_bq': 64.0,
     'L1_gnn_Wk': 23.431,
     'L1_gnn_bk': 64.0,
     'L1_gnn_bv': 8.0,
     'L1_gnn_bo': 2.899}
    for name, (base, spread) in spreads.items():
        noise = np.random.default_rng([zlib.crc32(name.encode()), seed]).standard_normal(out[name].shape)
        drawn = base * np.exp(spread * noise) if base else spread * noise
        out[name] = jnp.asarray(drawn.astype(out[name].dtype))
    for name, factor in factors.items():
        out[name] = (out[name] * factor).astype(out[name].dtype)
    return out
```

```python
import concourse.bass as bass
from concourse import mybir
from contextlib import ExitStack

F32 = mybir.dt.float32
BF16 = mybir.dt.bfloat16
I32 = mybir.dt.int32
ALU = mybir.AluOpType
ACT = mybir.ActivationFunctionType
AX = mybir.AxisListType

N = 50000
E = 75000
F = 256
HEADS = 8
HD = F // HEADS
P = 128
BATCH = 7
NBK = 392
NBATCH = NBK // BATCH
ROW = F + HEADS
SLOTS = 2
SP_ROWS = P * NBK * SLOTS
T = 588
U = 7
NO_KEY = P
NO_NODE = N


class Chain:

    def __init__(self, eng, sem, per=0, turn=0, base=0):
        self.eng, self.sem, self.per, self.k = eng, sem, per, 0
        self.at = turn * per + base if per else base

    def done(self, ins):
        self.k += 1
        ins.then_inc(self.sem, 1)
        return self.at + self.k

    def link(self, ins):
        self.eng.wait_ge(self.sem, self.done(ins))

    def close(self):
        assert self.k == self.per, f"a turn has {self.k} increments, not {self.per}"


class Scope:

    def __init__(self, nc, ctx, tag):
        self.nc, self.ctx, self.tag, self.sems = nc, ctx, tag, []
        ctx.callback(self.clear)

    def sb(self, name, shape, dt=F32):
        return self.ctx.enter_context(self.nc.sbuf_tensor(f"{self.tag}_{name}", shape, dt))

    def ps(self, name, shape, dt=F32):
        return self.ctx.enter_context(self.nc.psum_tensor(f"{self.tag}_{name}", shape, dt))

    def sem(self, name):
        self.sems.append(self.ctx.enter_context(self.nc.semaphore(f"{self.tag}_{name}")))
        return self.sems[-1]

    def clear(self):
        if self.sems:
            with self.nc.Block() as block:

                @block.sync
                def _(sp):
                    for sem in self.sems:
                        sp.sem_clear(sem)


def make_constants(nc, k):
    with ExitStack() as ctx:
        s = Scope(nc, ctx, "const")
        filled, cast = s.sem("filled"), s.sem("cast")
        block = ctx.enter_context(nc.Block())

        @block.gpsimd
        def _(pool):
            pool.memset(k.ones[:], 1.0).then_inc(filled, 1)
            pool.iota(k.iota_f[:], pattern=[[1, NBK]], base=0, channel_multiplier=0,
                      allow_small_or_imprecise_dtypes=True).then_inc(filled, 1)
            pool.iota(k.slot_f[:], pattern=[[P, SLOTS]], base=0, channel_multiplier=1,
                      allow_small_or_imprecise_dtypes=True).then_inc(filled, 1)
            pool.wait_ge(filled, 3)
            pool.affine_select(out=k.ident[:], in_=k.ones[:], compare_op=ALU.is_equal, fill=0.0,
                               base=0, pattern=[[1, P]], channel_multiplier=-1).then_inc(filled, 1)
            pool.affine_select(out=k.tri_f[:], in_=k.ones[:], compare_op=ALU.is_gt, fill=0.0,
                               base=0, pattern=[[1, P]], channel_multiplier=-1).then_inc(filled, 1)

        @block.vector
        def _(dve):
            dve.wait_ge(filled, 5)
            ch = Chain(dve, cast)
            dve.tensor_copy(k.iota_b[:], k.iota_f[:, 0:2 * P])
            dve.tensor_copy(k.ident_b[:], k.ident[:])
            dve.tensor_copy(k.before_b[:], k.tri_f[:])
            dve.tensor_tensor(k.notbefore_b[:], k.ones[:], k.tri_f[:], ALU.subtract)
            dve.tensor_scalar(k.all256_b[:], k.ones[:], 256.0, None, ALU.mult)
            dve.tensor_scalar(k.ones_b[:], k.ones[:], 1.0, None, ALU.mult)
            dve.memset(k.zeros_b[:], 0.0)
            ch.link(dve.memset(k.fill_i[:, :, 0:1], NO_NODE))
            ch.link(dve.memset(k.fill_i[:, :, 1:2], NO_KEY))


def distribute(nc, k, keys, others, places):
    NG = 2
    with ExitStack() as ctx:
        s = Scope(nc, ctx, "deal")
        key_i = [s.sb(f"key{g}", [P, T], I32) for g in range(NG)]
        oth_i = [s.sb(f"oth{g}", [P, T], I32) for g in range(NG)]
        tmp_i = s.sb("tmp", [P, T], I32)
        bucket = [s.sb(f"bucket{g}", [P, T]) for g in range(NG)]
        pair = [s.sb(f"pair{g}", [P, T, 2], I32) for g in range(NG)]
        onehot = [s.sb(f"onehot{g}", [P, 2, NBK], BF16) for g in range(NG)]
        junk = [s.sb(f"junk{g}", [P, 2, NBK], BF16) for g in range(NG)]
        rank = [s.sb(f"rank{g}", [P, U]) for g in range(NG)]
        wrap = [s.sb(f"wrap{g}", [P, U]) for g in range(NG)]
        lin = [s.sb(f"lin{g}", [P, U]) for g in range(NG)]
        place = [s.sb(f"place{g}", [P, 2, U], I32) for g in range(NG)]
        payload = [s.sb(f"payload{g}", [P, 2, U, 2], I32) for g in range(NG)]
        earlier = [s.ps(f"earlier{g}", [P, 512]) for g in range(NG)]
        loaded, filled, padded = s.sem("loaded"), s.sem("filled"), s.sem("padded")
        chain = s.sem("chain")
        keyed = s.sem("keyed")
        hot = [s.sem(f"hot{g}") for g in range(NG)]
        counted = [s.sem(f"counted{g}") for g in range(NG)]
        ranked = [s.sem(f"ranked{g}") for g in range(NG)]
        placed = [s.sem(f"placed{g}") for g in range(NG)]
        passed = s.sem("passed")
        scattered = [[k.pool_dma[2 * g + h] for h in range(2)] for g in range(NG)]
        block = ctx.enter_context(nc.Block())
        full, rest = E // T, E % T
        turns = T // (2 * U)

        @block.sync
        def _(sp):
            for g in range(NG):
                sp.dma_start(places[g].rearrange("(p r) c -> p (r c)", p=P),
                             k.fill_i[:].rearrange("p r c -> p (r c)")).then_inc(filled, 16)
            sp.wait_ge(padded, 1)
            for g in range(NG):
                for to, of in ((key_i[g], keys[g]), (oth_i[g], others[g])):
                    for lo, hi in ((0, 112), (112, full)):
                        sp.dma_start(to[lo:hi, :],
                                     of[lo * T:hi * T].rearrange("(p t) -> p t", t=T)).then_inc(loaded, 16)
                    sp.dma_start(to[full:full + 1, 0:rest],
                                 of[full * T:E].rearrange("(p t) -> p t", p=1)).then_inc(loaded, 16)

        @block.vector
        def _(dve):
            ch = Chain(dve, chain)
            for g in range(NG):
                dve.memset(key_i[g][:], (NBK - 1) * P)
                ch.link(dve.memset(oth_i[g][:], 0))
            dve.sem_inc(padded, 1)
            dve.wait_ge(loaded, 16 * 3 * 2 * NG)
            for g in range(NG):
                dve.tensor_copy(pair[g][:, :, 0], oth_i[g][:])
                ch.link(dve.tensor_scalar(pair[g][:, :, 1], key_i[g][:], P - 1, None, ALU.bitwise_and))
                ch.link(dve.tensor_scalar(tmp_i[:], key_i[g][:], 7, None, ALU.logical_shift_right))
                ch.link(dve.tensor_copy(bucket[g][:], tmp_i[:]))
            base = ch.k
            PER = 10 * NG // 2 * 2
            with dve.Fori(0, turns) as turn:
                ch = Chain(dve, chain, per=4 * NG, turn=turn, base=base)
                for half in range(2):
                    for u in range(U):
                        t = turn * (2 * U) + (half * U + u)
                        slot = (half * U + u) % 2
                        for g in range(NG):
                            dve.wait_ge(counted[g], 2 * t)
                            dve.tensor_scalar(onehot[g][:, slot, :], k.iota_f[:], bucket[g][:, bass.ds(t, 1)],
                                              None, ALU.is_equal).then_inc(hot[g], 1)
                        for g in range(NG):
                            dve.wait_ge(counted[g], 2 * t + 1)
                            dve.wait_ge(hot[g], t + 1)
                            dve.tensor_tensor_reduce(out=junk[g][:, slot, :], in0=earlier[g][:, 0:NBK],
                                                     in1=onehot[g][:, slot, :], scale=1.0, scalar=0.0,
                                                     op0=ALU.mult, op1=ALU.add,
                                                     accum_out=rank[g][:, u:u + 1]).then_inc(ranked[g], 1)
                    t0 = turn * (2 * U) + half * U
                    for g in range(NG):
                        dve.wait_ge(ranked[g], t0 + U)
                        dve.tensor_scalar(wrap[g][:], rank[g][:], float(P), float(1 - P * NBK * SLOTS),
                                          ALU.is_ge, ALU.mult)
                        ch.link(dve.tensor_scalar(lin[g][:], rank[g][:], float(NBK * SLOTS), None, ALU.mult))
                        ch.link(dve.scalar_tensor_tensor(out=lin[g][:], in0=bucket[g][:, bass.ds(t0, U)],
                                                         scalar=float(SLOTS), in1=lin[g][:],
                                                         op0=ALU.mult, op1=ALU.add))
                        dve.wait_ge(scattered[g][half], turn * (16 * U))
                        dve.tensor_tensor(place[g][:, half, :], lin[g][:], wrap[g][:], ALU.add).then_inc(placed[g], 1)
                        dve.tensor_copy(payload[g][:, half, :, :],
                                        pair[g][:, bass.ds(t0, U), :]).then_inc(placed[g], 1)
                ch.per = ch.k
                assert ch.k == 4 * NG, ch.k

        @block.tensor
        def _(pe):
            for g in range(NG):
                nc.tensor.matmul(earlier[g][:, 0:NBK], k.zeros_b[:, 0:P], k.zeros_b[:], start=True, stop=True,
                                 skip_group_check=True)
            with pe.Fori(0, turns) as turn:
                for v in range(2 * U):
                    t = turn * (2 * U) + v
                    for g in range(NG):
                        pe.wait_ge(hot[g], t + 1)
                        nc.tensor.matmul(earlier[g][:, 0:NBK], k.before_b[:], onehot[g][:, v % 2, :],
                                         start=False, stop=True, skip_group_check=True).then_inc(counted[g], 1)
                    for g in range(NG):
                        pe.wait_ge(ranked[g], t + 1)
                        nc.tensor.matmul(earlier[g][:, 0:NBK], k.notbefore_b[:], onehot[g][:, v % 2, :],
                                         start=False, stop=True, skip_group_check=True).then_inc(counted[g], 1)

        @block.gpsimd
        def _(pool):
            pool.wait_ge(filled, 16 * NG)
            with pool.Fori(0, turns) as turn:
                for half in range(2):
                    for g in range(NG):
                        pool.wait_ge(placed[g], (turn * 2 + half + 1) * 2)
                        pool.sem_inc(passed, 1)
                        for u in range(U):
                            pool.indirect_dma_start(
                                places[g], bass.IndirectOffsetOnAxis(place[g][:, half, u:u + 1], 0),
                                payload[g][:, half, u, :], None,
                                bounds_check=SP_ROWS - 1, oob_is_err=False).then_inc(scattered[g][half], 16)
            for g in range(NG):
                for half in range(2):
                    pool.wait_ge(scattered[g][half], turns * 16 * U)
                    k.pool_count[2 * g + half] += turns * 16 * U


def sort_buckets(nc, k, places, index, local):
    G = 14
    with ExitStack() as ctx:
        s = Scope(nc, ctx, "sort")
        raw = s.sb("raw", [P, NBK, SLOTS, 2], I32)
        tmp_i = s.sb("tmp", [P, NBK, SLOTS], I32)
        loc = s.sb("loc", [P, NBK, SLOTS])
        code = s.sb("code", [P, NBK, SLOTS])
        parts = s.sb("parts", [P, NBK, SLOTS, 3], BF16)
        diag = s.sb("diag", [P, G, SLOTS, P], BF16)
        junk = s.sb("junk", [P, 2, SLOTS, SLOTS * P], BF16)
        rank = s.sb("rank", [P, G, SLOTS])
        perm = s.sb("perm", [P, 2, SLOTS, SLOTS * P], BF16)
        slot_row = s.sb("slotrow", [P, SLOTS, P], BF16)
        codes = [s.ps(f"codes{i}", [P, 512]) for i in range(2)]
        moved = s.ps("moved", [P, 512])
        took = s.sb("took", [P, G * SLOTS, 3])
        loaded, chain = s.sem("loaded"), s.sem("chain")
        diag_ready, codes_ready, codes_free = s.sem("diag_ready"), s.sem("codes_ready"), s.sem("codes_free")
        perm_ready, perm_used, moved_read = s.sem("perm_ready"), s.sem("perm_used"), s.sem("moved_read")
        block = ctx.enter_context(nc.Block())
        turns = NBK // G
        NG = len(places)

        @block.sync
        def _(sp):
            for g in range(NG):
                if g:
                    sp.wait_ge(codes_free, 2 + g * NBK)
                sp.dma_start(raw[:].rearrange("p b j c -> p (b j c)"),
                             places[g].rearrange("(p r) c -> p (r c)", p=P)).then_inc(loaded, 16)

        @block.vector
        def _(dve):
            ch = Chain(dve, chain)
            for j in range(SLOTS):
                ch.link(dve.tensor_scalar(slot_row[:, j, :], k.ident[:], k.slot_f[:, j:j + 1], None, ALU.mult))
            dve.sem_inc(codes_free, 2)
            base = ch.k
            for g in range(NG):
                dve.wait_ge(loaded, 16 * (g + 1))
                ch = Chain(dve, chain, base=base)
                ch.link(dve.tensor_copy(loc[:], raw[:, :, :, 1]))
                dve.tensor_copy(parts[:, :, :, 2], loc[:])
                ch.link(dve.tensor_scalar(tmp_i[:], raw[:, :, :, 0], 8, None, ALU.logical_shift_right))
                ch.link(dve.tensor_copy(parts[:, :, :, 0], tmp_i[:]))
                ch.link(dve.tensor_scalar(tmp_i[:], raw[:, :, :, 0], 255, None, ALU.bitwise_and))
                ch.link(dve.tensor_copy(parts[:, :, :, 1], tmp_i[:]))
                for j in range(SLOTS):
                    last = dve.tensor_scalar(code[:, :, j], loc[:, :, j], 256.0, k.slot_f[:, j:j + 1],
                                             ALU.mult, ALU.add)
                ch.link(last)
                base += ch.k
                flat_loc = loc[:].rearrange("p b j -> p (b j)")
                flat_code = code[:].rearrange("p b j -> p (b j)")
                with dve.Fori(0, turns) as turn:
                    ch = Chain(dve, chain, per=G + 1, turn=turn, base=base)
                    n0 = turn * G + g * NBK
                    for i in range(G):
                        for j in range(SLOTS):
                            last = dve.tensor_scalar(diag[:, i, j, :], k.ident_b[:],
                                                     flat_loc[:, bass.ds(turn * (G * SLOTS) + (i * SLOTS + j), 1)],
                                                     None, ALU.mult)
                        last.then_inc(diag_ready, 1)
                    for i in range(G):
                        dve.wait_ge(codes_ready, n0 + i + 1)
                        for j in range(SLOTS):
                            last = dve.tensor_scalar(junk[:, i % 2, j, :], codes[i % 2][:, 0:SLOTS * P],
                                                     flat_code[:, bass.ds(turn * (G * SLOTS) + (i * SLOTS + j), 1)],
                                                     0.0, ALU.is_lt, ALU.add, accum_out=rank[:, i, j:j + 1])
                        ch.link(last)
                        dve.sem_inc(codes_free, 1)
                        dve.wait_ge(perm_used, n0 + i)
                        for j in range(SLOTS):
                            last = dve.tensor_scalar(perm[:, i % 2, j, :], k.iota_b[:], rank[:, i, j:j + 1],
                                                     None, ALU.is_equal)
                        last.then_inc(perm_ready, 1)
                    dve.wait_ge(perm_used, n0 + G + 1)
                    ch.link(dve.tensor_copy(took[:].rearrange("p s c -> p (s c)"), moved[:, 0:G * SLOTS * 3]))
                    at = bass.ds(turn * (G * SLOTS), G * SLOTS)
                    dve.scalar_tensor_tensor(out=index[g][:, at], in0=took[:, :, 0], scalar=256.0, in1=took[:, :, 1],
                                             op0=ALU.mult, op1=ALU.add)
                    dve.tensor_copy(local[g][:, at], took[:, :, 2]).then_inc(moved_read, 1)
                    ch.close()
                base += turns * (G + 1)

        @block.tensor
        def _(pe):
            pe.sem_inc(perm_used, 1)
            for g in range(NG):
                with pe.Fori(0, turns) as turn:
                    n0 = turn * G + g * NBK

                    def spread(i):
                        pe.wait_ge(diag_ready, n0 + i + 1)
                        pe.wait_ge(codes_free, n0 + i + 1)
                        to = codes[i % 2][:, 0:SLOTS * P]
                        nc.tensor.matmul(to, k.all256_b[:], diag[:, i, :, :], start=True, stop=False)
                        nc.tensor.matmul(to, k.ones_b[:], slot_row[:], start=False, stop=True).then_inc(codes_ready, 1)

                    spread(0)
                    for i in range(G):
                        if i + 1 < G:
                            spread(i + 1)
                        pe.wait_ge(perm_ready, n0 + i + 1)
                        if i == 0:
                            pe.wait_ge(moved_read, turn + g * turns)
                        for hi in range(SLOTS):
                            c0 = (i * SLOTS + hi) * 3
                            for j in range(SLOTS):
                                last = nc.tensor.matmul(
                                    moved[:, c0:c0 + 3], perm[:, i % 2, j, hi * P:(hi + 1) * P],
                                    parts[:].rearrange("p b j c -> p (b j c)")[
                                        :, bass.ds(turn * (G * SLOTS * 3) + (i * SLOTS + j) * 3, 3)],
                                    start=(j == 0), stop=(j == SLOTS - 1))
                        last.then_inc(perm_used, 1)


class Constants:
    def __init__(self, s):
        self.pool_dma = [s.sem(f"pool_dma{i}") for i in range(4)]
        self.pool_count = [0] * 4
        self.ones = s.sb("ones", [P, P])
        self.ident = s.sb("ident", [P, P])
        self.tri_f = s.sb("tri", [P, P])
        self.iota_f = s.sb("iota", [P, NBK])
        self.slot_f = s.sb("slot", [P, SLOTS])
        self.iota_b = s.sb("iota_b", [P, SLOTS * P], BF16)
        self.ident_b = s.sb("ident_b", [P, P], BF16)
        self.before_b = s.sb("before_b", [P, P], BF16)
        self.notbefore_b = s.sb("notbefore_b", [P, P], BF16)
        self.all256_b = s.sb("all256_b", [P, P], BF16)
        self.ones_b = s.sb("ones_b", [P, P], BF16)
        self.zeros_b = s.sb("zeros_b", [P, NBK], BF16)
        self.fill_i = s.sb("fill", [P, NBK * SLOTS, 2], I32)


NP = NBK * P
WCOLS = F + 2 * HEADS
EPS = 1e-5
SLOPE_ATTN = 0.2
SLOPE_ACT = 0.01
FAR = 1e30
TINY = 1e-30
TAIL = N - (NBK - BATCH) * P
TAIL_FULL = TAIL // P
TAIL_REST = TAIL % P


class Graph:

    def __init__(self, index, local):
        self.index, self.local = index, local


def load_weights(nc, k, W, al, ar, b, w_qkv, b_qkv, w_o, b_o):
    L = 3
    with ExitStack() as ctx:
        s = Scope(nc, ctx, "weights")
        a_rows = s.sb("a_rows", [P, 2, L, F])
        prod = s.sb("prod", [P, 2, F])
        rest = s.sb("rest", [1, 5 * F])
        part = s.sb("part", [1, 3, 5 * F], BF16)
        loaded, chain, moved = s.sem("loaded"), s.sem("chain"), s.sem("moved")
        split = s.sem("split")
        block = ctx.enter_context(nc.Block())

        @block.sync
        def _(sp):
            for l in range(L):
                sp.dma_start(k.w_gat[:, l, :, 0:F], W[l].rearrange("(c p) n -> p c n", p=P)).then_inc(loaded, 16)
                for i, a in enumerate((al, ar)):
                    sp.dma_start(a_rows[:, i, l, :], a[l:l + 1].rearrange("o h d -> o (h d)").to_broadcast([P, F])
                                 ).then_inc(loaded, 16)
            with nc.allow_non_contiguous_dma(reason="256 words of a bias, once"):
                sp.dma_start(k.b_col[:], b.rearrange("l (c p) -> p l c", p=P)).then_inc(loaded, 16)
            sp.dma_start(k.b2_row[:], b[2:3].to_broadcast([P, F])).then_inc(loaded, 16)
            sp.dma_start(k.w_qkv[:], w_qkv.rearrange("(c p) n -> p c n", p=P)).then_inc(loaded, 16)
            sp.dma_start(k.w_o[:], w_o.rearrange("(c p) n -> p c n", p=P)).then_inc(loaded, 16)
            sp.dma_start(rest[:, 0:3 * F], b_qkv.rearrange("(o n) -> o n", o=1)).then_inc(loaded, 16)
            sp.dma_start(rest[:, 3 * F:4 * F], b_o.rearrange("(o n) -> o n", o=1)).then_inc(loaded, 16)
            sp.wait_ge(split, 1)
            for i in range(3):
                sp.dma_start(k.bias_parts[i:i + 1, :], part[:, i, 0:4 * F]).then_inc(moved, 16)
            sp.wait_ge(moved, 48)

        @block.vector
        def _(dve):
            dve.wait_ge(loaded, 16 * (3 * L + 6))
            ch = Chain(dve, chain)
            for l in range(L):
                for i in range(2):
                    for c in range(2):
                        ch.link(dve.tensor_tensor(prod[:, c, :], k.w_gat[:, l, c, 0:F], a_rows[:, i, l, :], ALU.mult))
                        ch.link(dve.tensor_reduce(k.w_gat[:, l, c, F + i * HEADS:F + (i + 1) * HEADS],
                                                  prod[:, c, :].rearrange("p (h d) -> p h d", h=HEADS),
                                                  axis=AX.X, op=ALU.add))
            r = rest[:, 0:4 * F]
            for i in range(3):
                ch.link(dve.tensor_copy(part[:, i, 0:4 * F], r))
                if i < 2:
                    ch.link(dve.tensor_tensor(r, r, part[:, i, 0:4 * F], ALU.subtract))
            dve.sem_inc(split, 1)


def load_nodes(sp, x, to, i, loaded, last):
    a = TAIL_FULL
    if not last:
        v = x[bass.ds(i * (BATCH * P), BATCH * P), :].rearrange("(b p) f -> p b f", p=P)
        sp.dma_start(to[:, 0:a, :], v[:, 0:a, :]).then_inc(loaded, 16)
        sp.dma_start(to[:, a:BATCH, :], v[:, a:BATCH, :]).then_inc(loaded, 16)
    else:
        n0 = (NBATCH - 1) * BATCH * P
        sp.dma_start(to[:, 0:a, :], x[n0:n0 + a * P, :].rearrange("(b p) f -> p b f", p=P)).then_inc(loaded, 16)
        sp.dma_start(to[0:TAIL_REST, a, :], x[n0 + a * P:N, :]).then_inc(loaded, 16)


R = 2
BH = BATCH * HEADS
PAIR = SLOTS * P


class Batch:

    def __init__(self, turn, h, i=None):
        self.turn, self.h = turn, h
        self.i = turn * R + h if i is None else i
        self.s, self.q, self.round = h % R, h % 2, turn + h // R
        self.pairs = turn * (R // 2) + h // 2

    def plus(self, d):
        return Batch(self.turn, self.h + d, self.i + d)

    def n(self, b):
        return self.i * BATCH + b, (self.h * BATCH + b) % 2


def over_batches(eng, first, batch, turns):
    first()
    with eng.Fori(0, turns - 1) as turn, eng.register() as number:
        for h in range(R):
            eng.reg_mov(number, turn * R + h)
            batch(Batch(turn, h, eng.snap(number, min_val=0, max_val=NBATCH - R - 1)), R)
    for h in range(R):
        batch(Batch(turns - 1, h), R - 1 - h)


def gat_layer(nc, k, graph, table_in, layer, table_out):
    with ExitStack() as ctx:
        s = Scope(nc, ctx, f"gat{layer}")
        rows = s.sb("rows", [P, R, BATCH, SLOTS, ROW])
        place = s.sb("place", [P, R, BATCH * SLOTS], I32)
        onehot = s.sb("onehot", [P, R, BATCH * SLOTS, P])
        onehot_t = s.sb("onehot_t", [P, 2, PAIR])
        er_edge = s.sb("er_edge", [P, 2, SLOTS, BH])
        logit = s.sb("logit", [P, 2, SLOTS, BH])
        key_bh = s.sb("key_bh", [P, 2, SLOTS, BH])
        key_t = s.sb("key_t", [BH, PAIR])
        wall = s.sb("wall", [BH, PAIR + 1])
        run_max = s.sb("run_max", [BH, PAIR])
        node_max = s.sb("node_max", [BH, PAIR])
        below_max = s.sb("below_max", [BH, 2, PAIR])
        total = s.sb("total", [P, 2, HEADS])
        mean = s.sb("mean", [P, 2, F])
        mean_t = s.sb("mean_t", [P, 2, 2, P])
        out_rows = s.sb("out_rows", [P, 2, BATCH, ROW])
        p_turn = s.ps("p_turn", [P, 512])
        p_er = s.ps("p_er", [P, 512])
        p_soft = s.ps("p_soft", [P, 512])
        p_sum = [s.ps(f"p_sum{i}", [P, 512]) for i in range(2)]
        p_mean = s.ps("p_mean", [P, 512])
        p_next = [s.ps(f"p_next{i}", [P, 512]) for i in range(2)]
        (placed, hot, hot_turned, hot_copied, er_made, er_taken, logits, soft_turned, below, soft_back, weights,
         messages, summed, averaged, mean_turned, mean_copied, product, row_done, chain_er, chain_soft,
         chain_mean, passed, passed_pe, shifted) = (s.sem(n) for n in (
             "placed", "hot", "hot_turned", "hot_copied", "er_made", "er_taken", "logits", "soft_turned", "below",
             "soft_back", "weights", "messages", "summed", "averaged", "mean_turned", "mean_copied", "product",
             "row_done", "chain_er", "chain_soft", "chain_mean", "passed", "passed_pe", "shifted"))
        gathered, before = k.pool_dma[0:R], k.pool_count[0:R]
        stored = [s.sem(f"stored{i}") for i in range(2)]
        walls_set = s.sem("walls_set")
        rows_clear = s.sem("rows_clear")
        AHEAD = R * BATCH
        block = ctx.enter_context(nc.Block())
        turns = NBATCH // R
        flat_local = graph.local[:].rearrange("p (b j) -> p b j", j=SLOTS)

        @block.gpsimd
        def _(pool):
            pool.wait_ge(rows_clear, 1)

            def gather(a):
                pool.wait_ge(placed, a.i + 1)
                for b in range(BATCH):
                    pool.wait_ge(averaged, a.n(b)[0] + 1)
                    pool.sem_inc(passed, 1)
                    for j in range(SLOTS):
                        c = b * SLOTS + j
                        pool.indirect_dma_start(rows[:, a.s, b, j, :], None, table_in,
                                                bass.IndirectOffsetOnAxis(place[:, a.s, c:c + 1], 0),
                                                bounds_check=N - 1, oob_is_err=False).then_inc(gathered[a.s], 16)

            with pool.Fori(0, turns) as turn:
                for h in range(R):
                    gather(Batch(turn, h))
            for h in range(R):
                k.pool_count[h] += turns * 16 * BATCH * SLOTS

        @block.sync
        def _(sp):
            with sp.Fori(0, turns) as turn:
                for h in range(R):
                    a = Batch(turn, h)
                    sp.wait_ge(row_done, (a.i + 1) * BATCH + 1)
                    sp.dma_start(table_out[bass.ds(a.i * (BATCH * P), BATCH * P), :].rearrange("(b p) f -> p b f", p=P),
                                 out_rows[:, a.q]).then_inc(stored[a.q], 16)
            for q in range(2):
                sp.wait_ge(stored[q], 16 * (NBATCH // 2))

        @block.vector
        def _(dve):
            def make_place(a):
                dve.wait_ge(gathered[a.s], a.round * (16 * BATCH * SLOTS) + before[a.s])
                dve.tensor_copy(place[:, a.s, :], graph.index[:, bass.ds(a.i * (BATCH * SLOTS), BATCH * SLOTS)]
                                ).then_inc(placed, 1)

            def make_onehot(a, b):
                for j in range(SLOTS):
                    last = dve.tensor_scalar(onehot[:, a.s, b * SLOTS + j, :], k.iota_f[:, 0:P],
                                             graph.local[:, bass.ds((a.i * BATCH + b) * SLOTS + j, 1)],
                                             None, ALU.is_equal)
                last.then_inc(hot, 1)

            def take_er(a):
                ch = Chain(dve, chain_er, per=1, turn=a.i)
                dve.wait_ge(er_made, (a.i + 1) * BATCH + 1)
                ch.link(dve.tensor_copy(er_edge[:, a.q].rearrange("p j c -> p (j c)"), p_er[:, 0:SLOTS * BH]))
                dve.sem_inc(er_taken, 1)
                ch.close()

            def make_logits(a, ch):
                for j in range(SLOTS):
                    last = dve.tensor_copy(
                        key_bh[:, a.q, j, :].rearrange("p (b h) -> p b h", h=HEADS),
                        flat_local[:, bass.ds(a.i * BATCH, BATCH), j:j + 1].to_broadcast([P, BATCH, HEADS]))
                dve.wait_ge(gathered[a.s], (a.round + 1) * (16 * BATCH * SLOTS) + before[a.s])
                for j in range(SLOTS):
                    last = dve.tensor_tensor(logit[:, a.q, j, :].rearrange("p (b h) -> p b h", h=HEADS),
                                             rows[:, a.s, :, j, F:ROW],
                                             er_edge[:, a.q, j, :].rearrange("p (b h) -> p b h", h=HEADS), ALU.add)
                ch.link(last)
                dve.scalar_tensor_tensor(out=logit[:, a.q], in0=logit[:, a.q], scalar=SLOPE_ATTN, in1=logit[:, a.q],
                                         op0=ALU.mult, op1=ALU.max).then_inc(logits, 1)

            def subtract_max(a, ch):
                dve.wait_ge(soft_turned, a.i + 1)
                ch.link(dve.tensor_copy(key_t[:], p_soft[0:BH, PAIR:2 * PAIR]))
                ch.link(dve.tensor_tensor(wall[:, 1:PAIR], key_t[:, 1:PAIR], key_t[:, 0:PAIR - 1], ALU.is_equal))
                ch.link(dve.tensor_scalar(wall[:, 1:PAIR], wall[:, 1:PAIR], 1.0, FAR, ALU.subtract, ALU.mult))
                ch.link(dve.tensor_tensor_scan(run_max[:], wall[:, 0:PAIR], p_soft[0:BH, 0:PAIR], 0.0,
                                               ALU.add, ALU.max))
                ch.link(dve.tensor_tensor_scan(node_max[:, ::-1], wall[:, PAIR:0:-1], run_max[:, ::-1], 0.0,
                                               ALU.add, ALU.max))
                dve.tensor_tensor(below_max[:, a.q], p_soft[0:BH, 0:PAIR], node_max[:], ALU.subtract).then_inc(below, 1)

            def weigh(a, b):
                if b == 0:
                    dve.wait_ge(weights, a.i + 1)
                v = rows[:, a.s, b, :, 0:F].rearrange("p j (h d) -> p j h d", h=HEADS)
                w = rows[:, a.s, b, :, F:ROW]
                for j in range(SLOTS):
                    last = dve.tensor_tensor(v[:, j], v[:, j], w[:, j].unsqueeze(2).to_broadcast([P, HEADS, HD]),
                                             ALU.mult)
                last.then_inc(messages, 1)

            def average(a, b):
                n, q = a.n(b)
                ch = Chain(dve, chain_mean, per=2, turn=n)
                dve.wait_ge(summed, n + 1)
                ch.link(dve.tensor_scalar(total[:, q], p_sum[q][:, F:ROW], TINY, None, ALU.max))
                ch.link(dve.reciprocal(total[:, q], total[:, q]))
                dve.wait_ge(mean_turned, n)
                dve.tensor_tensor(mean[:, q].rearrange("p (h d) -> p h d", h=HEADS),
                                  p_sum[q][:, 0:F].rearrange("p (h d) -> p h d", h=HEADS),
                                  total[:, q].unsqueeze(2).to_broadcast([P, HEADS, HD]), ALU.mult).then_inc(averaged, 1)

            def leak(a, b):
                n, q = a.n(b)
                dve.wait_ge(shifted, n + 1)
                v = mean_t[:, q].rearrange("p c n -> p (c n)")
                dve.scalar_tensor_tensor(out=v, in0=v, scalar=SLOPE_ACT, in1=v,
                                         op0=ALU.mult, op1=ALU.max).then_inc(mean_copied, 1)

            SOFT = 6

            def first():
                dve.memset(rows[:], 0.0).then_inc(rows_clear, 1)
                dve.wait_ge(rows_clear, 1)
                dve.memset(wall[:, 0:1], -FAR).then_inc(walls_set, 1)
                dve.memset(wall[:, PAIR:PAIR + 1], -FAR).then_inc(walls_set, 1)
                dve.wait_ge(walls_set, 2)
                dve.sem_inc(averaged, AHEAD)
                for h in range(R):
                    make_place(Batch(0, h))
                for h in range(2):
                    for b in range(BATCH):
                        make_onehot(Batch(0, h), b)
                    take_er(Batch(0, h))
                a = Batch(0, 0)
                ch = Chain(dve, chain_soft, per=SOFT, turn=0)
                make_logits(a, ch)
                subtract_max(a, ch)
                ch.close()

            def batch(a, after):
                for st in range(9):
                    if st == 0 and after >= 2:
                        make_place(a.plus(2))
                    if st < BATCH:
                        weigh(a, st)
                    if st == 1 and after >= 1:
                        ch = Chain(dve, chain_soft, per=SOFT, turn=a.plus(1).i)
                        make_logits(a.plus(1), ch)
                    if st == 3 and after >= 1:
                        subtract_max(a.plus(1), ch)
                        ch.close()
                    if 1 <= st <= BATCH:
                        average(a, st - 1)
                        if after >= 2:
                            make_onehot(a.plus(2), st - 1)
                    if 2 <= st:
                        leak(a, st - 2)
                    if st == 8 and after >= 2:
                        take_er(a.plus(2))

            over_batches(dve, first, batch, turns)

        @block.tensor
        def _(pe):
            def turn_onehot(a, b):
                n, q = a.n(b)
                pe.wait_ge(hot, n + 1)
                pe.wait_ge(hot_copied, n)
                for j in range(SLOTS):
                    last = nc.tensor.transpose(p_turn[:, j * P:(j + 1) * P], onehot[:, a.s, b * SLOTS + j, :], k.ident[:])
                last.then_inc(hot_turned, 1)

            def make_er(a, b):
                n, q = a.n(b)
                pe.wait_ge(hot_copied, n + 1)
                if b == 0:
                    pe.wait_ge(er_taken, a.i)
                for j in range(SLOTS):
                    c = j * BH + b * HEADS
                    last = nc.tensor.matmul(p_er[:, c:c + HEADS], onehot_t[:, q, j * P:(j + 1) * P],
                                            k.er[:, bass.ds(n * HEADS, HEADS)], start=True, stop=True)
                last.then_inc(er_made, 1)

            def turn_soft(a):
                pe.wait_ge(logits, a.i + 1)
                pe.wait_ge(weights, a.i)
                pe.sem_inc(passed_pe, 1)
                for x, c in ((logit, 0), (key_bh, PAIR)):
                    for j in range(SLOTS):
                        last = nc.tensor.transpose(p_soft[0:BH, c + j * P:c + (j + 1) * P], x[:, a.q, j, :], k.ident[:])
                last.then_inc(soft_turned, 1)

            def turn_back(a):
                pe.wait_ge(below, a.i + 1)
                pe.sem_inc(passed_pe, 1)
                for j in range(SLOTS):
                    last = nc.tensor.transpose(p_soft[:, j * BH:(j + 1) * BH], below_max[:, a.q, j * P:(j + 1) * P],
                                               k.ident[0:BH, 0:BH])
                last.then_inc(soft_back, 1)

            def add_up(a, b):
                n, q = a.n(b)
                pe.wait_ge(messages, n + 1)
                pe.wait_ge(averaged, n + (AHEAD - 1))
                for j in range(SLOTS):
                    last = nc.tensor.matmul(p_sum[q][:, 0:ROW], onehot[:, a.s, b * SLOTS + j, :], rows[:, a.s, b, j, :],
                                            start=(j == 0), stop=(j == SLOTS - 1))
                last.then_inc(summed, 1)

            def turn_mean(a, b):
                n, q = a.n(b)
                pe.wait_ge(averaged, n + (AHEAD + 1))
                pe.wait_ge(mean_copied, n)
                for c in range(2):
                    last = nc.tensor.transpose(p_mean[:, c * P:(c + 1) * P], mean[:, q, c * P:(c + 1) * P], k.ident[:])
                last.then_inc(mean_turned, 1)

            def multiply(a, b):
                n, q = a.n(b)
                pe.wait_ge(mean_copied, n + 1)
                pe.wait_ge(row_done, n)
                for c in range(2):
                    last = nc.tensor.matmul(p_next[q][:, 0:WCOLS], mean_t[:, q, c, :], k.w_gat[:, layer + 1, c, :],
                                            start=(c == 0), stop=(c == 1))
                last.then_inc(product, 1)

            def first():
                for x in (mean_turned, product, er_made):
                    pe.sem_inc(x, 1)
                for h in range(2):
                    for b in range(BATCH + 1):
                        if b:
                            make_er(Batch(0, h), b - 1)
                        if b < BATCH:
                            turn_onehot(Batch(0, h), b)
                turn_soft(Batch(0, 0))
                turn_back(Batch(0, 0))

            def batch(a, after):
                for st in range(9):
                    if st < BATCH:
                        add_up(a, st)
                    if 2 <= st and after >= 2:
                        make_er(a.plus(2), st - 2)
                    if 1 <= st <= BATCH and after >= 2:
                        turn_onehot(a.plus(2), st - 1)
                    if st == 2 and after >= 1:
                        turn_soft(a.plus(1))
                    if st == 6 and after >= 1:
                        turn_back(a.plus(1))
                    if 1 <= st <= BATCH:
                        turn_mean(a, st - 1)
                    if 2 <= st:
                        multiply(a, st - 2)

            over_batches(pe, first, batch, turns)

        @block.scalar
        def _(act):
            def copy_onehot(a, b):
                n, q = a.n(b)
                act.wait_ge(hot_turned, n + 1)
                act.wait_ge(er_made, n)
                nc.scalar.copy(onehot_t[:, q, :], p_turn[:, 0:PAIR]).then_inc(hot_copied, 1)

            def exponentiate(a):
                act.wait_ge(soft_back, a.i + 1)
                for j in range(SLOTS):
                    last = nc.scalar.activation(
                        rows[:, a.s, :, j, F:ROW],
                        p_soft[:, j * BH:(j + 1) * BH].rearrange("p (b h) -> p b h", h=HEADS), ACT.Exp)
                last.then_inc(weights, 1)

            def activate(a, b):
                n, q = a.n(b)
                act.wait_ge(mean_turned, n + 2)
                act.wait_ge(product, n)
                for c in range(2):
                    last = nc.scalar.activation(mean_t[:, q, c, :], p_mean[:, c * P:(c + 1) * P], ACT.Identity,
                                                bias=k.b_col[:, layer, c:c + 1])
                last.then_inc(shifted, 1)

            def finish(a, b):
                n, q = a.n(b)
                act.wait_ge(product, n + 2)
                if b == 0:
                    act.wait_ge(stored[a.q], a.pairs * 16)
                nc.scalar.copy(out_rows[:, a.q, b, :], p_next[q][:, 0:ROW])
                nc.scalar.copy(k.er[:, bass.ds(n * HEADS, HEADS)], p_next[q][:, ROW:WCOLS]).then_inc(row_done, 1)

            def first():
                act.sem_inc(row_done, 1)
                for h in range(2):
                    for b in range(BATCH):
                        copy_onehot(Batch(0, h), b)
                exponentiate(Batch(0, 0))

            def batch(a, after):
                for st in range(9):
                    if 1 <= st <= BATCH and after >= 2:
                        copy_onehot(a.plus(2), st - 1)
                    if 1 <= st <= BATCH:
                        activate(a, st - 1)
                    if st == 7 and after >= 1:
                        exponentiate(a.plus(1))
                    if 2 <= st:
                        finish(a, st - 2)

            over_batches(act, first, batch, turns)


def last_gat_layer(nc, k, graph, table_in, x, x_out):
    with ExitStack() as ctx:
        s = Scope(nc, ctx, "gat2")
        rows = s.sb("rows", [P, R, BATCH, SLOTS, ROW])
        place = s.sb("place", [P, R, BATCH * SLOTS], I32)
        onehot = s.sb("onehot", [P, R, BATCH * SLOTS, P])
        onehot_t = s.sb("onehot_t", [P, 2, PAIR])
        er_edge = s.sb("er_edge", [P, 2, SLOTS, BH])
        logit = s.sb("logit", [P, 2, SLOTS, BH])
        key_bh = s.sb("key_bh", [P, 2, SLOTS, BH])
        key_t = s.sb("key_t", [BH, PAIR])
        wall = s.sb("wall", [BH, PAIR + 1])
        run_max = s.sb("run_max", [BH, PAIR])
        node_max = s.sb("node_max", [BH, PAIR])
        below_max = s.sb("below_max", [BH, 2, PAIR])
        total = s.sb("total", [P, 2, HEADS])
        mean = s.sb("mean", [P, 2, F])
        x_rows = s.sb("x_rows", [P, 2, BATCH, F])
        p_turn = s.ps("p_turn", [P, 512])
        p_er = s.ps("p_er", [P, 512])
        p_soft = s.ps("p_soft", [P, 512])
        p_sum = [s.ps(f"p_sum{i}", [P, 512]) for i in range(2)]
        (placed, hot, hot_turned, hot_copied, er_made, er_taken, logits, soft_turned, below, soft_back, weights,
         messages, summed, averaged, row_done, chain_er, chain_soft,
         chain_mean, passed, passed_pe) = (s.sem(n) for n in (
             "placed", "hot", "hot_turned", "hot_copied", "er_made", "er_taken", "logits", "soft_turned", "below",
             "soft_back", "weights", "messages", "summed", "averaged", "row_done",
             "chain_er", "chain_soft", "chain_mean", "passed", "passed_pe"))
        gathered, before = k.pool_dma[0:R], k.pool_count[0:R]
        loaded = [s.sem(f"loaded{i}") for i in range(2)]
        stored = [s.sem(f"stored{i}") for i in range(2)]
        walls_set = s.sem("walls_set")
        rows_clear = s.sem("rows_clear")
        AHEAD = R * BATCH
        block = ctx.enter_context(nc.Block())
        turns = NBATCH // R
        flat_local = graph.local[:].rearrange("p (b j) -> p b j", j=SLOTS)

        @block.gpsimd
        def _(pool):
            pool.wait_ge(rows_clear, 1)

            def gather(a):
                pool.wait_ge(placed, a.i + 1)
                for b in range(BATCH):
                    pool.wait_ge(averaged, a.n(b)[0] + 1)
                    pool.sem_inc(passed, 1)
                    for j in range(SLOTS):
                        c = b * SLOTS + j
                        pool.indirect_dma_start(rows[:, a.s, b, j, :], None, table_in,
                                                bass.IndirectOffsetOnAxis(place[:, a.s, c:c + 1], 0),
                                                bounds_check=N - 1, oob_is_err=False).then_inc(gathered[a.s], 16)

            with pool.Fori(0, turns) as turn:
                for h in range(R):
                    gather(Batch(turn, h))
            for h in range(R):
                k.pool_count[h] += turns * 16 * BATCH * SLOTS

        @block.sync
        def _(sp):
            sp.wait_ge(rows_clear, 1)

            def load(a, last):
                sp.wait_ge(stored[a.q], a.pairs * 16)
                load_nodes(sp, x, x_rows[:, a.q], a.i, loaded[a.q], last)

            def store(a):
                sp.wait_ge(row_done, (a.i + 1) * BATCH)
                sp.dma_start(x_out[bass.ds(a.i * (BATCH * P), BATCH * P), :].rearrange("(b p) f -> p b f", p=P),
                             x_rows[:, a.q]).then_inc(stored[a.q], 16)

            load(Batch(0, 0), False)
            with sp.Fori(0, turns - 1) as turn:
                for h in range(R):
                    load(Batch(turn, h + 1), False)
                    store(Batch(turn, h))
            load(Batch(turns - 1, 1), True)
            for h in range(R):
                store(Batch(turns - 1, h))
            for q in range(2):
                sp.wait_ge(stored[q], 16 * (NBATCH // 2))

        @block.vector
        def _(dve):
            def make_place(a):
                dve.wait_ge(gathered[a.s], a.round * (16 * BATCH * SLOTS) + before[a.s])
                dve.tensor_copy(place[:, a.s, :], graph.index[:, bass.ds(a.i * (BATCH * SLOTS), BATCH * SLOTS)]
                                ).then_inc(placed, 1)

            def make_onehot(a, b):
                for j in range(SLOTS):
                    last = dve.tensor_scalar(onehot[:, a.s, b * SLOTS + j, :], k.iota_f[:, 0:P],
                                             graph.local[:, bass.ds((a.i * BATCH + b) * SLOTS + j, 1)],
                                             None, ALU.is_equal)
                last.then_inc(hot, 1)

            def take_er(a):
                ch = Chain(dve, chain_er, per=1, turn=a.i)
                dve.wait_ge(er_made, (a.i + 1) * BATCH + 1)
                ch.link(dve.tensor_copy(er_edge[:, a.q].rearrange("p j c -> p (j c)"), p_er[:, 0:SLOTS * BH]))
                dve.sem_inc(er_taken, 1)
                ch.close()

            def make_logits(a, ch):
                for j in range(SLOTS):
                    last = dve.tensor_copy(
                        key_bh[:, a.q, j, :].rearrange("p (b h) -> p b h", h=HEADS),
                        flat_local[:, bass.ds(a.i * BATCH, BATCH), j:j + 1].to_broadcast([P, BATCH, HEADS]))
                dve.wait_ge(gathered[a.s], (a.round + 1) * (16 * BATCH * SLOTS) + before[a.s])
                for j in range(SLOTS):
                    last = dve.tensor_tensor(logit[:, a.q, j, :].rearrange("p (b h) -> p b h", h=HEADS),
                                             rows[:, a.s, :, j, F:ROW],
                                             er_edge[:, a.q, j, :].rearrange("p (b h) -> p b h", h=HEADS), ALU.add)
                ch.link(last)
                dve.scalar_tensor_tensor(out=logit[:, a.q], in0=logit[:, a.q], scalar=SLOPE_ATTN, in1=logit[:, a.q],
                                         op0=ALU.mult, op1=ALU.max).then_inc(logits, 1)

            def subtract_max(a, ch):
                dve.wait_ge(soft_turned, a.i + 1)
                ch.link(dve.tensor_copy(key_t[:], p_soft[0:BH, PAIR:2 * PAIR]))
                ch.link(dve.tensor_tensor(wall[:, 1:PAIR], key_t[:, 1:PAIR], key_t[:, 0:PAIR - 1], ALU.is_equal))
                ch.link(dve.tensor_scalar(wall[:, 1:PAIR], wall[:, 1:PAIR], 1.0, FAR, ALU.subtract, ALU.mult))
                ch.link(dve.tensor_tensor_scan(run_max[:], wall[:, 0:PAIR], p_soft[0:BH, 0:PAIR], 0.0,
                                               ALU.add, ALU.max))
                ch.link(dve.tensor_tensor_scan(node_max[:, ::-1], wall[:, PAIR:0:-1], run_max[:, ::-1], 0.0,
                                               ALU.add, ALU.max))
                dve.tensor_tensor(below_max[:, a.q], p_soft[0:BH, 0:PAIR], node_max[:], ALU.subtract).then_inc(below, 1)

            def weigh(a, b):
                if b == 0:
                    dve.wait_ge(weights, a.i + 1)
                v = rows[:, a.s, b, :, 0:F].rearrange("p j (h d) -> p j h d", h=HEADS)
                w = rows[:, a.s, b, :, F:ROW]
                for j in range(SLOTS):
                    last = dve.tensor_tensor(v[:, j], v[:, j], w[:, j].unsqueeze(2).to_broadcast([P, HEADS, HD]),
                                             ALU.mult)
                last.then_inc(messages, 1)

            def average(a, b):
                n, q = a.n(b)
                ch = Chain(dve, chain_mean, per=3, turn=n)
                dve.wait_ge(summed, n + 1)
                ch.link(dve.tensor_scalar(total[:, q], p_sum[q][:, F:ROW], TINY, None, ALU.max))
                ch.link(dve.reciprocal(total[:, q], total[:, q]))
                ins = dve.tensor_tensor(mean[:, q].rearrange("p (h d) -> p h d", h=HEADS),
                                        p_sum[q][:, 0:F].rearrange("p (h d) -> p h d", h=HEADS),
                                        total[:, q].unsqueeze(2).to_broadcast([P, HEADS, HD]), ALU.mult)
                ins.then_inc(averaged, 1)
                dve.wait_ge(averaged, n + (AHEAD + 1))
                if b == 0:
                    dve.wait_ge(loaded[a.q], (a.pairs + 1) * 32)
                ch.link(dve.tensor_tensor(mean[:, q], mean[:, q], k.b2_row[:], ALU.add))
                dve.tensor_tensor(x_rows[:, a.q, b, :], mean[:, q], x_rows[:, a.q, b, :], ALU.add).then_inc(row_done, 1)

            SOFT = 6

            def first():
                dve.memset(x_rows[:], 0.0)
                dve.memset(rows[:], 0.0).then_inc(rows_clear, 1)
                dve.wait_ge(rows_clear, 1)
                dve.memset(wall[:, 0:1], -FAR).then_inc(walls_set, 1)
                dve.memset(wall[:, PAIR:PAIR + 1], -FAR).then_inc(walls_set, 1)
                dve.wait_ge(walls_set, 2)
                dve.sem_inc(averaged, AHEAD)
                for h in range(R):
                    make_place(Batch(0, h))
                for h in range(2):
                    for b in range(BATCH):
                        make_onehot(Batch(0, h), b)
                    take_er(Batch(0, h))
                a = Batch(0, 0)
                ch = Chain(dve, chain_soft, per=SOFT, turn=0)
                make_logits(a, ch)
                subtract_max(a, ch)
                ch.close()

            def batch(a, after):
                for st in range(9):
                    if st == 0 and after >= 2:
                        make_place(a.plus(2))
                    if st < BATCH:
                        weigh(a, st)
                    if st == 1 and after >= 1:
                        ch = Chain(dve, chain_soft, per=SOFT, turn=a.plus(1).i)
                        make_logits(a.plus(1), ch)
                    if st == 3 and after >= 1:
                        subtract_max(a.plus(1), ch)
                        ch.close()
                    if 1 <= st <= BATCH:
                        average(a, st - 1)
                        if after >= 2:
                            make_onehot(a.plus(2), st - 1)
                    if st == 8 and after >= 2:
                        take_er(a.plus(2))

            over_batches(dve, first, batch, turns)

        @block.tensor
        def _(pe):
            def turn_onehot(a, b):
                n, q = a.n(b)
                pe.wait_ge(hot, n + 1)
                pe.wait_ge(hot_copied, n)
                for j in range(SLOTS):
                    last = nc.tensor.transpose(p_turn[:, j * P:(j + 1) * P], onehot[:, a.s, b * SLOTS + j, :], k.ident[:])
                last.then_inc(hot_turned, 1)

            def make_er(a, b):
                n, q = a.n(b)
                pe.wait_ge(hot_copied, n + 1)
                if b == 0:
                    pe.wait_ge(er_taken, a.i)
                for j in range(SLOTS):
                    c = j * BH + b * HEADS
                    last = nc.tensor.matmul(p_er[:, c:c + HEADS], onehot_t[:, q, j * P:(j + 1) * P],
                                            k.er[:, bass.ds(n * HEADS, HEADS)], start=True, stop=True)
                last.then_inc(er_made, 1)

            def turn_soft(a):
                pe.wait_ge(logits, a.i + 1)
                pe.wait_ge(weights, a.i)
                pe.sem_inc(passed_pe, 1)
                for x, c in ((logit, 0), (key_bh, PAIR)):
                    for j in range(SLOTS):
                        last = nc.tensor.transpose(p_soft[0:BH, c + j * P:c + (j + 1) * P], x[:, a.q, j, :], k.ident[:])
                last.then_inc(soft_turned, 1)

            def turn_back(a):
                pe.wait_ge(below, a.i + 1)
                pe.sem_inc(passed_pe, 1)
                for j in range(SLOTS):
                    last = nc.tensor.transpose(p_soft[:, j * BH:(j + 1) * BH], below_max[:, a.q, j * P:(j + 1) * P],
                                               k.ident[0:BH, 0:BH])
                last.then_inc(soft_back, 1)

            def add_up(a, b):
                n, q = a.n(b)
                pe.wait_ge(messages, n + 1)
                pe.wait_ge(averaged, n + (AHEAD - 1))
                for j in range(SLOTS):
                    last = nc.tensor.matmul(p_sum[q][:, 0:ROW], onehot[:, a.s, b * SLOTS + j, :], rows[:, a.s, b, j, :],
                                            start=(j == 0), stop=(j == SLOTS - 1))
                last.then_inc(summed, 1)

            def first():
                pe.sem_inc(er_made, 1)
                for h in range(2):
                    for b in range(BATCH + 1):
                        if b:
                            make_er(Batch(0, h), b - 1)
                        if b < BATCH:
                            turn_onehot(Batch(0, h), b)
                turn_soft(Batch(0, 0))
                turn_back(Batch(0, 0))

            def batch(a, after):
                for st in range(9):
                    if st < BATCH:
                        add_up(a, st)
                    if 2 <= st and after >= 2:
                        make_er(a.plus(2), st - 2)
                    if 1 <= st <= BATCH and after >= 2:
                        turn_onehot(a.plus(2), st - 1)
                    if st == 2 and after >= 1:
                        turn_soft(a.plus(1))
                    if st == 6 and after >= 1:
                        turn_back(a.plus(1))

            over_batches(pe, first, batch, turns)

        @block.scalar
        def _(act):
            def copy_onehot(a, b):
                n, q = a.n(b)
                act.wait_ge(hot_turned, n + 1)
                act.wait_ge(er_made, n)
                nc.scalar.copy(onehot_t[:, q, :], p_turn[:, 0:PAIR]).then_inc(hot_copied, 1)

            def exponentiate(a):
                act.wait_ge(soft_back, a.i + 1)
                for j in range(SLOTS):
                    last = nc.scalar.activation(
                        rows[:, a.s, :, j, F:ROW],
                        p_soft[:, j * BH:(j + 1) * BH].rearrange("p (b h) -> p b h", h=HEADS), ACT.Exp)
                last.then_inc(weights, 1)

            def first():
                for h in range(2):
                    for b in range(BATCH):
                        copy_onehot(Batch(0, h), b)
                exponentiate(Batch(0, 0))

            def batch(a, after):
                for st in range(9):
                    if 1 <= st <= BATCH and after >= 2:
                        copy_onehot(a.plus(2), st - 1)
                    if st == 7 and after >= 1:
                        exponentiate(a.plus(1))

            over_batches(act, first, batch, turns)


def project(nc, k, tag, x, parts, er=None):
    padded = x.shape[0] == NP
    with ExitStack() as ctx:
        s = Scope(nc, ctx, tag)
        xin = s.sb("xin", [P, 2, BATCH, F])
        stats = s.sb("stats", [P, 2, BATCH, 6])
        mv = s.sb("mv", [P, 2, BATCH, 2])
        rstd = s.sb("rstd", [P, 2, BATCH])
        shift = s.sb("shift", [P, 2, BATCH])
        hidden = s.sb("hidden", [P, 2, F])
        hidden_t = s.sb("hidden_t", [P, 2, 2, P])
        rows = [s.sb(f"rows{m}", [P, 2, BATCH, part[1]]) for m, part in enumerate(parts)]
        turned = [s.ps(f"turned{i}", [P, 512]) for i in range(2)]
        product = [[s.ps(f"product{m}{i}", [P, 512]) for i in range(2)] for m in range(len(parts))]
        (zeroed, passed, chain, variances, roots, scaled, hid, hid_turned, copied, multiplied) = (s.sem(n) for n in (
            "zeroed", "passed", "chain", "variances", "roots", "scaled", "hidden_ready", "hidden_turned",
            "copied", "multiplied"))
        taken = [s.sem(f"taken{m}") for m in range(len(parts))]
        loaded = [s.sem(f"loaded{i}") for i in range(2)]
        stored = [s.sem(f"stored{i}") for i in range(2)]
        block = ctx.enter_context(nc.Block())
        turns = NBATCH // R

        @block.sync
        def _(sp):
            sp.wait_ge(zeroed, 1)

            def load(a, last=False):
                sp.wait_ge(hid, (a.i + 1) * BATCH)
                load_nodes(sp, x, xin[:, a.q], a.i, loaded[a.q], last and not padded)

            def store(a):
                for m, part in enumerate(parts):
                    sp.wait_ge(taken[m], (a.i + 1) * BATCH + 1)
                    sp.dma_start(part[0][bass.ds(a.i * (BATCH * P), BATCH * P), :].rearrange("(b p) f -> p b f", p=P),
                                 rows[m][:, a.q]).then_inc(stored[a.q], 16)

            for h in range(R):
                load(Batch(0, h))
            with sp.Fori(0, turns - 2) as turn:
                for h in range(R):
                    load(Batch(turn, h + 2))
                    store(Batch(turn, h))
            for h in range(2 * R):
                a = Batch(turns - 2, h)
                if h < R:
                    load(a.plus(2), h == R - 1)
                store(a)
            for q in range(2):
                sp.wait_ge(stored[q], 16 * turns * len(parts))

        @block.vector
        def _(dve):
            def variance(a, ch):
                dve.wait_ge(loaded[a.q], (a.pairs + 1) * 32)
                dve.wait_ge(hid, (a.i + 1) * BATCH)
                for b in range(BATCH):
                    last = dve.bn_stats(stats[:, a.q, b, :], xin[:, a.q, b, :])
                ch.link(last)
                dve.sem_inc(passed, 1)
                for b in range(BATCH):
                    last = dve.bn_aggr(mv[:, a.q, b, :], stats[:, a.q, b, :])
                ch.link(last)
                dve.tensor_scalar(rstd[:, a.q], mv[:, a.q, :, 1], EPS, None, ALU.add).then_inc(variances, 1)

            def scale(a, ch):
                dve.wait_ge(roots, a.i + 1)
                ch.link(dve.reciprocal(rstd[:, a.q], rstd[:, a.q]))
                dve.scalar_tensor_tensor(out=shift[:, a.q], in0=mv[:, a.q, :, 0], scalar=-1.0, in1=rstd[:, a.q],
                                         op0=ALU.mult, op1=ALU.mult).then_inc(scaled, 1)

            def copy(a, b):
                n, q = a.n(b)
                dve.wait_ge(hid_turned, n + 2)
                dve.wait_ge(multiplied, n)
                dve.tensor_copy(hidden_t[:, q].rearrange("p c n -> p (c n)"), turned[q][:, 0:F]).then_inc(copied, 1)

            def take(a, b):
                n, q = a.n(b)
                dve.wait_ge(multiplied, n + 2)
                if b == 0:
                    dve.wait_ge(stored[a.q], a.pairs * (16 * len(parts)))
                dve.tensor_copy(rows[1][:, a.q, b, :], product[1][q][:, 0:parts[1][1]]).then_inc(taken[1], 1)

            def first():
                dve.memset(xin[:], 0.0).then_inc(zeroed, 1)
                dve.sem_inc(copied, 1)
                if len(parts) > 1:
                    dve.sem_inc(taken[1], 1)
                ch = Chain(dve, chain, per=3, turn=0)
                variance(Batch(0, 0), ch)
                scale(Batch(0, 0), ch)
                ch.close()

            def batch(a, after):
                for st in range(BATCH + 1):
                    if st < BATCH:
                        copy(a, st)
                    if st == 0 and after >= 1:
                        ch = Chain(dve, chain, per=3, turn=a.plus(1).i)
                        variance(a.plus(1), ch)
                    if st == 3 and after >= 1:
                        scale(a.plus(1), ch)
                        ch.close()
                    if st and len(parts) > 1:
                        take(a, st - 1)

            over_batches(dve, first, batch, turns)

        @block.scalar
        def _(act):
            def root(a):
                act.wait_ge(variances, a.i + 1)
                nc.scalar.activation(rstd[:, a.q], rstd[:, a.q], ACT.Sqrt).then_inc(roots, 1)

            def relu(a, b):
                n, q = a.n(b)
                if b == 0:
                    act.wait_ge(scaled, a.i + 1)
                act.wait_ge(hid_turned, n)
                nc.scalar.activation(hidden[:, q, :], xin[:, a.q, b, :], ACT.Relu,
                                     bias=shift[:, a.q, b:b + 1], scale=rstd[:, a.q, b:b + 1]).then_inc(hid, 1)

            def take(a, b):
                n, q = a.n(b)
                act.wait_ge(multiplied, n + 2)
                if b == 0:
                    act.wait_ge(stored[a.q], a.pairs * (16 * len(parts)))
                last = nc.scalar.copy(rows[0][:, a.q, b, :], product[0][q][:, 0:parts[0][1]])
                if er is not None:
                    last = nc.scalar.copy(er[:, bass.ds(n * HEADS, HEADS)], product[0][q][:, ROW:WCOLS])
                last.then_inc(taken[0], 1)

            def first():
                act.sem_inc(hid, 2 * BATCH)
                act.sem_inc(taken[0], 1)
                root(Batch(0, 0))
                relu(Batch(0, 0), 0)

            def batch(a, after):
                for b in range(BATCH):
                    if b < BATCH - 1:
                        relu(a, b + 1)
                    elif after >= 1:
                        relu(a.plus(1), 0)
                    if b == 2 and after >= 1:
                        root(a.plus(1))
                    take(a, b)

            over_batches(act, first, batch, turns)

        @block.tensor
        def _(pe):
            def turn_hidden(a, b):
                n, q = a.n(b)
                pe.wait_ge(hid, n + (1 + 2 * BATCH))
                pe.wait_ge(copied, n)
                for c in range(2):
                    last = nc.tensor.transpose(turned[q][:, c * P:(c + 1) * P], hidden[:, q, c * P:(c + 1) * P], k.ident[:])
                last.then_inc(hid_turned, 1)

            def multiply(a, b):
                n, q = a.n(b)
                pe.wait_ge(copied, n + 2)
                for m, (_, _, w, cols, bias) in enumerate(parts):
                    pe.wait_ge(taken[m], n)
                    for c in range(2):
                        last = nc.tensor.matmul(product[m][q][:, 0:cols], hidden_t[:, q, c, :], w[:, c, :],
                                                start=(c == 0), stop=(c == 1 and bias is None))
                    if bias is not None:
                        last = nc.tensor.matmul(product[m][q][:, 0:cols], k.ones_b[0:3, :], k.bias_parts[:, bias:bias + cols],
                                                start=False, stop=True)
                last.then_inc(multiplied, 1)

            def first():
                pe.sem_inc(hid_turned, 1)
                pe.sem_inc(multiplied, 1)
                turn_hidden(Batch(0, 0), 0)

            def batch(a, after):
                for b in range(BATCH):
                    if b < BATCH - 1:
                        turn_hidden(a, b + 1)
                    elif after >= 1:
                        turn_hidden(a.plus(1), 0)
                    multiply(a, b)

            over_batches(pe, first, batch, turns)


SCALE = HD ** -0.5


def dot_layer(nc, k, graph, q_table, kv_table, x_in, x_out):
    KV = 2 * F
    with ExitStack() as ctx:
        s = Scope(nc, ctx, "dot")
        rows = s.sb("rows", [P, R, BATCH, SLOTS, KV])
        q_rows = s.sb("q_rows", [P, 2, BATCH, F])
        x_rows = s.sb("x_rows", [P, 2, BATCH, F])
        place = s.sb("place", [P, R, BATCH * SLOTS], I32)
        onehot = s.sb("onehot", [P, R, BATCH * SLOTS, P])
        onehot_t = s.sb("onehot_t", [P, 2, PAIR])
        logit = s.sb("logit", [P, 2, SLOTS, BH])
        key_bh = s.sb("key_bh", [P, 2, SLOTS, BH])
        key_t = s.sb("key_t", [BH, PAIR])
        wall = s.sb("wall", [BH, PAIR + 1])
        run_max = s.sb("run_max", [BH, PAIR])
        node_max = s.sb("node_max", [BH, PAIR])
        below_max = s.sb("below_max", [BH, 2, PAIR])
        total = s.sb("total", [P, 2, HEADS])
        mean = s.sb("mean", [P, 2, F])
        mean_t = s.sb("mean_t", [P, 2, 2, P])
        p_turn = s.ps("p_turn", [P, 512])
        p_q = [s.ps(f"p_q{i}", [P, 512]) for i in range(2)]
        p_soft = s.ps("p_soft", [P, 512])
        p_sum = [s.ps(f"p_sum{i}", [P, 512]) for i in range(2)]
        p_mean = s.ps("p_mean", [P, 512])
        p_next = s.ps("p_next", [P, 512])
        (placed, hot, hot_turned, hot_copied, spread, dotted, logits, soft_turned, below, soft_back, weights,
         messages, summed, averaged, mean_turned, mean_copied, product, row_done, chain_dot, chain_soft,
         chain_mean, passed, passed_pe) = (s.sem(n) for n in (
             "placed", "hot", "hot_turned", "hot_copied", "spread", "dotted", "logits", "soft_turned", "below",
             "soft_back", "weights", "messages", "summed", "averaged", "mean_turned", "mean_copied", "product",
             "row_done", "chain_dot", "chain_soft", "chain_mean", "passed", "passed_pe"))
        gathered, before = k.pool_dma[0:R], k.pool_count[0:R]
        loaded = [s.sem(f"loaded{i}") for i in range(2)]
        q_loaded = [s.sem(f"q_loaded{i}") for i in range(2)]
        stored = [s.sem(f"stored{i}") for i in range(2)]
        walls_set = s.sem("walls_set")
        rows_clear = s.sem("rows_clear")
        AHEAD = R * BATCH
        block = ctx.enter_context(nc.Block())
        turns = NBATCH // R
        flat_local = graph.local[:].rearrange("p (b j) -> p b j", j=SLOTS)

        @block.gpsimd
        def _(pool):
            pool.wait_ge(rows_clear, 1)

            def gather(a):
                pool.wait_ge(placed, a.i + 1)
                for b in range(BATCH):
                    pool.wait_ge(averaged, a.n(b)[0] + 1)
                    pool.sem_inc(passed, 1)
                    for j in range(SLOTS):
                        c = b * SLOTS + j
                        pool.indirect_dma_start(rows[:, a.s, b, j, :], None, kv_table,
                                                bass.IndirectOffsetOnAxis(place[:, a.s, c:c + 1], 0),
                                                bounds_check=N - 1, oob_is_err=False).then_inc(gathered[a.s], 16)

            with pool.Fori(0, turns) as turn:
                for h in range(R):
                    gather(Batch(turn, h))
            for h in range(R):
                k.pool_count[h] += turns * 16 * BATCH * SLOTS

        @block.sync
        def _(sp):
            def load_q(a, used=None):
                if used:
                    sp.wait_ge(spread, used.i * BATCH + (BATCH + 1))
                sp.dma_start(q_rows[:, a.q], q_table[bass.ds(a.i * (BATCH * P), BATCH * P), :].rearrange(
                    "(b p) f -> p b f", p=P)).then_inc(q_loaded[a.q], 16)

            def load_x(a):
                sp.wait_ge(stored[a.q], a.pairs * 32)
                sp.dma_start(x_rows[:, a.q], x_in[bass.ds(a.i * (BATCH * P), BATCH * P), :].rearrange(
                    "(b p) f -> p b f", p=P)).then_inc(loaded[a.q], 16)

            def store(a, last=False):
                sp.wait_ge(row_done, (a.i + 1) * BATCH)
                m = TAIL_FULL
                if last:
                    n0 = (NBATCH - 1) * BATCH * P
                    sp.dma_start(x_out[n0:n0 + m * P, :].rearrange("(b p) f -> p b f", p=P),
                                 x_rows[:, a.q, 0:m, :]).then_inc(stored[a.q], 16)
                    sp.dma_start(x_out[n0 + m * P:N, :], x_rows[0:TAIL_REST, a.q, m, :]).then_inc(stored[a.q], 16)
                else:
                    v = x_out[bass.ds(a.i * (BATCH * P), BATCH * P), :].rearrange("(b p) f -> p b f", p=P)
                    sp.dma_start(v[:, 0:m, :], x_rows[:, a.q, 0:m, :]).then_inc(stored[a.q], 16)
                    sp.dma_start(v[:, m:BATCH, :], x_rows[:, a.q, m:BATCH, :]).then_inc(stored[a.q], 16)

            for h in range(R):
                load_q(Batch(0, h))
            load_x(Batch(0, 0))
            with sp.Fori(0, turns - 1) as turn:
                for h in range(R):
                    load_x(Batch(turn, h + 1))
                    load_q(Batch(turn, h + 2), Batch(turn, h))
                    store(Batch(turn, h))
            load_x(Batch(turns - 1, 1))
            store(Batch(turns - 1, 0))
            store(Batch(turns - 1, 1), True)
            for q in range(2):
                sp.wait_ge(stored[q], 32 * (NBATCH // 2))

        @block.vector
        def _(dve):
            def make_place(a):
                dve.wait_ge(gathered[a.s], a.round * (16 * BATCH * SLOTS) + before[a.s])
                dve.tensor_copy(place[:, a.s, :], graph.index[:, bass.ds(a.i * (BATCH * SLOTS), BATCH * SLOTS)]
                                ).then_inc(placed, 1)

            def make_onehot(a, b):
                for j in range(SLOTS):
                    last = dve.tensor_scalar(onehot[:, a.s, b * SLOTS + j, :], k.iota_f[:, 0:P],
                                             graph.local[:, bass.ds((a.i * BATCH + b) * SLOTS + j, 1)],
                                             None, ALU.is_equal)
                last.then_inc(hot, 1)

            def dot(a, b):
                n, q = a.n(b)
                ch = Chain(dve, chain_dot, per=1, turn=n)
                if b == 0:
                    dve.wait_ge(gathered[a.s], (a.round + 1) * (16 * BATCH * SLOTS) + before[a.s])
                dve.wait_ge(spread, n + 2)
                kq = rows[:, a.s, b, :, 0:F]
                ins = dve.tensor_tensor(kq, kq, p_q[q][:].rearrange("p (j f) -> p j f", j=SLOTS), ALU.mult)
                ch.link(ins)
                last = dve.tensor_reduce(logit[:, a.q, :, b * HEADS:(b + 1) * HEADS],
                                         kq.rearrange("p j (h d) -> p j h d", h=HEADS), axis=AX.X, op=ALU.add)
                last.then_inc(dotted, 1)

            def copy_keys(a):
                for j in range(SLOTS):
                    last = dve.tensor_copy(
                        key_bh[:, a.q, j, :].rearrange("p (b h) -> p b h", h=HEADS),
                        flat_local[:, bass.ds(a.i * BATCH, BATCH), j:j + 1].to_broadcast([P, BATCH, HEADS]))
                last.then_inc(logits, 1)

            def subtract_max(a, ch):
                dve.wait_ge(soft_turned, a.i + 1)
                ch.link(dve.tensor_copy(key_t[:], p_soft[0:BH, PAIR:2 * PAIR]))
                ch.link(dve.tensor_tensor(wall[:, 1:PAIR], key_t[:, 1:PAIR], key_t[:, 0:PAIR - 1], ALU.is_equal))
                ch.link(dve.tensor_scalar(wall[:, 1:PAIR], wall[:, 1:PAIR], 1.0, FAR, ALU.subtract, ALU.mult))
                ch.link(dve.tensor_tensor_scan(run_max[:], wall[:, 0:PAIR], p_soft[0:BH, 0:PAIR], 0.0,
                                               ALU.add, ALU.max))
                ch.link(dve.tensor_tensor_scan(node_max[:, ::-1], wall[:, PAIR:0:-1], run_max[:, ::-1], 0.0,
                                               ALU.add, ALU.max))
                dve.tensor_tensor(below_max[:, a.q], p_soft[0:BH, 0:PAIR], node_max[:], ALU.subtract).then_inc(below, 1)

            def weigh(a, b):
                if b == 0:
                    dve.wait_ge(weights, a.i + 1)
                v = rows[:, a.s, b, :, F:KV].rearrange("p j (h d) -> p j h d", h=HEADS)
                w = rows[:, a.s, b, :, F - HEADS:F]
                for j in range(SLOTS):
                    last = dve.tensor_tensor(v[:, j], v[:, j], w[:, j].unsqueeze(2).to_broadcast([P, HEADS, HD]),
                                             ALU.mult)
                last.then_inc(messages, 1)

            def average(a, b):
                n, q = a.n(b)
                ch = Chain(dve, chain_mean, per=2, turn=n)
                dve.wait_ge(summed, n + 1)
                ch.link(dve.tensor_scalar(total[:, q], p_sum[q][:, 0:HEADS], TINY, None, ALU.max))
                ch.link(dve.reciprocal(total[:, q], total[:, q]))
                dve.wait_ge(mean_turned, n)
                dve.tensor_tensor(mean[:, q].rearrange("p (h d) -> p h d", h=HEADS),
                                  p_sum[q][:, HEADS:ROW].rearrange("p (h d) -> p h d", h=HEADS),
                                  total[:, q].unsqueeze(2).to_broadcast([P, HEADS, HD]), ALU.mult).then_inc(averaged, 1)

            def finish(a, b):
                n, q = a.n(b)
                dve.wait_ge(product, n + 2)
                if b == 0:
                    dve.wait_ge(loaded[a.q], (a.pairs + 1) * 16)
                v = x_rows[:, a.q, b, :]
                dve.tensor_tensor(v, p_next[:, 0:F], v, ALU.add).then_inc(row_done, 1)

            SOFT = 5

            def first():
                dve.memset(rows[:], 0.0).then_inc(rows_clear, 1)
                dve.wait_ge(rows_clear, 1)
                dve.memset(wall[:, 0:1], -FAR).then_inc(walls_set, 1)
                dve.memset(wall[:, PAIR:PAIR + 1], -FAR).then_inc(walls_set, 1)
                dve.wait_ge(walls_set, 2)
                dve.sem_inc(averaged, AHEAD)
                dve.sem_inc(dotted, 1)
                for h in range(R):
                    make_place(Batch(0, h))
                a = Batch(0, 0)
                for b in range(BATCH):
                    make_onehot(a, b)
                for b in range(BATCH):
                    dot(a, b)
                copy_keys(a)
                ch = Chain(dve, chain_soft, per=SOFT, turn=0)
                subtract_max(a, ch)
                ch.close()

            def batch(a, after):
                for st in range(9):
                    if st == 0 and after >= 2:
                        make_place(a.plus(2))
                    if st < BATCH:
                        weigh(a, st)
                    if st < BATCH and after >= 1:
                        make_onehot(a.plus(1), st)
                    if 1 <= st <= BATCH:
                        average(a, st - 1)
                    if 2 <= st:
                        finish(a, st - 2)
                    if 1 <= st <= BATCH and after >= 1:
                        dot(a.plus(1), st - 1)
                if after >= 1:
                    copy_keys(a.plus(1))
                    ch = Chain(dve, chain_soft, per=SOFT, turn=a.plus(1).i)
                    subtract_max(a.plus(1), ch)
                    ch.close()

            over_batches(dve, first, batch, turns)

        @block.tensor
        def _(pe):
            def turn_onehot(a, b):
                n, q = a.n(b)
                pe.wait_ge(hot, n + 1)
                pe.wait_ge(hot_copied, n)
                for j in range(SLOTS):
                    last = nc.tensor.transpose(p_turn[:, j * P:(j + 1) * P], onehot[:, a.s, b * SLOTS + j, :], k.ident[:])
                last.then_inc(hot_turned, 1)

            def spread_q(a, b):
                n, q = a.n(b)
                pe.wait_ge(hot_copied, n + 1)
                pe.wait_ge(dotted, n)
                if b == 0:
                    pe.wait_ge(q_loaded[a.q], (a.pairs + 1) * 16)
                for j in range(SLOTS):
                    last = nc.tensor.matmul(p_q[q][:, j * F:(j + 1) * F], onehot_t[:, q, j * P:(j + 1) * P],
                                            q_rows[:, a.q, b, :], start=True, stop=True)
                last.then_inc(spread, 1)

            def turn_soft(a):
                pe.wait_ge(logits, a.i + 1)
                pe.wait_ge(weights, a.i)
                pe.sem_inc(passed_pe, 1)
                for x, c in ((logit, 0), (key_bh, PAIR)):
                    for j in range(SLOTS):
                        last = nc.tensor.transpose(p_soft[0:BH, c + j * P:c + (j + 1) * P], x[:, a.q, j, :], k.ident[:])
                last.then_inc(soft_turned, 1)

            def turn_back(a):
                pe.wait_ge(below, a.i + 1)
                pe.sem_inc(passed_pe, 1)
                for j in range(SLOTS):
                    last = nc.tensor.transpose(p_soft[:, j * BH:(j + 1) * BH], below_max[:, a.q, j * P:(j + 1) * P],
                                               k.ident[0:BH, 0:BH])
                last.then_inc(soft_back, 1)

            def add_up(a, b):
                n, q = a.n(b)
                pe.wait_ge(messages, n + 1)
                pe.wait_ge(averaged, n + (AHEAD - 1))
                for j in range(SLOTS):
                    last = nc.tensor.matmul(p_sum[q][:, 0:ROW], onehot[:, a.s, b * SLOTS + j, :], rows[:, a.s, b, j, F - HEADS:KV],
                                            start=(j == 0), stop=(j == SLOTS - 1))
                last.then_inc(summed, 1)

            def turn_mean(a, b):
                n, q = a.n(b)
                pe.wait_ge(averaged, n + (AHEAD + 1))
                pe.wait_ge(mean_copied, n)
                for c in range(2):
                    last = nc.tensor.transpose(p_mean[:, c * P:(c + 1) * P], mean[:, q, c * P:(c + 1) * P], k.ident[:])
                last.then_inc(mean_turned, 1)

            def multiply(a, b):
                n, q = a.n(b)
                pe.wait_ge(mean_copied, n + 1)
                pe.wait_ge(row_done, n)
                for c in range(2):
                    nc.tensor.matmul(p_next[:, 0:F], mean_t[:, q, c, :], k.w_o[:, c, :], start=(c == 0), stop=False)
                nc.tensor.matmul(p_next[:, 0:F], k.ones_b[0:3, :], k.bias_parts[:, 3 * F:4 * F],
                                 start=False, stop=True).then_inc(product, 1)

            def first():
                for x in (mean_turned, product, spread):
                    pe.sem_inc(x, 1)
                a = Batch(0, 0)
                for b in range(BATCH + 1):
                    if b:
                        spread_q(a, b - 1)
                    if b < BATCH:
                        turn_onehot(a, b)
                turn_soft(a)
                turn_back(a)

            def batch(a, after):
                for st in range(9):
                    if st < BATCH:
                        add_up(a, st)
                    if 1 <= st <= BATCH and after >= 1:
                        spread_q(a.plus(1), st - 1)
                    if st < BATCH and after >= 1:
                        turn_onehot(a.plus(1), st)
                    if 1 <= st <= BATCH:
                        turn_mean(a, st - 1)
                    if 2 <= st:
                        multiply(a, st - 2)
                if after >= 1:
                    turn_soft(a.plus(1))
                    turn_back(a.plus(1))

            over_batches(pe, first, batch, turns)

        @block.scalar
        def _(act):
            def copy_onehot(a, b):
                n, q = a.n(b)
                act.wait_ge(hot_turned, n + 1)
                act.wait_ge(spread, n)
                nc.scalar.copy(onehot_t[:, q, :], p_turn[:, 0:PAIR]).then_inc(hot_copied, 1)

            def exponentiate(a):
                act.wait_ge(soft_back, a.i + 1)
                for j in range(SLOTS):
                    last = nc.scalar.activation(
                        rows[:, a.s, :, j, F - HEADS:F],
                        p_soft[:, j * BH:(j + 1) * BH].rearrange("p (b h) -> p b h", h=HEADS), ACT.Exp, scale=SCALE)
                last.then_inc(weights, 1)

            def copy_mean(a, b):
                n, q = a.n(b)
                act.wait_ge(mean_turned, n + 2)
                act.wait_ge(product, n)
                nc.scalar.copy(mean_t[:, q].rearrange("p c n -> p (c n)"), p_mean[:, 0:F]).then_inc(mean_copied, 1)

            def first():
                for b in range(BATCH):
                    copy_onehot(Batch(0, 0), b)
                exponentiate(Batch(0, 0))

            def batch(a, after):
                for st in range(9):
                    if st < BATCH and after >= 1:
                        copy_onehot(a.plus(1), st)
                    if 1 <= st <= BATCH:
                        copy_mean(a, st - 1)
                if after >= 1:
                    exponentiate(a.plus(1))

            over_batches(act, first, batch, turns)


def gnn_kernel(nc, x, src, dst, W, al, ar, b, w_qkv, b_qkv, w_o, b_o, out):
    with ExitStack() as ctx:
        s = Scope(nc, ctx, "kept")
        k = Constants(s)
        k.w_gat = s.sb("w_gat", [P, 3, 2, WCOLS])
        k.b_col = s.sb("b_col", [P, 3, 2])
        k.b2_row = s.sb("b2_row", [P, F])
        k.w_qkv = s.sb("w_qkv", [P, 2, 3 * F])
        k.w_o = s.sb("w_o", [P, 2, F])
        k.bias_parts = s.sb("bias_parts", [3, 4 * F], BF16)
        k.er = s.sb("er", [P, NBK * HEADS])
        index = [s.sb(f"index{g}", [P, NBK * SLOTS], I32) for g in range(2)]
        local = [s.sb(f"local{g}", [P, NBK * SLOTS]) for g in range(2)]
        places = [nc.dram_tensor(f"places{g}", (SP_ROWS, 2), I32, kind="Internal").ap() for g in range(2)]
        tables = [nc.dram_tensor(f"table{i}", (NP, ROW), F32, kind="Internal").ap() for i in range(2)]
        x2 = nc.dram_tensor("x2", (NP, F), F32, kind="Internal").ap()
        q_table = nc.dram_tensor("q_table", (NP, F), F32, kind="Internal").ap()
        kv_table = nc.dram_tensor("kv_table", (NP, 2 * F), F32, kind="Internal").ap()

        make_constants(nc, k)
        load_weights(nc, k, W, al, ar, b, w_qkv, b_qkv, w_o, b_o)
        distribute(nc, k, [dst, src], [src, dst], places)
        sort_buckets(nc, k, places, index, local)
        by_dst, by_src = (Graph(index[g], local[g]) for g in range(2))
        project(nc, k, "first", x, [(tables[0], ROW, k.w_gat[:, 0], WCOLS, None)], k.er)
        gat_layer(nc, k, by_dst, tables[0], 0, tables[1])
        gat_layer(nc, k, by_dst, tables[1], 1, tables[0])
        last_gat_layer(nc, k, by_dst, tables[0], x, x2)
        project(nc, k, "qkv", x2, [(q_table, F, k.w_qkv[:, :, 0:F], F, 0),
                                   (kv_table, 2 * F, k.w_qkv[:, :, F:3 * F], 2 * F, F)])
        dot_layer(nc, k, by_src, q_table, kv_table, x2, out)


def kernel(x, src, dst, L0_gnn_W, L0_gnn_al, L0_gnn_ar, L0_gnn_b, L1_gnn_Wq, L1_gnn_bq, L1_gnn_Wk, L1_gnn_bk,
           L1_gnn_Wv, L1_gnn_bv, L1_gnn_Wo, L1_gnn_bo):
    import numpy as np
    import concourse.bacc as bacc
    from concourse.bass_utils import run_bass_kernel_spmd

    def head_major(a):
        a = np.asarray(a)
        return a.reshape(a.shape[:-1] + (HD, HEADS)).swapaxes(-1, -2).reshape(a.shape)

    w_qkv = np.concatenate([head_major(np.asarray(w).T) for w in (L1_gnn_Wq, L1_gnn_Wk, L1_gnn_Wv)], axis=1)
    b_qkv = np.concatenate([head_major(b) for b in (L1_gnn_bq, L1_gnn_bk, L1_gnn_bv)])
    given = {
        "x": x, "src": src, "dst": dst, "W": L0_gnn_W, "al": L0_gnn_al, "ar": L0_gnn_ar, "b": L0_gnn_b,
        "w_qkv": w_qkv, "b_qkv": b_qkv, "w_o": head_major(L1_gnn_Wo).T, "b_o": L1_gnn_bo,
    }
    nc = bacc.Bacc("TRN2", target_bir_lowering=False, num_devices=1)
    arrays, args = {}, []
    for name, a in given.items():
        a = np.ascontiguousarray(a)
        arrays[f"in_{name}"] = a
        args.append(nc.dram_tensor(f"in_{name}", a.shape, mybir.dt.from_np(a.dtype), kind="ExternalInput").ap())
    out = nc.dram_tensor("out_0", (N, F), F32, kind="ExternalOutput").ap()
    gnn_kernel(nc, *args, out)
    return run_bass_kernel_spmd(nc, [arrays], core_ids=[0]).results[0]["out_0"]
```

```python
import concourse.bass as bass
from concourse import mybir
from contextlib import ExitStack

F32 = mybir.dt.float32
BF16 = mybir.dt.bfloat16
F16 = mybir.dt.float16
I32 = mybir.dt.int32
ALU = mybir.AluOpType
ACT = mybir.ActivationFunctionType
AX = mybir.AxisListType

N = 50000
E = 75000
F = 256
HEADS = 8
HD = F // HEADS
P = 128
BATCH = 7
NBK = 392
NBATCH = NBK // BATCH
ROW = F + HEADS
SLOTS = 2
SP_ROWS = P * NBK * SLOTS
T = 588
U = 7
NO_KEY = P
NO_NODE = N


class Chain:

    def __init__(self, eng, sem, per=0, turn=0, base=0):
        self.eng, self.sem, self.per, self.k = eng, sem, per, 0
        self.at = turn * per + base if per else base

    def done(self, ins):
        self.k += 1
        ins.then_inc(self.sem, 1)
        return self.at + self.k

    def link(self, ins):
        self.eng.wait_ge(self.sem, self.done(ins))

    def close(self):
        assert self.k == self.per, f"a turn has {self.k} increments, not {self.per}"


class Scope:

    def __init__(self, nc, ctx, tag):
        self.nc, self.ctx, self.tag, self.sems = nc, ctx, tag, []
        ctx.callback(self.clear)

    def sb(self, name, shape, dt=F32):
        return self.ctx.enter_context(self.nc.sbuf_tensor(f"{self.tag}_{name}", shape, dt))

    def ps(self, name, shape, dt=F32):
        return self.ctx.enter_context(self.nc.psum_tensor(f"{self.tag}_{name}", shape, dt))

    def sem(self, name):
        self.sems.append(self.ctx.enter_context(self.nc.semaphore(f"{self.tag}_{name}")))
        return self.sems[-1]

    def clear(self):
        if self.sems:
            with self.nc.Block() as block:

                @block.sync
                def _(sp):
                    for sem in self.sems:
                        sp.sem_clear(sem)


def make_constants(nc, k):
    with ExitStack() as ctx:
        s = Scope(nc, ctx, "const")
        filled, cast = s.sem("filled"), s.sem("cast")
        block = ctx.enter_context(nc.Block())

        @block.gpsimd
        def _(pool):
            pool.memset(k.ones[:], 1.0).then_inc(filled, 1)
            pool.iota(k.iota_f[:], pattern=[[1, NBK]], base=0, channel_multiplier=0,
                      allow_small_or_imprecise_dtypes=True).then_inc(filled, 1)
            pool.iota(k.slot_f[:], pattern=[[P, SLOTS]], base=0, channel_multiplier=1,
                      allow_small_or_imprecise_dtypes=True).then_inc(filled, 1)
            pool.wait_ge(filled, 3)
            pool.affine_select(out=k.ident[:], in_=k.ones[:], compare_op=ALU.is_equal, fill=0.0,
                               base=0, pattern=[[1, P]], channel_multiplier=-1).then_inc(filled, 1)
            pool.affine_select(out=k.tri_f[:], in_=k.ones[:], compare_op=ALU.is_gt, fill=0.0,
                               base=0, pattern=[[1, P]], channel_multiplier=-1).then_inc(filled, 1)

        @block.vector
        def _(dve):
            dve.wait_ge(filled, 5)
            ch = Chain(dve, cast)
            dve.tensor_copy(k.iota_h[:], k.iota_f[:])
            dve.tensor_scalar(k.balance_b[:], k.iota_f[:, 0:SLOTS * P], 2.0, float(1 - SLOTS * P), ALU.mult, ALU.add)
            dve.tensor_copy(k.ident_b[:], k.ident[:])
            dve.tensor_copy(k.before_b[:], k.tri_f[:])
            dve.tensor_tensor(k.notbefore_b[:], k.ones[:], k.tri_f[:], ALU.subtract)
            dve.tensor_scalar(k.all256_b[:], k.ones[:], 256.0, None, ALU.mult)
            dve.tensor_scalar(k.ones_b[:], k.ones[:], 1.0, None, ALU.mult)
            dve.memset(k.zeros_b[:], 0.0)
            ch.link(dve.memset(k.fill_i[:, :, 0:1], NO_NODE))
            ch.link(dve.memset(k.fill_i[:, :, 1:2], NO_KEY))


def distribute(nc, k, keys, others, places):
    NG = 2
    with ExitStack() as ctx:
        s = Scope(nc, ctx, "deal")
        key_i = [s.sb(f"key{g}", [P, T], I32) for g in range(NG)]
        oth_i = [s.sb(f"oth{g}", [P, T], I32) for g in range(NG)]
        tmp_i = s.sb("tmp", [P, T], I32)
        bucket = [s.sb(f"bucket{g}", [P, T]) for g in range(NG)]
        pair = [s.sb(f"pair{g}", [P, T, 2], I32) for g in range(NG)]
        onehot = [s.sb(f"onehot{g}", [P, 2, NBK], BF16) for g in range(NG)]
        most = s.sb("most", [P, NG])
        junk = [s.sb(f"junk{g}", [P, 2, NBK], BF16) for g in range(NG)]
        rank = [s.sb(f"rank{g}", [P, U]) for g in range(NG)]
        wrap = [s.sb(f"wrap{g}", [P, U]) for g in range(NG)]
        lin = [s.sb(f"lin{g}", [P, U]) for g in range(NG)]
        place = [s.sb(f"place{g}", [P, 2, U], I32) for g in range(NG)]
        payload = [s.sb(f"payload{g}", [P, 2, U, 2], I32) for g in range(NG)]
        earlier = [s.ps(f"earlier{g}", [P, 512]) for g in range(NG)]
        loaded, filled, padded = s.sem("loaded"), s.sem("filled"), s.sem("padded")
        chain = s.sem("chain")
        keyed = s.sem("keyed")
        hot = [s.sem(f"hot{g}") for g in range(NG)]
        counted = [s.sem(f"counted{g}") for g in range(NG)]
        ranked = [s.sem(f"ranked{g}") for g in range(NG)]
        placed = [s.sem(f"placed{g}") for g in range(NG)]
        passed = s.sem("passed")
        scattered = [[k.pool_dma[2 * g + h] for h in range(2)] for g in range(NG)]
        block = ctx.enter_context(nc.Block())
        full, rest = E // T, E % T
        turns = T // (2 * U)

        @block.sync
        def _(sp):
            for g in range(NG):
                sp.dma_start(places[g].rearrange("(p r) c -> p (r c)", p=P),
                             k.fill_i[:].rearrange("p r c -> p (r c)")).then_inc(filled, 16)
            sp.wait_ge(padded, 1)
            for g in range(NG):
                for to, of in ((key_i[g], keys[g]), (oth_i[g], others[g])):
                    for lo, hi in ((0, 112), (112, full)):
                        sp.dma_start(to[lo:hi, :],
                                     of[lo * T:hi * T].rearrange("(p t) -> p t", t=T)).then_inc(loaded, 16)
                    sp.dma_start(to[full:full + 1, 0:rest],
                                 of[full * T:E].rearrange("(p t) -> p t", p=1)).then_inc(loaded, 16)

        @block.vector
        def _(dve):
            ch = Chain(dve, chain)
            for g in range(NG):
                dve.memset(key_i[g][:], (NBK - 1) * P)
                ch.link(dve.memset(oth_i[g][:], 0))
            dve.sem_inc(padded, 1)
            dve.wait_ge(loaded, 16 * 3 * 2 * NG)
            for g in range(NG):
                dve.tensor_copy(pair[g][:, :, 0], oth_i[g][:])
                ch.link(dve.tensor_scalar(pair[g][:, :, 1], key_i[g][:], P - 1, None, ALU.bitwise_and))
                ch.link(dve.tensor_scalar(tmp_i[:], key_i[g][:], 7, None, ALU.logical_shift_right))
                ch.link(dve.tensor_copy(bucket[g][:], tmp_i[:]))
            base = ch.k
            with dve.Fori(0, turns) as turn:
                ch = Chain(dve, chain, per=4 * NG, turn=turn, base=base)
                for half in range(2):
                    for u in range(U):
                        t = turn * (2 * U) + (half * U + u)
                        slot = (half * U + u) % 2
                        for g in range(NG):
                            dve.wait_ge(counted[g], 2 * t)
                            dve.tensor_scalar(onehot[g][:, slot, :], k.iota_h[:], bucket[g][:, bass.ds(t, 1)],
                                              None, ALU.is_equal).then_inc(hot[g], 1)
                        for g in range(NG):
                            dve.wait_ge(counted[g], 2 * t + 1)
                            dve.wait_ge(hot[g], t + 1)
                            dve.tensor_tensor_reduce(out=junk[g][:, slot, :], in0=earlier[g][:, 0:NBK],
                                                     in1=onehot[g][:, slot, :], scale=1.0, scalar=0.0,
                                                     op0=ALU.mult, op1=ALU.add,
                                                     accum_out=rank[g][:, u:u + 1]).then_inc(ranked[g], 1)
                    t0 = turn * (2 * U) + half * U
                    for g in range(NG):
                        dve.wait_ge(ranked[g], t0 + U)
                        dve.tensor_scalar(wrap[g][:], rank[g][:], float(P), float(1 - P * NBK * SLOTS),
                                          ALU.is_ge, ALU.mult)
                        ch.link(dve.tensor_scalar(lin[g][:], rank[g][:], float(NBK * SLOTS), None, ALU.mult))
                        ch.link(dve.scalar_tensor_tensor(out=lin[g][:], in0=bucket[g][:, bass.ds(t0, U)],
                                                         scalar=float(SLOTS), in1=lin[g][:],
                                                         op0=ALU.mult, op1=ALU.add))
                        dve.wait_ge(scattered[g][half], turn * (16 * U))
                        dve.tensor_tensor(place[g][:, half, :], lin[g][:], wrap[g][:], ALU.add).then_inc(placed[g], 1)
                        dve.tensor_copy(payload[g][:, half, :, :],
                                        pair[g][:, bass.ds(t0, U), :]).then_inc(placed[g], 1)
                ch.close()
            ch = Chain(dve, chain, base=base + 4 * NG * turns)
            for g in range(NG):
                dve.wait_ge(counted[g], 2 * T)
                ch.link(dve.tensor_reduce(most[:, g:g + 1], earlier[g][:, 0:NBK - 1], axis=AX.X, op=ALU.max))
            ch.link(dve.tensor_tensor(most[:, 0:1], most[:, 0:1], most[:, 1:2], ALU.max))
            ch.link(dve.tensor_scalar(k.crowded[:], most[:, 0:1], float(P * SLOTS), None, ALU.is_gt))

        @block.tensor
        def _(pe):
            for g in range(NG):
                nc.tensor.matmul(earlier[g][:, 0:NBK], k.zeros_b[:, 0:P], k.zeros_b[:], start=True, stop=True,
                                 skip_group_check=True)
            with pe.Fori(0, turns) as turn:
                for v in range(2 * U):
                    t = turn * (2 * U) + v
                    for g in range(NG):
                        pe.wait_ge(hot[g], t + 1)
                        nc.tensor.matmul(earlier[g][:, 0:NBK], k.before_b[:], onehot[g][:, v % 2, :],
                                         start=False, stop=True, skip_group_check=True).then_inc(counted[g], 1)
                    for g in range(NG):
                        pe.wait_ge(ranked[g], t + 1)
                        nc.tensor.matmul(earlier[g][:, 0:NBK], k.notbefore_b[:], onehot[g][:, v % 2, :],
                                         start=False, stop=True, skip_group_check=True).then_inc(counted[g], 1)

        @block.gpsimd
        def _(pool):
            pool.wait_ge(filled, 16 * NG)
            with pool.Fori(0, turns) as turn:
                for half in range(2):
                    for g in range(NG):
                        pool.wait_ge(placed[g], (turn * 2 + half + 1) * 2)
                        pool.sem_inc(passed, 1)
                        for u in range(U):
                            pool.indirect_dma_start(
                                places[g], bass.IndirectOffsetOnAxis(place[g][:, half, u:u + 1], 0),
                                payload[g][:, half, u, :], None,
                                bounds_check=SP_ROWS - 1, oob_is_err=False).then_inc(scattered[g][half], 16)
            for g in range(NG):
                for half in range(2):
                    pool.wait_ge(scattered[g][half], turns * 16 * U)
                    k.pool_count[2 * g + half] += turns * 16 * U


def sort_buckets(nc, k, places, index, local):
    G, RING, AHEAD = 14, 7, 3
    with ExitStack() as ctx:
        s = Scope(nc, ctx, "sort")
        raw = s.sb("raw", [P, NBK, SLOTS, 2], I32)
        tmp_i = s.sb("tmp", [P, NBK, SLOTS], I32)
        loc = s.sb("loc", [P, NBK + AHEAD + 1, SLOTS])
        code = s.sb("code", [P, NBK, SLOTS])
        parts = s.sb("parts", [P, NBK, SLOTS, 3], BF16)
        diag = s.sb("diag", [P, RING, SLOTS, P], BF16)
        junk = s.sb("junk", [P, 2, SLOTS, SLOTS * P], BF16)
        balance = s.sb("balance", [P, G, SLOTS])
        perm = s.sb("perm", [P, 2, SLOTS, SLOTS * P], BF16)
        slot_row = s.sb("slotrow", [P, SLOTS, P], BF16)
        codes = [s.ps(f"codes{i}", [P, 512]) for i in range(RING)]
        moved = s.ps("moved", [P, 512])
        took = s.sb("took", [P, G * SLOTS, 3])
        loaded, chain = s.sem("loaded"), s.sem("chain")
        diag_ready, codes_ready = s.sem("diag_ready"), s.sem("codes_ready")
        set_up, balanced = s.sem("set_up"), s.sem("balanced")
        perm_ready, perm_used, moved_read = s.sem("perm_ready"), s.sem("perm_used"), s.sem("moved_read")
        block = ctx.enter_context(nc.Block())
        turns = NBK // G
        NG = len(places)

        @block.sync
        def _(sp):
            for g in range(NG):
                if g:
                    sp.wait_ge(set_up, g)
                sp.dma_start(raw[:].rearrange("p b j c -> p (b j c)"),
                             places[g].rearrange("(p r) c -> p (r c)", p=P)).then_inc(loaded, 16)

        @block.vector
        def _(dve):
            ch = Chain(dve, chain)
            for j in range(SLOTS):
                ch.link(dve.tensor_scalar(slot_row[:, j, :], k.ident[:], k.slot_f[:, j:j + 1], None, ALU.mult))
            base = ch.k
            for g in range(NG):
                dve.wait_ge(loaded, 16 * (g + 1))
                if g:
                    dve.wait_ge(balanced, g * (NBK + AHEAD) + RING)
                    dve.wait_ge(perm_used, g * NBK + 1)
                ch = Chain(dve, chain, base=base)
                dve.memset(loc[:, NBK:NBK + AHEAD + 1, :], 0.0)
                ch.link(dve.tensor_copy(loc[:, 0:NBK, :], raw[:, :, :, 1]))
                dve.tensor_copy(parts[:, :, :, 2], loc[:, 0:NBK, :])
                ch.link(dve.tensor_scalar(tmp_i[:], raw[:, :, :, 0], 8, None, ALU.logical_shift_right))
                ch.link(dve.tensor_copy(parts[:, :, :, 0], tmp_i[:]))
                ch.link(dve.tensor_scalar(tmp_i[:], raw[:, :, :, 0], 255, None, ALU.bitwise_and))
                ch.link(dve.tensor_copy(parts[:, :, :, 1], tmp_i[:]))
                for j in range(SLOTS):
                    last = dve.tensor_scalar(code[:, :, j], loc[:, 0:NBK, j], 256.0, k.slot_f[:, j:j + 1],
                                             ALU.mult, ALU.add)
                ch.link(last)
                dve.sem_inc(set_up, 1)
                base += ch.k
                flat_loc = loc[:].rearrange("p b j -> p (b j)")

                def diagonals(slot, column):
                    for j in range(SLOTS):
                        last = dve.tensor_scalar(diag[:, slot, j, :], k.ident_b[:],
                                                 flat_loc[:, bass.ds(column + j, 1)], None, ALU.mult)
                    last.then_inc(diag_ready, 1)

                for i in range(AHEAD + 1):
                    diagonals(i, i * SLOTS)
                with dve.Fori(0, turns) as turn:
                    ch = Chain(dve, chain, per=1, turn=turn, base=base)
                    n0 = turn * G + g * NBK
                    m0 = turn * G + g * (NBK + AHEAD)
                    for i in range(G):
                        dve.wait_ge(balanced, m0 + i + RING + 1)
                        dve.wait_ge(perm_used, n0 + i)
                        for j in range(SLOTS):
                            last = dve.tensor_scalar(perm[:, i % 2, j, :], k.balance_b[:], balance[:, i, j:j + 1],
                                                     None, ALU.is_equal)
                        last.then_inc(perm_ready, 1)
                        diagonals((i + AHEAD + 1) % RING, turn * (G * SLOTS) + (i + AHEAD + 1) * SLOTS)
                    dve.wait_ge(perm_used, n0 + G + 1)
                    ch.link(dve.tensor_copy(took[:].rearrange("p s c -> p (s c)"), moved[:, 0:G * SLOTS * 3]))
                    at = bass.ds(turn * (G * SLOTS), G * SLOTS)
                    dve.scalar_tensor_tensor(out=index[g][:, at], in0=took[:, :, 0], scalar=256.0, in1=took[:, :, 1],
                                             op0=ALU.mult, op1=ALU.add)
                    dve.tensor_copy(local[g][:, at], took[:, :, 2]).then_inc(moved_read, 1)
                    ch.close()
                base += turns

        @block.scalar
        def _(act):
            act.sem_inc(balanced, RING)
            flat_code = code[:].rearrange("p b j -> p (b j)")
            for g in range(NG):
                act.wait_ge(set_up, g + 1)
                with act.Fori(0, turns) as turn:
                    m0 = turn * G + g * (NBK + AHEAD)
                    for i in range(G):
                        act.wait_ge(codes_ready, m0 + i + 1)
                        act.wait_ge(balanced, m0 + i + RING - 1)
                        for j in range(SLOTS):
                            last = nc.scalar.activation(
                                junk[:, i % 2, j, :], codes[i % RING][:, 0:SLOTS * P], ACT.Sign,
                                bias=flat_code[:, bass.ds(turn * (G * SLOTS) + (i * SLOTS + j), 1)], scale=-1.0,
                                accum_out=balance[:, i, j:j + 1])
                        last.then_inc(balanced, 1)
                act.wait_ge(codes_ready, (g + 1) * (NBK + AHEAD))
                act.wait_ge(balanced, (g + 1) * (NBK + AHEAD) + RING - AHEAD)
                act.sem_inc(balanced, AHEAD)

        @block.tensor
        def _(pe):
            pe.sem_inc(perm_used, 1)
            for g in range(NG):
                m0 = g * (NBK + AHEAD)

                def spread(slot, m):
                    pe.wait_ge(diag_ready, m + g + 1)
                    pe.wait_ge(balanced, m + 1)
                    to = codes[slot][:, 0:SLOTS * P]
                    nc.tensor.matmul(to, k.all256_b[:], diag[:, slot, :, :], start=True, stop=False)
                    nc.tensor.matmul(to, k.ones_b[:], slot_row[:], start=False, stop=True).then_inc(codes_ready, 1)

                for i in range(AHEAD):
                    spread(i, m0 + i)
                with pe.Fori(0, turns) as turn:
                    n0 = turn * G + g * NBK
                    for i in range(G):
                        spread((i + AHEAD) % RING, turn * G + (i + AHEAD + m0))
                        pe.wait_ge(perm_ready, n0 + i + 1)
                        if i == 0:
                            pe.wait_ge(moved_read, turn + g * turns)
                        for hi in range(SLOTS):
                            c0 = (i * SLOTS + hi) * 3
                            for j in range(SLOTS):
                                last = nc.tensor.matmul(
                                    moved[:, c0:c0 + 3], perm[:, i % 2, j, hi * P:(hi + 1) * P],
                                    parts[:].rearrange("p b j c -> p (b j c)")[
                                        :, bass.ds(turn * (G * SLOTS * 3) + (i * SLOTS + j) * 3, 3)],
                                    start=(j == 0), stop=(j == SLOTS - 1))
                        last.then_inc(perm_used, 1)


class Constants:
    def __init__(self, s):
        self.pool_dma = [s.sem(f"pool_dma{i}") for i in range(4)]
        self.pool_count = [0] * 4
        self.crowded = s.sb("crowded", [P, 1], I32)
        self.ones = s.sb("ones", [P, P])
        self.ident = s.sb("ident", [P, P])
        self.tri_f = s.sb("tri", [P, P])
        self.iota_f = s.sb("iota", [P, NBK])
        self.slot_f = s.sb("slot", [P, SLOTS])
        self.iota_h = s.sb("iota_h", [P, NBK], F16)
        self.balance_b = s.sb("balance_b", [P, SLOTS * P], BF16)
        self.ident_b = s.sb("ident_b", [P, P], BF16)
        self.before_b = s.sb("before_b", [P, P], BF16)
        self.notbefore_b = s.sb("notbefore_b", [P, P], BF16)
        self.all256_b = s.sb("all256_b", [P, P], BF16)
        self.ones_b = s.sb("ones_b", [P, P], BF16)
        self.zeros_b = s.sb("zeros_b", [P, NBK], BF16)
        self.fill_i = s.sb("fill", [P, NBK * SLOTS, 2], I32)


NP = NBK * P
WCOLS = F + 2 * HEADS
EPS = 1e-5
SLOPE_ATTN = 0.2
SLOPE_ACT = 0.01
FAR = 1e30
TINY = 1e-30
TAIL = N - (NBK - BATCH) * P
TAIL_FULL = TAIL // P
TAIL_REST = TAIL % P


class Graph:

    def __init__(self, index, local):
        self.index, self.local = index, local


def load_weights(nc, k, W, al, ar, b, w_qkv, b_qkv, w_o, b_o):
    L = 3
    with ExitStack() as ctx:
        s = Scope(nc, ctx, "weights")
        a_rows = s.sb("a_rows", [P, 2, L, F])
        prod = s.sb("prod", [P, 2, F])
        rest = s.sb("rest", [1, F])
        part = s.sb("part", [1, 3, F], BF16)
        loaded, chain, moved = s.sem("loaded"), s.sem("chain"), s.sem("moved")
        split = s.sem("split")
        block = ctx.enter_context(nc.Block())

        @block.sync
        def _(sp):
            for l in range(L):
                sp.dma_start(k.w_gat[:, l, :, 0:F], W[l].rearrange("(c p) n -> p c n", p=P)).then_inc(loaded, 16)
                for i, a in enumerate((al, ar)):
                    sp.dma_start(a_rows[:, i, l, :], a[l:l + 1].rearrange("o h d -> o (h d)").to_broadcast([P, F])
                                 ).then_inc(loaded, 16)
            with nc.allow_non_contiguous_dma(reason="256 words of a bias, once"):
                sp.dma_start(k.b_col[:], b.rearrange("l (c p) -> p l c", p=P)).then_inc(loaded, 16)
            sp.dma_start(k.b2_row[:], b[2:3].to_broadcast([P, F])).then_inc(loaded, 16)
            sp.dma_start(k.w_qkv[:], w_qkv.rearrange("(c p) n -> p c n", p=P)).then_inc(loaded, 16)
            sp.dma_start(k.w_o[:], w_o.rearrange("(c p) n -> p c n", p=P)).then_inc(loaded, 16)
            sp.dma_start(k.b_qkv_row[:], b_qkv.rearrange("(o n) -> o n", o=1).to_broadcast([P, 3 * F])).then_inc(loaded, 16)
            sp.dma_start(rest[:], b_o.rearrange("(o n) -> o n", o=1)).then_inc(loaded, 16)
            sp.wait_ge(split, 1)
            for i in range(3):
                sp.dma_start(k.bias_parts[i:i + 1, :], part[:, i, :]).then_inc(moved, 16)
            sp.wait_ge(moved, 48)

        @block.vector
        def _(dve):
            dve.wait_ge(loaded, 16 * (3 * L + 6))
            ch = Chain(dve, chain)
            for l in range(L):
                for i in range(2):
                    for c in range(2):
                        ch.link(dve.tensor_tensor(prod[:, c, :], k.w_gat[:, l, c, 0:F], a_rows[:, i, l, :], ALU.mult))
                        ch.link(dve.tensor_reduce(k.w_gat[:, l, c, F + i * HEADS:F + (i + 1) * HEADS],
                                                  prod[:, c, :].rearrange("p (h d) -> p h d", h=HEADS),
                                                  axis=AX.X, op=ALU.add))
            r = rest[:]
            for i in range(3):
                ch.link(dve.tensor_copy(part[:, i, :], r))
                if i < 2:
                    ch.link(dve.tensor_tensor(r, r, part[:, i, :], ALU.subtract))
            dve.sem_inc(split, 1)


def load_nodes(sp, x, to, i, loaded, last):
    a = TAIL_FULL
    if not last:
        v = x[bass.ds(i * (BATCH * P), BATCH * P), :].rearrange("(b p) f -> p b f", p=P)
        sp.dma_start(to[:, 0:a, :], v[:, 0:a, :]).then_inc(loaded, 16)
        sp.dma_start(to[:, a:BATCH, :], v[:, a:BATCH, :]).then_inc(loaded, 16)
    else:
        n0 = (NBATCH - 1) * BATCH * P
        sp.dma_start(to[:, 0:a, :], x[n0:n0 + a * P, :].rearrange("(b p) f -> p b f", p=P)).then_inc(loaded, 16)
        sp.dma_start(to[0:TAIL_REST, a, :], x[n0 + a * P:N, :]).then_inc(loaded, 16)


R = 2
BH = BATCH * HEADS
PAIR = SLOTS * P


class Batch:

    def __init__(self, turn, h, i=None, ring=R):
        self.turn, self.h, self.ring = turn, h, ring
        self.i = turn * ring + h if i is None else i
        self.s, self.q, self.round = h % ring, h % 2, turn + h // ring
        self.pairs = turn * (ring // 2) + h // 2

    def plus(self, d):
        return Batch(self.turn, self.h + d, self.i + d, self.ring)

    def n(self, b):
        return self.i * BATCH + b, (self.h * BATCH + b) % 2


def over_batches(eng, first, batch, turns, ring=R):
    first()
    with eng.Fori(0, turns - 1) as turn, eng.register() as number:
        for h in range(ring):
            eng.reg_mov(number, turn * ring + h)
            batch(Batch(turn, h, eng.snap(number, min_val=0, max_val=NBATCH - ring - 1), ring), ring)
    for h in range(ring):
        batch(Batch(turns - 1, h, ring=ring), ring - 1 - h)


def gat_layer(nc, k, graph, table_in, layer, table_out):
    with ExitStack() as ctx:
        s = Scope(nc, ctx, f"gat{layer}")
        rows = s.sb("rows", [P, R, BATCH, SLOTS, ROW])
        place = s.sb("place", [P, R, BATCH * SLOTS], I32)
        onehot = s.sb("onehot", [P, R, BATCH * SLOTS, P])
        onehot_t = s.sb("onehot_t", [P, 2, PAIR])
        er_edge = s.sb("er_edge", [P, 2, SLOTS, BH])
        logit = s.sb("logit", [P, 2, SLOTS, BH])
        key_bh = s.sb("key_bh", [P, 2, SLOTS, BH])
        key_t = s.sb("key_t", [BH, PAIR])
        wall = s.sb("wall", [BH, PAIR + 1])
        run_max = s.sb("run_max", [BH, PAIR])
        node_max = s.sb("node_max", [BH, PAIR])
        below_max = s.sb("below_max", [BH, 2, PAIR])
        total = s.sb("total", [P, 2, HEADS])
        mean = s.sb("mean", [P, 2, F])
        mean_t = s.sb("mean_t", [P, 2, 2, P])
        out_rows = s.sb("out_rows", [P, 2, BATCH, ROW])
        p_turn = s.ps("p_turn", [P, 512])
        p_er = s.ps("p_er", [P, 512])
        p_soft = s.ps("p_soft", [P, 512])
        p_sum = [s.ps(f"p_sum{i}", [P, 512]) for i in range(2)]
        p_mean = s.ps("p_mean", [P, 512])
        p_next = [s.ps(f"p_next{i}", [P, 512]) for i in range(2)]
        (placed, hot, hot_turned, hot_copied, er_made, er_taken, logits, soft_turned, below, soft_back, weights,
         messages, summed, averaged, mean_turned, mean_copied, product, row_done, chain_er, chain_soft,
         chain_mean, passed, passed_pe, shifted) = (s.sem(n) for n in (
             "placed", "hot", "hot_turned", "hot_copied", "er_made", "er_taken", "logits", "soft_turned", "below",
             "soft_back", "weights", "messages", "summed", "averaged", "mean_turned", "mean_copied", "product",
             "row_done", "chain_er", "chain_soft", "chain_mean", "passed", "passed_pe", "shifted"))
        gathered, before = k.pool_dma[0:R], k.pool_count[0:R]
        stored = [s.sem(f"stored{i}") for i in range(2)]
        walls_set = s.sem("walls_set")
        rows_clear = s.sem("rows_clear")
        AHEAD = R * BATCH
        block = ctx.enter_context(nc.Block())
        turns = NBATCH // R
        flat_local = graph.local[:].rearrange("p (b j) -> p b j", j=SLOTS)

        @block.gpsimd
        def _(pool):
            pool.wait_ge(rows_clear, 1)

            def gather(a):
                pool.wait_ge(placed, a.i + 1)
                for b in range(BATCH):
                    pool.wait_ge(averaged, a.n(b)[0] + 1)
                    pool.sem_inc(passed, 1)
                    for j in range(SLOTS):
                        c = b * SLOTS + j
                        pool.indirect_dma_start(rows[:, a.s, b, j, :], None, table_in,
                                                bass.IndirectOffsetOnAxis(place[:, a.s, c:c + 1], 0),
                                                bounds_check=N - 1, oob_is_err=False).then_inc(gathered[a.s], 16)

            with pool.Fori(0, turns) as turn:
                for h in range(R):
                    gather(Batch(turn, h))
            for h in range(R):
                k.pool_count[h] += turns * 16 * BATCH * SLOTS

        @block.sync
        def _(sp):
            with sp.Fori(0, turns) as turn:
                for h in range(R):
                    a = Batch(turn, h)
                    sp.wait_ge(row_done, (a.i + 1) * BATCH + 1)
                    sp.dma_start(table_out[bass.ds(a.i * (BATCH * P), BATCH * P), :].rearrange("(b p) f -> p b f", p=P),
                                 out_rows[:, a.q]).then_inc(stored[a.q], 16)
            for q in range(2):
                sp.wait_ge(stored[q], 16 * (NBATCH // 2))

        @block.vector
        def _(dve):
            def make_place(a):
                dve.wait_ge(gathered[a.s], a.round * (16 * BATCH * SLOTS) + before[a.s])
                dve.tensor_copy(place[:, a.s, :], graph.index[:, bass.ds(a.i * (BATCH * SLOTS), BATCH * SLOTS)]
                                ).then_inc(placed, 1)

            def make_onehot(a, b):
                for j in range(SLOTS):
                    last = dve.tensor_scalar(onehot[:, a.s, b * SLOTS + j, :], k.iota_f[:, 0:P],
                                             graph.local[:, bass.ds((a.i * BATCH + b) * SLOTS + j, 1)],
                                             None, ALU.is_equal)
                last.then_inc(hot, 1)

            def take_er(a):
                ch = Chain(dve, chain_er, per=1, turn=a.i)
                dve.wait_ge(er_made, (a.i + 1) * BATCH + 1)
                ch.link(dve.tensor_copy(er_edge[:, a.q].rearrange("p j c -> p (j c)"), p_er[:, 0:SLOTS * BH]))
                dve.sem_inc(er_taken, 1)
                ch.close()

            def make_logits(a, ch):
                for j in range(SLOTS):
                    last = dve.tensor_copy(
                        key_bh[:, a.q, j, :].rearrange("p (b h) -> p b h", h=HEADS),
                        flat_local[:, bass.ds(a.i * BATCH, BATCH), j:j + 1].to_broadcast([P, BATCH, HEADS]))
                dve.wait_ge(gathered[a.s], (a.round + 1) * (16 * BATCH * SLOTS) + before[a.s])
                for j in range(SLOTS):
                    last = dve.tensor_tensor(logit[:, a.q, j, :].rearrange("p (b h) -> p b h", h=HEADS),
                                             rows[:, a.s, :, j, F:ROW],
                                             er_edge[:, a.q, j, :].rearrange("p (b h) -> p b h", h=HEADS), ALU.add)
                ch.link(last)
                dve.scalar_tensor_tensor(out=logit[:, a.q], in0=logit[:, a.q], scalar=SLOPE_ATTN, in1=logit[:, a.q],
                                         op0=ALU.mult, op1=ALU.max).then_inc(logits, 1)

            def subtract_max(a, ch):
                dve.wait_ge(soft_turned, a.i + 1)
                ch.link(dve.tensor_copy(key_t[:], p_soft[0:BH, PAIR:2 * PAIR]))
                ch.link(dve.tensor_tensor(wall[:, 1:PAIR], key_t[:, 1:PAIR], key_t[:, 0:PAIR - 1], ALU.is_equal))
                ch.link(dve.tensor_scalar(wall[:, 1:PAIR], wall[:, 1:PAIR], 1.0, FAR, ALU.subtract, ALU.mult))
                ch.link(dve.tensor_tensor_scan(run_max[:], wall[:, 0:PAIR], p_soft[0:BH, 0:PAIR], 0.0,
                                               ALU.add, ALU.max))
                ch.link(dve.tensor_tensor_scan(node_max[:, ::-1], wall[:, PAIR:0:-1], run_max[:, ::-1], 0.0,
                                               ALU.add, ALU.max))
                dve.tensor_tensor(below_max[:, a.q], p_soft[0:BH, 0:PAIR], node_max[:], ALU.subtract).then_inc(below, 1)

            def weigh(a, b):
                if b == 0:
                    dve.wait_ge(weights, a.i + 1)
                v = rows[:, a.s, b, :, 0:F].rearrange("p j (h d) -> p j h d", h=HEADS)
                w = rows[:, a.s, b, :, F:ROW]
                for j in range(SLOTS):
                    last = dve.tensor_tensor(v[:, j], v[:, j], w[:, j].unsqueeze(2).to_broadcast([P, HEADS, HD]),
                                             ALU.mult)
                last.then_inc(messages, 1)

            def average(a, b):
                n, q = a.n(b)
                ch = Chain(dve, chain_mean, per=2, turn=n)
                dve.wait_ge(summed, n + 1)
                ch.link(dve.tensor_scalar(total[:, q], p_sum[q][:, F:ROW], TINY, None, ALU.max))
                ch.link(dve.reciprocal(total[:, q], total[:, q]))
                dve.wait_ge(mean_turned, n)
                dve.tensor_tensor(mean[:, q].rearrange("p (h d) -> p h d", h=HEADS),
                                  p_sum[q][:, 0:F].rearrange("p (h d) -> p h d", h=HEADS),
                                  total[:, q].unsqueeze(2).to_broadcast([P, HEADS, HD]), ALU.mult).then_inc(averaged, 1)

            def leak(a, b):
                n, q = a.n(b)
                dve.wait_ge(shifted, n + 1)
                v = mean_t[:, q].rearrange("p c n -> p (c n)")
                dve.scalar_tensor_tensor(out=v, in0=v, scalar=SLOPE_ACT, in1=v,
                                         op0=ALU.mult, op1=ALU.max).then_inc(mean_copied, 1)

            SOFT = 6

            def first():
                dve.memset(rows[:], 0.0).then_inc(rows_clear, 1)
                dve.wait_ge(rows_clear, 1)
                dve.memset(wall[:, 0:1], -FAR).then_inc(walls_set, 1)
                dve.memset(wall[:, PAIR:PAIR + 1], -FAR).then_inc(walls_set, 1)
                dve.wait_ge(walls_set, 2)
                dve.sem_inc(averaged, AHEAD)
                for h in range(R):
                    make_place(Batch(0, h))
                for h in range(2):
                    for b in range(BATCH):
                        make_onehot(Batch(0, h), b)
                    take_er(Batch(0, h))
                a = Batch(0, 0)
                ch = Chain(dve, chain_soft, per=SOFT, turn=0)
                make_logits(a, ch)
                subtract_max(a, ch)
                ch.close()

            def batch(a, after):
                for st in range(9):
                    if st == 0 and after >= 2:
                        make_place(a.plus(2))
                    if st < BATCH:
                        weigh(a, st)
                    if st == 1 and after >= 1:
                        ch = Chain(dve, chain_soft, per=SOFT, turn=a.plus(1).i)
                        make_logits(a.plus(1), ch)
                    if st == 3 and after >= 1:
                        subtract_max(a.plus(1), ch)
                        ch.close()
                    if 1 <= st <= BATCH:
                        average(a, st - 1)
                        if after >= 2:
                            make_onehot(a.plus(2), st - 1)
                    if 2 <= st:
                        leak(a, st - 2)
                    if st == 8 and after >= 2:
                        take_er(a.plus(2))

            over_batches(dve, first, batch, turns)

        @block.tensor
        def _(pe):
            def turn_onehot(a, b):
                n, q = a.n(b)
                pe.wait_ge(hot, n + 1)
                pe.wait_ge(hot_copied, n)
                for j in range(SLOTS):
                    last = nc.tensor.transpose(p_turn[:, j * P:(j + 1) * P], onehot[:, a.s, b * SLOTS + j, :], k.ident[:])
                last.then_inc(hot_turned, 1)

            def make_er(a, b):
                n, q = a.n(b)
                pe.wait_ge(hot_copied, n + 1)
                if b == 0:
                    pe.wait_ge(er_taken, a.i)
                for j in range(SLOTS):
                    c = j * BH + b * HEADS
                    last = nc.tensor.matmul(p_er[:, c:c + HEADS], onehot_t[:, q, j * P:(j + 1) * P],
                                            k.er[:, bass.ds(n * HEADS, HEADS)], start=True, stop=True)
                last.then_inc(er_made, 1)

            def turn_soft(a):
                pe.wait_ge(logits, a.i + 1)
                pe.wait_ge(weights, a.i)
                pe.sem_inc(passed_pe, 1)
                for x, c in ((logit, 0), (key_bh, PAIR)):
                    for j in range(SLOTS):
                        last = nc.tensor.transpose(p_soft[0:BH, c + j * P:c + (j + 1) * P], x[:, a.q, j, :], k.ident[:])
                last.then_inc(soft_turned, 1)

            def turn_back(a):
                pe.wait_ge(below, a.i + 1)
                pe.sem_inc(passed_pe, 1)
                for j in range(SLOTS):
                    last = nc.tensor.transpose(p_soft[:, j * BH:(j + 1) * BH], below_max[:, a.q, j * P:(j + 1) * P],
                                               k.ident[0:BH, 0:BH])
                last.then_inc(soft_back, 1)

            def add_up(a, b):
                n, q = a.n(b)
                pe.wait_ge(messages, n + 1)
                pe.wait_ge(averaged, n + (AHEAD - 1))
                for j in range(SLOTS):
                    last = nc.tensor.matmul(p_sum[q][:, 0:ROW], onehot[:, a.s, b * SLOTS + j, :], rows[:, a.s, b, j, :],
                                            start=(j == 0), stop=(j == SLOTS - 1))
                last.then_inc(summed, 1)

            def turn_mean(a, b):
                n, q = a.n(b)
                pe.wait_ge(averaged, n + (AHEAD + 1))
                pe.wait_ge(mean_copied, n)
                for c in range(2):
                    last = nc.tensor.transpose(p_mean[:, c * P:(c + 1) * P], mean[:, q, c * P:(c + 1) * P], k.ident[:])
                last.then_inc(mean_turned, 1)

            def multiply(a, b):
                n, q = a.n(b)
                pe.wait_ge(mean_copied, n + 1)
                pe.wait_ge(row_done, n)
                for c in range(2):
                    last = nc.tensor.matmul(p_next[q][:, 0:WCOLS], mean_t[:, q, c, :], k.w_gat[:, layer + 1, c, :],
                                            start=(c == 0), stop=(c == 1))
                last.then_inc(product, 1)

            def first():
                for x in (mean_turned, product, er_made):
                    pe.sem_inc(x, 1)
                for h in range(2):
                    for b in range(BATCH + 1):
                        if b:
                            make_er(Batch(0, h), b - 1)
                        if b < BATCH:
                            turn_onehot(Batch(0, h), b)
                turn_soft(Batch(0, 0))
                turn_back(Batch(0, 0))

            def batch(a, after):
                for st in range(9):
                    if st < BATCH:
                        add_up(a, st)
                    if 2 <= st and after >= 2:
                        make_er(a.plus(2), st - 2)
                    if 1 <= st <= BATCH and after >= 2:
                        turn_onehot(a.plus(2), st - 1)
                    if st == 2 and after >= 1:
                        turn_soft(a.plus(1))
                    if st == 6 and after >= 1:
                        turn_back(a.plus(1))
                    if 1 <= st <= BATCH:
                        turn_mean(a, st - 1)
                    if 2 <= st:
                        multiply(a, st - 2)

            over_batches(pe, first, batch, turns)

        @block.scalar
        def _(act):
            def copy_onehot(a, b):
                n, q = a.n(b)
                act.wait_ge(hot_turned, n + 1)
                act.wait_ge(er_made, n)
                nc.scalar.copy(onehot_t[:, q, :], p_turn[:, 0:PAIR]).then_inc(hot_copied, 1)

            def exponentiate(a):
                act.wait_ge(soft_back, a.i + 1)
                for j in range(SLOTS):
                    last = nc.scalar.activation(
                        rows[:, a.s, :, j, F:ROW],
                        p_soft[:, j * BH:(j + 1) * BH].rearrange("p (b h) -> p b h", h=HEADS), ACT.Exp)
                last.then_inc(weights, 1)

            def activate(a, b):
                n, q = a.n(b)
                act.wait_ge(mean_turned, n + 2)
                act.wait_ge(product, n)
                for c in range(2):
                    last = nc.scalar.activation(mean_t[:, q, c, :], p_mean[:, c * P:(c + 1) * P], ACT.Identity,
                                                bias=k.b_col[:, layer, c:c + 1])
                last.then_inc(shifted, 1)

            def finish(a, b):
                n, q = a.n(b)
                act.wait_ge(product, n + 2)
                if b == 0:
                    act.wait_ge(stored[a.q], a.pairs * 16)
                nc.scalar.copy(out_rows[:, a.q, b, :], p_next[q][:, 0:ROW])
                nc.scalar.copy(k.er[:, bass.ds(n * HEADS, HEADS)], p_next[q][:, ROW:WCOLS]).then_inc(row_done, 1)

            def first():
                act.sem_inc(row_done, 1)
                for h in range(2):
                    for b in range(BATCH):
                        copy_onehot(Batch(0, h), b)
                exponentiate(Batch(0, 0))

            def batch(a, after):
                for st in range(9):
                    if 1 <= st <= BATCH and after >= 2:
                        copy_onehot(a.plus(2), st - 1)
                    if 1 <= st <= BATCH:
                        activate(a, st - 1)
                    if st == 7 and after >= 1:
                        exponentiate(a.plus(1))
                    if 2 <= st:
                        finish(a, st - 2)

            over_batches(act, first, batch, turns)


def last_gat_layer(nc, k, graph, table_in, x, x_out):
    with ExitStack() as ctx:
        s = Scope(nc, ctx, "gat2")
        rows = s.sb("rows", [P, R, BATCH, SLOTS, ROW])
        place = s.sb("place", [P, R, BATCH * SLOTS], I32)
        onehot = s.sb("onehot", [P, R, BATCH * SLOTS, P])
        onehot_t = s.sb("onehot_t", [P, 2, PAIR])
        er_edge = s.sb("er_edge", [P, 2, SLOTS, BH])
        logit = s.sb("logit", [P, 2, SLOTS, BH])
        key_bh = s.sb("key_bh", [P, 2, SLOTS, BH])
        key_t = s.sb("key_t", [BH, PAIR])
        wall = s.sb("wall", [BH, PAIR + 1])
        run_max = s.sb("run_max", [BH, PAIR])
        node_max = s.sb("node_max", [BH, PAIR])
        below_max = s.sb("below_max", [BH, 2, PAIR])
        total = s.sb("total", [P, 2, HEADS])
        mean = s.sb("mean", [P, 2, F])
        x_rows = s.sb("x_rows", [P, 2, BATCH, F])
        p_turn = s.ps("p_turn", [P, 512])
        p_er = s.ps("p_er", [P, 512])
        p_soft = s.ps("p_soft", [P, 512])
        p_sum = [s.ps(f"p_sum{i}", [P, 512]) for i in range(2)]
        (placed, hot, hot_turned, hot_copied, er_made, er_taken, logits, soft_turned, below, soft_back, weights,
         messages, summed, averaged, row_done, chain_er, chain_soft,
         chain_mean, passed, passed_pe) = (s.sem(n) for n in (
             "placed", "hot", "hot_turned", "hot_copied", "er_made", "er_taken", "logits", "soft_turned", "below",
             "soft_back", "weights", "messages", "summed", "averaged", "row_done",
             "chain_er", "chain_soft", "chain_mean", "passed", "passed_pe"))
        gathered, before = k.pool_dma[0:R], k.pool_count[0:R]
        loaded = [s.sem(f"loaded{i}") for i in range(2)]
        stored = [s.sem(f"stored{i}") for i in range(2)]
        walls_set = s.sem("walls_set")
        rows_clear = s.sem("rows_clear")
        AHEAD = R * BATCH
        block = ctx.enter_context(nc.Block())
        turns = NBATCH // R
        flat_local = graph.local[:].rearrange("p (b j) -> p b j", j=SLOTS)

        @block.gpsimd
        def _(pool):
            pool.wait_ge(rows_clear, 1)

            def gather(a):
                pool.wait_ge(placed, a.i + 1)
                for b in range(BATCH):
                    pool.wait_ge(averaged, a.n(b)[0] + 1)
                    pool.sem_inc(passed, 1)
                    for j in range(SLOTS):
                        c = b * SLOTS + j
                        pool.indirect_dma_start(rows[:, a.s, b, j, :], None, table_in,
                                                bass.IndirectOffsetOnAxis(place[:, a.s, c:c + 1], 0),
                                                bounds_check=N - 1, oob_is_err=False).then_inc(gathered[a.s], 16)

            with pool.Fori(0, turns) as turn:
                for h in range(R):
                    gather(Batch(turn, h))
            for h in range(R):
                k.pool_count[h] += turns * 16 * BATCH * SLOTS

        @block.sync
        def _(sp):
            sp.wait_ge(rows_clear, 1)

            def load(a, last):
                sp.wait_ge(stored[a.q], a.pairs * 16)
                load_nodes(sp, x, x_rows[:, a.q], a.i, loaded[a.q], last)

            def store(a):
                sp.wait_ge(row_done, (a.i + 1) * BATCH)
                sp.dma_start(x_out[bass.ds(a.i * (BATCH * P), BATCH * P), :].rearrange("(b p) f -> p b f", p=P),
                             x_rows[:, a.q]).then_inc(stored[a.q], 16)

            load(Batch(0, 0), False)
            with sp.Fori(0, turns - 1) as turn:
                for h in range(R):
                    load(Batch(turn, h + 1), False)
                    store(Batch(turn, h))
            load(Batch(turns - 1, 1), True)
            for h in range(R):
                store(Batch(turns - 1, h))
            for q in range(2):
                sp.wait_ge(stored[q], 16 * (NBATCH // 2))

        @block.vector
        def _(dve):
            def make_place(a):
                dve.wait_ge(gathered[a.s], a.round * (16 * BATCH * SLOTS) + before[a.s])
                dve.tensor_copy(place[:, a.s, :], graph.index[:, bass.ds(a.i * (BATCH * SLOTS), BATCH * SLOTS)]
                                ).then_inc(placed, 1)

            def make_onehot(a, b):
                for j in range(SLOTS):
                    last = dve.tensor_scalar(onehot[:, a.s, b * SLOTS + j, :], k.iota_f[:, 0:P],
                                             graph.local[:, bass.ds((a.i * BATCH + b) * SLOTS + j, 1)],
                                             None, ALU.is_equal)
                last.then_inc(hot, 1)

            def take_er(a):
                ch = Chain(dve, chain_er, per=1, turn=a.i)
                dve.wait_ge(er_made, (a.i + 1) * BATCH + 1)
                ch.link(dve.tensor_copy(er_edge[:, a.q].rearrange("p j c -> p (j c)"), p_er[:, 0:SLOTS * BH]))
                dve.sem_inc(er_taken, 1)
                ch.close()

            def make_logits(a, ch):
                for j in range(SLOTS):
                    last = dve.tensor_copy(
                        key_bh[:, a.q, j, :].rearrange("p (b h) -> p b h", h=HEADS),
                        flat_local[:, bass.ds(a.i * BATCH, BATCH), j:j + 1].to_broadcast([P, BATCH, HEADS]))
                dve.wait_ge(gathered[a.s], (a.round + 1) * (16 * BATCH * SLOTS) + before[a.s])
                for j in range(SLOTS):
                    last = dve.tensor_tensor(logit[:, a.q, j, :].rearrange("p (b h) -> p b h", h=HEADS),
                                             rows[:, a.s, :, j, F:ROW],
                                             er_edge[:, a.q, j, :].rearrange("p (b h) -> p b h", h=HEADS), ALU.add)
                ch.link(last)
                dve.scalar_tensor_tensor(out=logit[:, a.q], in0=logit[:, a.q], scalar=SLOPE_ATTN, in1=logit[:, a.q],
                                         op0=ALU.mult, op1=ALU.max).then_inc(logits, 1)

            def subtract_max(a, ch):
                dve.wait_ge(soft_turned, a.i + 1)
                ch.link(dve.tensor_copy(key_t[:], p_soft[0:BH, PAIR:2 * PAIR]))
                ch.link(dve.tensor_tensor(wall[:, 1:PAIR], key_t[:, 1:PAIR], key_t[:, 0:PAIR - 1], ALU.is_equal))
                ch.link(dve.tensor_scalar(wall[:, 1:PAIR], wall[:, 1:PAIR], 1.0, FAR, ALU.subtract, ALU.mult))
                ch.link(dve.tensor_tensor_scan(run_max[:], wall[:, 0:PAIR], p_soft[0:BH, 0:PAIR], 0.0,
                                               ALU.add, ALU.max))
                ch.link(dve.tensor_tensor_scan(node_max[:, ::-1], wall[:, PAIR:0:-1], run_max[:, ::-1], 0.0,
                                               ALU.add, ALU.max))
                dve.tensor_tensor(below_max[:, a.q], p_soft[0:BH, 0:PAIR], node_max[:], ALU.subtract).then_inc(below, 1)

            def weigh(a, b):
                if b == 0:
                    dve.wait_ge(weights, a.i + 1)
                v = rows[:, a.s, b, :, 0:F].rearrange("p j (h d) -> p j h d", h=HEADS)
                w = rows[:, a.s, b, :, F:ROW]
                for j in range(SLOTS):
                    last = dve.tensor_tensor(v[:, j], v[:, j], w[:, j].unsqueeze(2).to_broadcast([P, HEADS, HD]),
                                             ALU.mult)
                last.then_inc(messages, 1)

            def average(a, b):
                n, q = a.n(b)
                ch = Chain(dve, chain_mean, per=3, turn=n)
                dve.wait_ge(summed, n + 1)
                ch.link(dve.tensor_scalar(total[:, q], p_sum[q][:, F:ROW], TINY, None, ALU.max))
                ch.link(dve.reciprocal(total[:, q], total[:, q]))
                ins = dve.tensor_tensor(mean[:, q].rearrange("p (h d) -> p h d", h=HEADS),
                                        p_sum[q][:, 0:F].rearrange("p (h d) -> p h d", h=HEADS),
                                        total[:, q].unsqueeze(2).to_broadcast([P, HEADS, HD]), ALU.mult)
                ins.then_inc(averaged, 1)
                dve.wait_ge(averaged, n + (AHEAD + 1))
                if b == 0:
                    dve.wait_ge(loaded[a.q], (a.pairs + 1) * 32)
                ch.link(dve.tensor_tensor(mean[:, q], mean[:, q], k.b2_row[:], ALU.add))
                dve.tensor_tensor(x_rows[:, a.q, b, :], mean[:, q], x_rows[:, a.q, b, :], ALU.add).then_inc(row_done, 1)

            SOFT = 6

            def first():
                dve.memset(x_rows[:], 0.0)
                dve.memset(rows[:], 0.0).then_inc(rows_clear, 1)
                dve.wait_ge(rows_clear, 1)
                dve.memset(wall[:, 0:1], -FAR).then_inc(walls_set, 1)
                dve.memset(wall[:, PAIR:PAIR + 1], -FAR).then_inc(walls_set, 1)
                dve.wait_ge(walls_set, 2)
                dve.sem_inc(averaged, AHEAD)
                for h in range(R):
                    make_place(Batch(0, h))
                for h in range(2):
                    for b in range(BATCH):
                        make_onehot(Batch(0, h), b)
                    take_er(Batch(0, h))
                a = Batch(0, 0)
                ch = Chain(dve, chain_soft, per=SOFT, turn=0)
                make_logits(a, ch)
                subtract_max(a, ch)
                ch.close()

            def batch(a, after):
                for st in range(9):
                    if st == 0 and after >= 2:
                        make_place(a.plus(2))
                    if st < BATCH:
                        weigh(a, st)
                    if st == 1 and after >= 1:
                        ch = Chain(dve, chain_soft, per=SOFT, turn=a.plus(1).i)
                        make_logits(a.plus(1), ch)
                    if st == 3 and after >= 1:
                        subtract_max(a.plus(1), ch)
                        ch.close()
                    if 1 <= st <= BATCH:
                        average(a, st - 1)
                        if after >= 2:
                            make_onehot(a.plus(2), st - 1)
                    if st == 8 and after >= 2:
                        take_er(a.plus(2))

            over_batches(dve, first, batch, turns)

        @block.tensor
        def _(pe):
            def turn_onehot(a, b):
                n, q = a.n(b)
                pe.wait_ge(hot, n + 1)
                pe.wait_ge(hot_copied, n)
                for j in range(SLOTS):
                    last = nc.tensor.transpose(p_turn[:, j * P:(j + 1) * P], onehot[:, a.s, b * SLOTS + j, :], k.ident[:])
                last.then_inc(hot_turned, 1)

            def make_er(a, b):
                n, q = a.n(b)
                pe.wait_ge(hot_copied, n + 1)
                if b == 0:
                    pe.wait_ge(er_taken, a.i)
                for j in range(SLOTS):
                    c = j * BH + b * HEADS
                    last = nc.tensor.matmul(p_er[:, c:c + HEADS], onehot_t[:, q, j * P:(j + 1) * P],
                                            k.er[:, bass.ds(n * HEADS, HEADS)], start=True, stop=True)
                last.then_inc(er_made, 1)

            def turn_soft(a):
                pe.wait_ge(logits, a.i + 1)
                pe.wait_ge(weights, a.i)
                pe.sem_inc(passed_pe, 1)
                for x, c in ((logit, 0), (key_bh, PAIR)):
                    for j in range(SLOTS):
                        last = nc.tensor.transpose(p_soft[0:BH, c + j * P:c + (j + 1) * P], x[:, a.q, j, :], k.ident[:])
                last.then_inc(soft_turned, 1)

            def turn_back(a):
                pe.wait_ge(below, a.i + 1)
                pe.sem_inc(passed_pe, 1)
                for j in range(SLOTS):
                    last = nc.tensor.transpose(p_soft[:, j * BH:(j + 1) * BH], below_max[:, a.q, j * P:(j + 1) * P],
                                               k.ident[0:BH, 0:BH])
                last.then_inc(soft_back, 1)

            def add_up(a, b):
                n, q = a.n(b)
                pe.wait_ge(messages, n + 1)
                pe.wait_ge(averaged, n + (AHEAD - 1))
                for j in range(SLOTS):
                    last = nc.tensor.matmul(p_sum[q][:, 0:ROW], onehot[:, a.s, b * SLOTS + j, :], rows[:, a.s, b, j, :],
                                            start=(j == 0), stop=(j == SLOTS - 1))
                last.then_inc(summed, 1)

            def first():
                pe.sem_inc(er_made, 1)
                for h in range(2):
                    for b in range(BATCH + 1):
                        if b:
                            make_er(Batch(0, h), b - 1)
                        if b < BATCH:
                            turn_onehot(Batch(0, h), b)
                turn_soft(Batch(0, 0))
                turn_back(Batch(0, 0))

            def batch(a, after):
                for st in range(9):
                    if st < BATCH:
                        add_up(a, st)
                    if 2 <= st and after >= 2:
                        make_er(a.plus(2), st - 2)
                    if 1 <= st <= BATCH and after >= 2:
                        turn_onehot(a.plus(2), st - 1)
                    if st == 2 and after >= 1:
                        turn_soft(a.plus(1))
                    if st == 6 and after >= 1:
                        turn_back(a.plus(1))

            over_batches(pe, first, batch, turns)

        @block.scalar
        def _(act):
            def copy_onehot(a, b):
                n, q = a.n(b)
                act.wait_ge(hot_turned, n + 1)
                act.wait_ge(er_made, n)
                nc.scalar.copy(onehot_t[:, q, :], p_turn[:, 0:PAIR]).then_inc(hot_copied, 1)

            def exponentiate(a):
                act.wait_ge(soft_back, a.i + 1)
                for j in range(SLOTS):
                    last = nc.scalar.activation(
                        rows[:, a.s, :, j, F:ROW],
                        p_soft[:, j * BH:(j + 1) * BH].rearrange("p (b h) -> p b h", h=HEADS), ACT.Exp)
                last.then_inc(weights, 1)

            def first():
                for h in range(2):
                    for b in range(BATCH):
                        copy_onehot(Batch(0, h), b)
                exponentiate(Batch(0, 0))

            def batch(a, after):
                for st in range(9):
                    if 1 <= st <= BATCH and after >= 2:
                        copy_onehot(a.plus(2), st - 1)
                    if st == 7 and after >= 1:
                        exponentiate(a.plus(1))

            over_batches(act, first, batch, turns)


RP = 4


def project(nc, k, tag, x, parts, er=None):
    padded = x.shape[0] == NP
    two = len(parts) > 1
    products = 2 if two else RP
    with ExitStack() as ctx:
        s = Scope(nc, ctx, tag)
        xin = s.sb("xin", [P, RP, BATCH, F])
        stats = s.sb("stats", [P, RP, BATCH, 6])
        mv = s.sb("mv", [P, RP, BATCH, 2])
        rstd = s.sb("rstd", [P, RP, BATCH])
        shift = s.sb("shift", [P, RP, BATCH])
        hidden = s.sb("hidden", [P, RP, F])
        hidden_t = s.sb("hidden_t", [P, RP, 2, P])
        rows = [s.sb(f"rows{m}", [P, 2, BATCH, part[1]]) for m, part in enumerate(parts)]
        turned = [s.ps(f"turned{i}", [P, 512]) for i in range(RP)]
        product = [[s.ps(f"product{m}{i}", [P, 512]) for i in range(products)] for m in range(len(parts))]
        (zeroed, passed, chain, chain_scale, variances, roots, scaled, hid, hid_turned, copied, multiplied, taken) = (
            s.sem(n) for n in (
                "zeroed", "passed", "chain", "chain_scale", "variances", "roots", "scaled", "hidden_ready",
                "hidden_turned", "copied", "multiplied", "taken"))
        loaded = [s.sem(f"loaded{i}") for i in range(RP)]
        stored = [s.sem(f"stored{i}") for i in range(2)]
        block = ctx.enter_context(nc.Block())
        turns = NBATCH // RP
        HID0, RING0, TAKEN0 = (RP - 1) * BATCH, RP - 1, products - 1

        def batch_of(turn, h):
            return Batch(turn, h, ring=RP)

        def ahead(one, a, b, d, after):
            if b + d < BATCH:
                one(a, b + d)
            elif after >= 1:
                one(a.plus(1), b + d - BATCH)

        def block_of(a, b):
            m = a.h * BATCH + b
            return a.i * BATCH + b, m % RP, m % products

        @block.sync
        def _(sp):
            sp.wait_ge(zeroed, 1)

            def load(a, last=False):
                sp.wait_ge(hid, a.i * BATCH)
                load_nodes(sp, x, xin[:, a.s], a.i, loaded[a.s], last and not padded)

            def store(a):
                sp.wait_ge(taken, (a.i + 1) * BATCH + TAKEN0)
                for m, part in enumerate(parts):
                    sp.dma_start(part[0][bass.ds(a.i * (BATCH * P), BATCH * P), :].rearrange("(b p) f -> p b f", p=P),
                                 rows[m][:, a.q]).then_inc(stored[a.q], 16)

            for h in range(RP):
                load(batch_of(0, h))
            with sp.Fori(0, turns - 2) as turn:
                for h in range(RP):
                    load(batch_of(turn, h + RP))
                    store(batch_of(turn, h))
            for h in range(2 * RP):
                a = batch_of(turns - 2, h)
                if h < RP:
                    load(a.plus(RP), h == RP - 1)
                store(a)
            for q in range(2):
                sp.wait_ge(stored[q], 16 * (NBATCH // 2) * len(parts))

        def copy(eng, a, b):
            n, r, _ = block_of(a, b)
            eng.wait_ge(hid_turned, n + (1 + RING0))
            eng.wait_ge(multiplied, n)
            to = hidden_t[:, r].rearrange("p c n -> p (c n)")
            if two:
                nc.scalar.copy(to, turned[r][:, 0:F]).then_inc(copied, 1)
            else:
                eng.tensor_copy(to, turned[r][:, 0:F]).then_inc(copied, 1)

        @block.vector
        def _(dve):
            def statistics(a, b):
                if b == 0:
                    dve.wait_ge(loaded[a.s], (a.round + 1) * 32)
                last = dve.bn_stats(stats[:, a.s, b, :], xin[:, a.s, b, :])
                if b == BATCH - 1:
                    ch = Chain(dve, chain, per=2, turn=a.i)
                    ch.link(last)
                    dve.sem_inc(passed, 1)
                    for i in range(BATCH):
                        last = dve.bn_aggr(mv[:, a.s, i, :], stats[:, a.s, i, :])
                    ch.link(last)
                    dve.tensor_scalar(rstd[:, a.s], mv[:, a.s, :, 1], EPS, None, ALU.add).then_inc(variances, 1)
                    ch.close()

            def scale(a):
                ch = Chain(dve, chain_scale, per=1, turn=a.i)
                dve.wait_ge(roots, a.i + 1)
                ch.link(dve.reciprocal(rstd[:, a.s], rstd[:, a.s]))
                dve.scalar_tensor_tensor(out=shift[:, a.s], in0=mv[:, a.s, :, 0], scalar=-1.0, in1=rstd[:, a.s],
                                         op0=ALU.mult, op1=ALU.mult).then_inc(scaled, 1)
                ch.close()

            def take(a, b):
                n, _, r = block_of(a, b)
                dve.wait_ge(multiplied, n + (1 + RING0))
                if b == 0:
                    dve.wait_ge(stored[a.q], a.pairs * (16 * len(parts)))
                for m, (_, cols, _, _, bias) in enumerate(parts):
                    last = dve.tensor_tensor(rows[m][:, a.q, b, :], product[m][r][:, 0:cols], bias, ALU.add)
                last.then_inc(taken, 1)

            def first():
                dve.memset(xin[:], 0.0).then_inc(zeroed, 1)
                for h in range(2):
                    for b in range(BATCH):
                        statistics(batch_of(0, h), b)
                scale(batch_of(0, 0))
                if two:
                    dve.sem_inc(taken, TAKEN0)
                else:
                    dve.sem_inc(copied, RING0)
                    copy(dve, batch_of(0, 0), 0)

            def batch(a, after):
                for b in range(BATCH):
                    if not two:
                        ahead(lambda a, b: copy(dve, a, b), a, b, 1, after)
                    if b == 1 and after >= 1:
                        scale(a.plus(1))
                    if two:
                        take(a, b)
                    if after >= 2:
                        statistics(a.plus(2), b)

            over_batches(dve, first, batch, turns, RP)

        @block.scalar
        def _(act):
            def root(a):
                act.wait_ge(variances, a.i + 1)
                nc.scalar.activation(rstd[:, a.s], rstd[:, a.s], ACT.Sqrt).then_inc(roots, 1)

            def relu(a, b):
                n, r, _ = block_of(a, b)
                if b == 0:
                    act.wait_ge(scaled, a.i + 1)
                act.wait_ge(hid_turned, n)
                nc.scalar.activation(hidden[:, r, :], xin[:, a.s, b, :], ACT.Relu,
                                     bias=shift[:, a.s, b:b + 1], scale=rstd[:, a.s, b:b + 1]).then_inc(hid, 1)

            def take(a, b):
                n, _, r = block_of(a, b)
                act.wait_ge(multiplied, n + (1 + RING0))
                if b == 0:
                    act.wait_ge(stored[a.q], a.pairs * (16 * len(parts)))
                last = nc.scalar.copy(rows[0][:, a.q, b, :], product[0][r][:, 0:parts[0][1]])
                if er is not None:
                    last = nc.scalar.copy(er[:, bass.ds(n * HEADS, HEADS)], product[0][r][:, ROW:WCOLS])
                last.then_inc(taken, 1)

            def first():
                act.sem_inc(hid, HID0)
                for h in range(2):
                    root(batch_of(0, h))
                for b in range(3):
                    relu(batch_of(0, 0), b)
                if two:
                    act.sem_inc(copied, RING0)
                    copy(act, batch_of(0, 0), 0)
                else:
                    act.sem_inc(taken, TAKEN0)

            def batch(a, after):
                for b in range(BATCH):
                    ahead(relu, a, b, 3, after)
                    if two:
                        ahead(lambda a, b: copy(act, a, b), a, b, 1, after)
                    else:
                        take(a, b)
                if after >= 2:
                    root(a.plus(2))

            over_batches(act, first, batch, turns, RP)

        @block.tensor
        def _(pe):
            def turn_hidden(a, b):
                n, r, _ = block_of(a, b)
                pe.wait_ge(hid, n + (1 + HID0))
                pe.wait_ge(copied, n)
                for c in range(2):
                    last = nc.tensor.transpose(turned[r][:, c * P:(c + 1) * P], hidden[:, r, c * P:(c + 1) * P], k.ident[:])
                last.then_inc(hid_turned, 1)

            def multiply(a, b):
                n, r, out = block_of(a, b)
                pe.wait_ge(copied, n + (1 + RING0))
                pe.wait_ge(taken, n)
                for m, (_, _, w, cols, _) in enumerate(parts):
                    for c in range(2):
                        last = nc.tensor.matmul(product[m][out][:, 0:cols], hidden_t[:, r, c, :], w[:, c, :],
                                                start=(c == 0), stop=(c == 1))
                last.then_inc(multiplied, 1)

            def first():
                pe.sem_inc(hid_turned, RING0)
                pe.sem_inc(multiplied, RING0)
                for b in range(2):
                    turn_hidden(batch_of(0, 0), b)

            def batch(a, after):
                for b in range(BATCH):
                    ahead(turn_hidden, a, b, 2, after)
                    multiply(a, b)

            over_batches(pe, first, batch, turns, RP)


SCALE = HD ** -0.5


def dot_layer(nc, k, graph, q_table, kv_table, x_in, x_out):
    KV = 2 * F
    with ExitStack() as ctx:
        s = Scope(nc, ctx, "dot")
        rows = s.sb("rows", [P, R, BATCH, SLOTS, KV])
        q_rows = s.sb("q_rows", [P, 2, BATCH, F])
        x_rows = s.sb("x_rows", [P, 2, BATCH, F])
        place = s.sb("place", [P, R, BATCH * SLOTS], I32)
        onehot = s.sb("onehot", [P, R, BATCH * SLOTS, P])
        onehot_t = s.sb("onehot_t", [P, 2, PAIR])
        logit = s.sb("logit", [P, 2, SLOTS, BH])
        key_bh = s.sb("key_bh", [P, 2, SLOTS, BH])
        key_t = s.sb("key_t", [BH, PAIR])
        wall = s.sb("wall", [BH, PAIR + 1])
        run_max = s.sb("run_max", [BH, PAIR])
        node_max = s.sb("node_max", [BH, PAIR])
        below_max = s.sb("below_max", [BH, 2, PAIR])
        total = s.sb("total", [P, 2, HEADS])
        mean = s.sb("mean", [P, 2, F])
        mean_t = s.sb("mean_t", [P, 2, 2, P])
        p_turn = s.ps("p_turn", [P, 512])
        p_q = [s.ps(f"p_q{i}", [P, 512]) for i in range(2)]
        p_soft = s.ps("p_soft", [P, 512])
        p_sum = [s.ps(f"p_sum{i}", [P, 512]) for i in range(2)]
        p_mean = s.ps("p_mean", [P, 512])
        p_next = s.ps("p_next", [P, 512])
        (placed, hot, hot_turned, hot_copied, spread, dotted, logits, soft_turned, below, soft_back, weights,
         messages, summed, averaged, mean_turned, mean_copied, product, row_done, chain_dot, chain_soft,
         chain_mean, passed, passed_pe) = (s.sem(n) for n in (
             "placed", "hot", "hot_turned", "hot_copied", "spread", "dotted", "logits", "soft_turned", "below",
             "soft_back", "weights", "messages", "summed", "averaged", "mean_turned", "mean_copied", "product",
             "row_done", "chain_dot", "chain_soft", "chain_mean", "passed", "passed_pe"))
        gathered, before = k.pool_dma[0:R], k.pool_count[0:R]
        loaded = [s.sem(f"loaded{i}") for i in range(2)]
        q_loaded = [s.sem(f"q_loaded{i}") for i in range(2)]
        stored = [s.sem(f"stored{i}") for i in range(2)]
        walls_set = s.sem("walls_set")
        rows_clear = s.sem("rows_clear")
        AHEAD = R * BATCH
        block = ctx.enter_context(nc.Block())
        turns = NBATCH // R
        flat_local = graph.local[:].rearrange("p (b j) -> p b j", j=SLOTS)

        @block.gpsimd
        def _(pool):
            pool.wait_ge(rows_clear, 1)

            def gather(a):
                pool.wait_ge(placed, a.i + 1)
                for b in range(BATCH):
                    pool.wait_ge(averaged, a.n(b)[0] + 1)
                    pool.sem_inc(passed, 1)
                    for j in range(SLOTS):
                        c = b * SLOTS + j
                        pool.indirect_dma_start(rows[:, a.s, b, j, :], None, kv_table,
                                                bass.IndirectOffsetOnAxis(place[:, a.s, c:c + 1], 0),
                                                bounds_check=N - 1, oob_is_err=False).then_inc(gathered[a.s], 16)

            with pool.Fori(0, turns) as turn:
                for h in range(R):
                    gather(Batch(turn, h))
            for h in range(R):
                k.pool_count[h] += turns * 16 * BATCH * SLOTS

        @block.sync
        def _(sp):
            def load_q(a, used=None):
                if used:
                    sp.wait_ge(spread, used.i * BATCH + (BATCH + 1))
                sp.dma_start(q_rows[:, a.q], q_table[bass.ds(a.i * (BATCH * P), BATCH * P), :].rearrange(
                    "(b p) f -> p b f", p=P)).then_inc(q_loaded[a.q], 16)

            def load_x(a):
                sp.wait_ge(stored[a.q], a.pairs * 32)
                sp.dma_start(x_rows[:, a.q], x_in[bass.ds(a.i * (BATCH * P), BATCH * P), :].rearrange(
                    "(b p) f -> p b f", p=P)).then_inc(loaded[a.q], 16)

            def store(a, last=False):
                sp.wait_ge(row_done, (a.i + 1) * BATCH)
                m = TAIL_FULL
                if last:
                    n0 = (NBATCH - 1) * BATCH * P
                    sp.dma_start(x_out[n0:n0 + m * P, :].rearrange("(b p) f -> p b f", p=P),
                                 x_rows[:, a.q, 0:m, :]).then_inc(stored[a.q], 16)
                    sp.dma_start(x_out[n0 + m * P:N, :], x_rows[0:TAIL_REST, a.q, m, :]).then_inc(stored[a.q], 16)
                else:
                    v = x_out[bass.ds(a.i * (BATCH * P), BATCH * P), :].rearrange("(b p) f -> p b f", p=P)
                    sp.dma_start(v[:, 0:m, :], x_rows[:, a.q, 0:m, :]).then_inc(stored[a.q], 16)
                    sp.dma_start(v[:, m:BATCH, :], x_rows[:, a.q, m:BATCH, :]).then_inc(stored[a.q], 16)

            for h in range(R):
                load_q(Batch(0, h))
            load_x(Batch(0, 0))
            with sp.Fori(0, turns - 1) as turn:
                for h in range(R):
                    load_x(Batch(turn, h + 1))
                    load_q(Batch(turn, h + 2), Batch(turn, h))
                    store(Batch(turn, h))
            load_x(Batch(turns - 1, 1))
            store(Batch(turns - 1, 0))
            store(Batch(turns - 1, 1), True)
            for q in range(2):
                sp.wait_ge(stored[q], 32 * (NBATCH // 2))

        @block.vector
        def _(dve):
            def make_place(a):
                dve.wait_ge(gathered[a.s], a.round * (16 * BATCH * SLOTS) + before[a.s])
                dve.tensor_copy(place[:, a.s, :], graph.index[:, bass.ds(a.i * (BATCH * SLOTS), BATCH * SLOTS)]
                                ).then_inc(placed, 1)

            def make_onehot(a, b):
                for j in range(SLOTS):
                    last = dve.tensor_scalar(onehot[:, a.s, b * SLOTS + j, :], k.iota_f[:, 0:P],
                                             graph.local[:, bass.ds((a.i * BATCH + b) * SLOTS + j, 1)],
                                             None, ALU.is_equal)
                last.then_inc(hot, 1)

            def dot(a, b):
                n, q = a.n(b)
                ch = Chain(dve, chain_dot, per=1, turn=n)
                if b == 0:
                    dve.wait_ge(gathered[a.s], (a.round + 1) * (16 * BATCH * SLOTS) + before[a.s])
                dve.wait_ge(spread, n + 2)
                kq = rows[:, a.s, b, :, 0:F]
                ins = dve.tensor_tensor(kq, kq, p_q[q][:].rearrange("p (j f) -> p j f", j=SLOTS), ALU.mult)
                ch.link(ins)
                last = dve.tensor_reduce(logit[:, a.q, :, b * HEADS:(b + 1) * HEADS],
                                         kq.rearrange("p j (h d) -> p j h d", h=HEADS), axis=AX.X, op=ALU.add)
                last.then_inc(dotted, 1)

            def copy_keys(a):
                for j in range(SLOTS):
                    last = dve.tensor_copy(
                        key_bh[:, a.q, j, :].rearrange("p (b h) -> p b h", h=HEADS),
                        flat_local[:, bass.ds(a.i * BATCH, BATCH), j:j + 1].to_broadcast([P, BATCH, HEADS]))
                last.then_inc(logits, 1)

            def subtract_max(a, ch):
                dve.wait_ge(soft_turned, a.i + 1)
                ch.link(dve.tensor_copy(key_t[:], p_soft[0:BH, PAIR:2 * PAIR]))
                ch.link(dve.tensor_tensor(wall[:, 1:PAIR], key_t[:, 1:PAIR], key_t[:, 0:PAIR - 1], ALU.is_equal))
                ch.link(dve.tensor_scalar(wall[:, 1:PAIR], wall[:, 1:PAIR], 1.0, FAR, ALU.subtract, ALU.mult))
                ch.link(dve.tensor_tensor_scan(run_max[:], wall[:, 0:PAIR], p_soft[0:BH, 0:PAIR], 0.0,
                                               ALU.add, ALU.max))
                ch.link(dve.tensor_tensor_scan(node_max[:, ::-1], wall[:, PAIR:0:-1], run_max[:, ::-1], 0.0,
                                               ALU.add, ALU.max))
                dve.tensor_tensor(below_max[:, a.q], p_soft[0:BH, 0:PAIR], node_max[:], ALU.subtract).then_inc(below, 1)

            def weigh(a, b):
                if b == 0:
                    dve.wait_ge(weights, a.i + 1)
                v = rows[:, a.s, b, :, F:KV].rearrange("p j (h d) -> p j h d", h=HEADS)
                w = rows[:, a.s, b, :, F - HEADS:F]
                for j in range(SLOTS):
                    last = dve.tensor_tensor(v[:, j], v[:, j], w[:, j].unsqueeze(2).to_broadcast([P, HEADS, HD]),
                                             ALU.mult)
                last.then_inc(messages, 1)

            def average(a, b):
                n, q = a.n(b)
                ch = Chain(dve, chain_mean, per=2, turn=n)
                dve.wait_ge(summed, n + 1)
                ch.link(dve.tensor_scalar(total[:, q], p_sum[q][:, 0:HEADS], TINY, None, ALU.max))
                ch.link(dve.reciprocal(total[:, q], total[:, q]))
                dve.wait_ge(mean_turned, n)
                dve.tensor_tensor(mean[:, q].rearrange("p (h d) -> p h d", h=HEADS),
                                  p_sum[q][:, HEADS:ROW].rearrange("p (h d) -> p h d", h=HEADS),
                                  total[:, q].unsqueeze(2).to_broadcast([P, HEADS, HD]), ALU.mult).then_inc(averaged, 1)

            def finish(a, b):
                n, q = a.n(b)
                dve.wait_ge(product, n + 2)
                if b == 0:
                    dve.wait_ge(loaded[a.q], (a.pairs + 1) * 16)
                v = x_rows[:, a.q, b, :]
                dve.tensor_tensor(v, p_next[:, 0:F], v, ALU.add).then_inc(row_done, 1)

            SOFT = 5

            def first():
                dve.memset(rows[:], 0.0).then_inc(rows_clear, 1)
                dve.wait_ge(rows_clear, 1)
                dve.memset(wall[:, 0:1], -FAR).then_inc(walls_set, 1)
                dve.memset(wall[:, PAIR:PAIR + 1], -FAR).then_inc(walls_set, 1)
                dve.wait_ge(walls_set, 2)
                dve.sem_inc(averaged, AHEAD)
                dve.sem_inc(dotted, 1)
                for h in range(R):
                    make_place(Batch(0, h))
                a = Batch(0, 0)
                for b in range(BATCH):
                    make_onehot(a, b)
                for b in range(BATCH):
                    dot(a, b)
                copy_keys(a)
                ch = Chain(dve, chain_soft, per=SOFT, turn=0)
                subtract_max(a, ch)
                ch.close()

            def batch(a, after):
                for st in range(9):
                    if st == 0 and after >= 2:
                        make_place(a.plus(2))
                    if st < BATCH:
                        weigh(a, st)
                    if st < BATCH and after >= 1:
                        make_onehot(a.plus(1), st)
                    if 1 <= st <= BATCH:
                        average(a, st - 1)
                    if 2 <= st:
                        finish(a, st - 2)
                    if 1 <= st <= BATCH and after >= 1:
                        dot(a.plus(1), st - 1)
                if after >= 1:
                    copy_keys(a.plus(1))
                    ch = Chain(dve, chain_soft, per=SOFT, turn=a.plus(1).i)
                    subtract_max(a.plus(1), ch)
                    ch.close()

            over_batches(dve, first, batch, turns)

        @block.tensor
        def _(pe):
            def turn_onehot(a, b):
                n, q = a.n(b)
                pe.wait_ge(hot, n + 1)
                pe.wait_ge(hot_copied, n)
                for j in range(SLOTS):
                    last = nc.tensor.transpose(p_turn[:, j * P:(j + 1) * P], onehot[:, a.s, b * SLOTS + j, :], k.ident[:])
                last.then_inc(hot_turned, 1)

            def spread_q(a, b):
                n, q = a.n(b)
                pe.wait_ge(hot_copied, n + 1)
                pe.wait_ge(dotted, n)
                if b == 0:
                    pe.wait_ge(q_loaded[a.q], (a.pairs + 1) * 16)
                for j in range(SLOTS):
                    last = nc.tensor.matmul(p_q[q][:, j * F:(j + 1) * F], onehot_t[:, q, j * P:(j + 1) * P],
                                            q_rows[:, a.q, b, :], start=True, stop=True)
                last.then_inc(spread, 1)

            def turn_soft(a):
                pe.wait_ge(logits, a.i + 1)
                pe.wait_ge(weights, a.i)
                pe.sem_inc(passed_pe, 1)
                for x, c in ((logit, 0), (key_bh, PAIR)):
                    for j in range(SLOTS):
                        last = nc.tensor.transpose(p_soft[0:BH, c + j * P:c + (j + 1) * P], x[:, a.q, j, :], k.ident[:])
                last.then_inc(soft_turned, 1)

            def turn_back(a):
                pe.wait_ge(below, a.i + 1)
                pe.sem_inc(passed_pe, 1)
                for j in range(SLOTS):
                    last = nc.tensor.transpose(p_soft[:, j * BH:(j + 1) * BH], below_max[:, a.q, j * P:(j + 1) * P],
                                               k.ident[0:BH, 0:BH])
                last.then_inc(soft_back, 1)

            def add_up(a, b):
                n, q = a.n(b)
                pe.wait_ge(messages, n + 1)
                pe.wait_ge(averaged, n + (AHEAD - 1))
                for j in range(SLOTS):
                    last = nc.tensor.matmul(p_sum[q][:, 0:ROW], onehot[:, a.s, b * SLOTS + j, :], rows[:, a.s, b, j, F - HEADS:KV],
                                            start=(j == 0), stop=(j == SLOTS - 1))
                last.then_inc(summed, 1)

            def turn_mean(a, b):
                n, q = a.n(b)
                pe.wait_ge(averaged, n + (AHEAD + 1))
                pe.wait_ge(mean_copied, n)
                for c in range(2):
                    last = nc.tensor.transpose(p_mean[:, c * P:(c + 1) * P], mean[:, q, c * P:(c + 1) * P], k.ident[:])
                last.then_inc(mean_turned, 1)

            def multiply(a, b):
                n, q = a.n(b)
                pe.wait_ge(mean_copied, n + 1)
                pe.wait_ge(row_done, n)
                for c in range(2):
                    nc.tensor.matmul(p_next[:, 0:F], mean_t[:, q, c, :], k.w_o[:, c, :], start=(c == 0), stop=False)
                nc.tensor.matmul(p_next[:, 0:F], k.ones_b[0:3, :], k.bias_parts[:],
                                 start=False, stop=True).then_inc(product, 1)

            def first():
                for x in (mean_turned, product, spread):
                    pe.sem_inc(x, 1)
                a = Batch(0, 0)
                for b in range(BATCH + 1):
                    if b:
                        spread_q(a, b - 1)
                    if b < BATCH:
                        turn_onehot(a, b)
                turn_soft(a)
                turn_back(a)

            def batch(a, after):
                for st in range(9):
                    if st < BATCH:
                        add_up(a, st)
                    if 1 <= st <= BATCH and after >= 1:
                        spread_q(a.plus(1), st - 1)
                    if st < BATCH and after >= 1:
                        turn_onehot(a.plus(1), st)
                    if 1 <= st <= BATCH:
                        turn_mean(a, st - 1)
                    if 2 <= st:
                        multiply(a, st - 2)
                if after >= 1:
                    turn_soft(a.plus(1))
                    turn_back(a.plus(1))

            over_batches(pe, first, batch, turns)

        @block.scalar
        def _(act):
            def copy_onehot(a, b):
                n, q = a.n(b)
                act.wait_ge(hot_turned, n + 1)
                act.wait_ge(spread, n)
                nc.scalar.copy(onehot_t[:, q, :], p_turn[:, 0:PAIR]).then_inc(hot_copied, 1)

            def exponentiate(a):
                act.wait_ge(soft_back, a.i + 1)
                for j in range(SLOTS):
                    last = nc.scalar.activation(
                        rows[:, a.s, :, j, F - HEADS:F],
                        p_soft[:, j * BH:(j + 1) * BH].rearrange("p (b h) -> p b h", h=HEADS), ACT.Exp, scale=SCALE)
                last.then_inc(weights, 1)

            def copy_mean(a, b):
                n, q = a.n(b)
                act.wait_ge(mean_turned, n + 2)
                act.wait_ge(product, n)
                nc.scalar.copy(mean_t[:, q].rearrange("p c n -> p (c n)"), p_mean[:, 0:F]).then_inc(mean_copied, 1)

            def first():
                for b in range(BATCH):
                    copy_onehot(Batch(0, 0), b)
                exponentiate(Batch(0, 0))

            def batch(a, after):
                for st in range(9):
                    if st < BATCH and after >= 1:
                        copy_onehot(a.plus(1), st)
                    if 1 <= st <= BATCH:
                        copy_mean(a, st - 1)
                if after >= 1:
                    exponentiate(a.plus(1))

            over_batches(act, first, batch, turns)


STATE = ROW + HEADS


def any_degrees_layer(nc, k, tag, keys, others, table, side, finish, scale=None):
    dot = scale is not None
    cols, side_cols, at = (2 * F, F, F) if dot else (ROW, HEADS, 0)
    state = nc.dram_tensor(f"{tag}_state", (NP, STATE), F32, kind="Internal").ap()
    with ExitStack() as ctx:
        s = Scope(nc, ctx, tag)
        key_i = s.sb("key", [P, T], I32)
        oth_i = s.sb("oth", [P, T], I32)
        ask = s.sb("ask", [P, 3], I32)
        key_f = s.sb("key_f", [P, 1])
        later = s.sb("later", [P, P])
        empty = s.sb("empty", [P, BATCH, STATE])
        rows = s.sb("rows", [P, cols])
        mine = s.sb("mine", [P, side_cols])
        old = s.sb("old", [P, STATE])
        new = s.sb("new", [P, STATE])
        diag = s.sb("diag", [P, P])
        diags = s.sb("diags", [P, HEADS, P])
        same = s.sb("same", [P, P])
        apart = s.sb("apart", [P, P])
        masked = s.sb("masked", [P, HEADS, P])
        count = s.sb("count", [P, 1])
        logit = s.sb("logit", [P, HEADS])
        diffs = s.sb("diffs", [P, 2, HEADS])
        powers = s.sb("powers", [P, HEADS])
        message = s.sb("message", [P, ROW])
        p_key = s.ps("p_key", [P, 512])
        p_logit = [s.ps(f"p_logit{i}", [P, 512]) for i in range(2)]
        p_sum = s.ps("p_sum", [P, 512])
        (loaded, cleared, emptied, chain, asked, diag_ready, key_spread, logits, logits_spread, maxima, powered,
         messages, summed, updated, passed) = (s.sem(n) for n in (
             "loaded", "cleared", "emptied", "chain", "asked", "diag_ready", "key_spread", "logits",
             "logits_spread", "maxima", "powered", "messages", "summed", "updated", "passed"))
        arrived, before = k.pool_dma, list(k.pool_count)
        block = ctx.enter_context(nc.Block())
        full, rest = E // T, E % T

        @block.sync
        def _(sp):
            sp.wait_ge(cleared, 1)
            for to, of in ((key_i, keys), (oth_i, others)):
                for lo, hi in ((0, 112), (112, full)):
                    sp.dma_start(to[lo:hi, :], of[lo * T:hi * T].rearrange("(p t) -> p t", t=T)).then_inc(loaded, 16)
                sp.dma_start(to[full:full + 1, 0:rest],
                             of[full * T:E].rearrange("(p t) -> p t", p=1)).then_inc(loaded, 16)
            for i in range(NBATCH):
                sp.dma_start(state[i * BATCH * P:(i + 1) * BATCH * P, :].rearrange("(b p) c -> p b c", p=P),
                             empty[:]).then_inc(emptied, 16)
            sp.wait_ge(emptied, 16 * NBATCH)

        @block.gpsimd
        def _(pool):
            pool.wait_ge(emptied, 16 * NBATCH)
            with pool.Fori(0, T) as t:
                pool.wait_ge(arrived[3], t * 16 + before[3])
                pool.wait_ge(asked, t + 1)
                pool.sem_inc(passed, 1)
                for i, (to, of, c, bound) in enumerate(((old, state, 0, NP), (rows, table, 1, N), (mine, side, 0, NP))):
                    pool.indirect_dma_start(to[:], None, of, bass.IndirectOffsetOnAxis(ask[:, c:c + 1], 0),
                                            bounds_check=bound - 1, oob_is_err=False).then_inc(arrived[i], 16)
                pool.wait_ge(updated, t + 1)
                pool.sem_inc(passed, 1)
                pool.indirect_dma_start(state, bass.IndirectOffsetOnAxis(ask[:, 2:3], 0), new[:], None,
                                        bounds_check=NP - 1, oob_is_err=False).then_inc(arrived[3], 16)
            pool.wait_ge(arrived[3], T * 16 + before[3])
            for i in range(4):
                k.pool_count[i] += T * 16

        @block.vector
        def _(dve):
            ch = Chain(dve, chain)
            dve.memset(key_i[:], (NBK - 1) * P)
            dve.memset(oth_i[:], 0)
            ch.link(dve.memset(empty[:, :, 0:ROW], 0.0))
            ch.link(dve.memset(empty[:, :, ROW:STATE], -FAR))
            dve.sem_inc(cleared, 1)
            ch.link(dve.tensor_tensor(later[:], k.ones[:], k.tri_f[:], ALU.subtract))
            ch.link(dve.tensor_tensor(later[:], later[:], k.ident[:], ALU.subtract))
            dve.wait_ge(loaded, 16 * 6)
            base, PER = ch.k, (15 if dot else 14)
            with dve.Fori(0, T) as t:
                ch = Chain(dve, chain, per=PER, turn=t, base=base)
                dve.wait_ge(arrived[3], t * 16 + before[3])
                dve.tensor_copy(ask[:, 0:1], key_i[:, bass.ds(t, 1)])
                dve.tensor_copy(ask[:, 1:2], oth_i[:, bass.ds(t, 1)]).then_inc(asked, 1)
                ch.link(dve.tensor_copy(key_f[:], key_i[:, bass.ds(t, 1)]))
                dve.tensor_scalar(diag[:], k.ident[:], key_f[:], None, ALU.mult).then_inc(diag_ready, 1)
                dve.wait_ge(key_spread, t + 1)
                ch.link(dve.tensor_scalar(same[:], p_key[:, 0:P], key_f[:], None, ALU.is_equal))
                ch.link(dve.tensor_scalar(apart[:], same[:], 1.0, FAR, ALU.subtract, ALU.mult))
                ch.link(dve.tensor_tensor(diag[:], same[:], later[:], ALU.mult))
                ch.link(dve.tensor_reduce(count[:], diag[:], axis=AX.X, op=ALU.add))
                ch.link(dve.tensor_scalar(count[:], count[:], 0.5, float(1 << 20), ALU.is_ge, ALU.mult))
                ch.link(dve.tensor_tensor(ask[:, 2:3], count[:], key_f[:], ALU.add))
                for i in range(3):
                    dve.wait_ge(arrived[i], (t + 1) * 16 + before[i])
                if dot:
                    ch.link(dve.tensor_tensor(rows[:, 0:F], rows[:, 0:F], mine[:], ALU.mult))
                    ch.link(dve.tensor_reduce(logit[:], rows[:, 0:F].rearrange("p (h d) -> p h d", h=HEADS),
                                              axis=AX.X, op=ALU.add))
                    ch.link(dve.tensor_scalar(logit[:], logit[:], scale, None, ALU.mult))
                else:
                    ch.link(dve.tensor_tensor(logit[:], rows[:, F:ROW], mine[:], ALU.add))
                    ch.link(dve.scalar_tensor_tensor(out=logit[:], in0=logit[:], scalar=SLOPE_ATTN, in1=logit[:],
                                                     op0=ALU.mult, op1=ALU.max))
                dve.tensor_tensor(diags[:], k.ident[:].unsqueeze(1).to_broadcast([P, HEADS, P]),
                                  logit[:].unsqueeze(2).to_broadcast([P, HEADS, P]), ALU.mult).then_inc(logits, 1)
                dve.wait_ge(logits_spread, t + 1)
                half = HEADS // 2
                for i in range(2):
                    last = dve.tensor_tensor(masked[:, i * half:(i + 1) * half, :],
                                             p_logit[i][:].rearrange("p (h e) -> p h e", h=half),
                                             apart[:].unsqueeze(1).to_broadcast([P, half, P]), ALU.add)
                ch.link(last)
                ch.link(dve.tensor_reduce(powers[:], masked[:], axis=AX.X, op=ALU.max))
                ch.link(dve.tensor_tensor(new[:, ROW:STATE], powers[:], old[:, ROW:STATE], ALU.max))
                dve.tensor_tensor(diffs[:, 0], old[:, ROW:STATE], new[:, ROW:STATE], ALU.subtract)
                dve.tensor_tensor(diffs[:, 1], logit[:], new[:, ROW:STATE], ALU.subtract).then_inc(maxima, 1)
                dve.wait_ge(powered, t + 1)
                v = rows[:, at:at + F].rearrange("p (h d) -> p h d", h=HEADS)
                dve.tensor_tensor(message[:, HEADS:ROW].rearrange("p (h d) -> p h d", h=HEADS), v,
                                  message[:, 0:HEADS].unsqueeze(2).to_broadcast([P, HEADS, HD]),
                                  ALU.mult).then_inc(messages, 1)
                dve.tensor_tensor(old[:, 0:HEADS], old[:, 0:HEADS], powers[:], ALU.mult)
                o = old[:, HEADS:ROW].rearrange("p (h d) -> p h d", h=HEADS)
                ch.link(dve.tensor_tensor(o, o, powers[:].unsqueeze(2).to_broadcast([P, HEADS, HD]), ALU.mult))
                dve.wait_ge(summed, t + 1)
                ch.link(dve.tensor_tensor(new[:, 0:ROW], p_sum[:, 0:ROW], old[:, 0:ROW], ALU.add))
                dve.sem_inc(updated, 1)
                ch.close()

        @block.tensor
        def _(pe):
            with pe.Fori(0, T) as t:
                pe.wait_ge(diag_ready, t + 1)
                nc.tensor.matmul(p_key[:, 0:P], k.ones[:], diag[:], start=True, stop=True).then_inc(key_spread, 1)
                pe.wait_ge(logits, t + 1)
                half = HEADS // 2
                for i in range(2):
                    last = nc.tensor.matmul(p_logit[i][:], k.ones[:], diags[:, i * half:(i + 1) * half, :],
                                            start=True, stop=True)
                last.then_inc(logits_spread, 1)
                pe.wait_ge(messages, t + 1)
                nc.tensor.matmul(p_sum[:, 0:ROW], same[:], message[:], start=True, stop=True).then_inc(summed, 1)

        @block.scalar
        def _(act):
            with act.Fori(0, T) as t:
                act.wait_ge(maxima, t + 1)
                nc.scalar.activation(powers[:], diffs[:, 0], ACT.Exp)
                nc.scalar.activation(message[:, 0:HEADS], diffs[:, 1], ACT.Exp).then_inc(powered, 1)

    finish(state)


def write_er(nc, k, layer, er_table):
    with ExitStack() as ctx:
        s = Scope(nc, ctx, f"er_rows{layer}")
        written = s.sem("written")
        block = ctx.enter_context(nc.Block())

        @block.sync
        def _(sp):
            sp.dma_start(er_table.rearrange("(b p) h -> p b h", p=P),
                         k.er[:].rearrange("p (b h) -> p b h", h=HEADS)).then_inc(written, 16)
            sp.wait_ge(written, 16)


def finish_nodes(nc, k, tag, state, kind, layer=0, table_out=None, x_in=None, x_out=None):
    with ExitStack() as ctx:
        s = Scope(nc, ctx, tag)
        st = s.sb("st", [P, STATE])
        total = s.sb("total", [P, HEADS])
        mean = s.sb("mean", [P, F])
        mean_t = s.sb("mean_t", [P, 2, P])
        x_row = s.sb("x_row", [P, F])
        out_row = s.sb("out_row", [P, ROW])
        p_mean = s.ps("p_mean", [P, 512])
        p_next = s.ps("p_next", [P, 512])
        loaded, x_loaded, chain, divided, turned, copied, product, made, stored = (s.sem(n) for n in (
            "loaded", "x_loaded", "chain", "divided", "turned", "copied", "product", "made", "stored"))
        block = ctx.enter_context(nc.Block())
        full = N // P
        ends = [(full, N - full * P), (full + 1, 0)]
        out = table_out if kind == "table" else x_out
        width = ROW if kind == "table" else F
        padded = out.shape[0] == NP
        use_x = kind != "table"

        def each(eng, one):
            with eng.Fori(0, full) as b:
                one(b, P)
            for b, have in ends:
                one(b, have)

        @block.sync
        def _(sp):
            def one(b, have):
                sp.wait_ge(stored, b * 16)
                sp.dma_start(st[:], state[bass.ds(b * P, P), :]).then_inc(loaded, 16)
                if use_x and (have or x_in.shape[0] == NP):
                    n = P if x_in.shape[0] == NP else have
                    sp.dma_start(x_row[0:n, :], x_in[bass.ds(b * P, n), :]).then_inc(x_loaded, 16)
                elif use_x:
                    sp.sem_inc(x_loaded, 16)
                sp.wait_ge(made, b + 1)
                n = P if padded else have
                if n:
                    sp.dma_start(out[bass.ds(b * P, n), :], out_row[0:n, 0:width]).then_inc(stored, 16)
                    if not isinstance(b, int) or b < full + (1 if padded else 0):
                        return
                    sp.wait_ge(stored, (b + 1) * 16)
                else:
                    sp.sem_inc(stored, 16)

            each(sp, one)

        @block.vector
        def _(dve):
            dve.memset(x_row[:], 0.0)
            PER = {"table": 3, "sum": 4, "product": 3}[kind]

            def one(b, have):
                ch = Chain(dve, chain, per=PER, turn=b)
                dve.wait_ge(loaded, (b + 1) * 16)
                ch.link(dve.tensor_scalar(total[:], st[:, 0:HEADS], TINY, None, ALU.max))
                ch.link(dve.reciprocal(total[:], total[:]))
                ins = dve.tensor_tensor(mean[:].rearrange("p (h d) -> p h d", h=HEADS),
                                        st[:, HEADS:ROW].rearrange("p (h d) -> p h d", h=HEADS),
                                        total[:].unsqueeze(2).to_broadcast([P, HEADS, HD]), ALU.mult)
                ch.link(ins)
                dve.sem_inc(divided, 1)
                if use_x:
                    dve.wait_ge(x_loaded, (b + 1) * 16)
                if kind == "sum":
                    ch.link(dve.tensor_tensor(mean[:], mean[:], k.b2_row[:], ALU.add))
                    dve.tensor_tensor(out_row[:, 0:F], mean[:], x_row[:], ALU.add).then_inc(made, 1)
                if kind == "table":
                    dve.wait_ge(turned, (b + 1) * 2)
                    v = mean_t[:].rearrange("p c n -> p (c n)")
                    dve.scalar_tensor_tensor(out=v, in0=v, scalar=SLOPE_ACT, in1=v,
                                             op0=ALU.mult, op1=ALU.max).then_inc(copied, 1)
                if kind == "product":
                    dve.wait_ge(product, b + 1)
                    dve.tensor_tensor(out_row[:, 0:F], p_next[:, 0:F], x_row[:], ALU.add).then_inc(made, 1)
                ch.close()

            each(dve, one)

        @block.tensor
        def _(pe):
            def one(b, have):
                pe.wait_ge(divided, b + 1)
                for c in range(2):
                    last = nc.tensor.transpose(p_mean[:, c * P:(c + 1) * P], mean[:, c * P:(c + 1) * P], k.ident[:])
                last.then_inc(turned, 1)
                pe.wait_ge(copied, b + 1)
                w = k.w_gat[:, layer + 1] if kind == "table" else k.w_o
                cols = WCOLS if kind == "table" else F
                for c in range(2):
                    last = nc.tensor.matmul(p_next[:, 0:cols], mean_t[:, c, :], w[:, c, :],
                                            start=(c == 0), stop=(c == 1 and kind == "table"))
                if kind == "product":
                    last = nc.tensor.matmul(p_next[:, 0:cols], k.ones_b[0:3, :], k.bias_parts[:],
                                            start=False, stop=True)
                last.then_inc(product, 1)

            if kind != "sum":
                each(pe, one)

        @block.scalar
        def _(act):
            def one(b, have):
                if kind == "table":
                    act.wait_ge(turned, b * 2 + 1)
                    for c in range(2):
                        last = nc.scalar.activation(mean_t[:, c, :], p_mean[:, c * P:(c + 1) * P], ACT.Identity,
                                                    bias=k.b_col[:, layer, c:c + 1])
                    last.then_inc(turned, 1)
                    act.wait_ge(product, b + 1)
                    nc.scalar.copy(out_row[:], p_next[:, 0:ROW])
                    nc.scalar.copy(k.er[:, bass.ds(b * HEADS, HEADS)], p_next[:, ROW:WCOLS]).then_inc(made, 1)
                else:
                    act.wait_ge(turned, b + 1)
                    nc.scalar.copy(mean_t[:].rearrange("p c n -> p (c n)"), p_mean[:, 0:F]).then_inc(copied, 1)

            if kind != "sum":
                each(act, one)


FITS = 0


def gnn_kernel(nc, x, src, dst, W, al, ar, b, w_qkv, b_qkv, w_o, b_o, out):
    with ExitStack() as ctx:
        s = Scope(nc, ctx, "kept")
        k = Constants(s)
        k.w_gat = s.sb("w_gat", [P, 3, 2, WCOLS])
        k.b_col = s.sb("b_col", [P, 3, 2])
        k.b2_row = s.sb("b2_row", [P, F])
        k.w_qkv = s.sb("w_qkv", [P, 2, 3 * F])
        k.w_o = s.sb("w_o", [P, 2, F])
        k.b_qkv_row = s.sb("b_qkv_row", [P, 3 * F])
        k.bias_parts = s.sb("bias_parts", [3, F], BF16)
        k.er = s.sb("er", [P, NBK * HEADS])
        index = [s.sb(f"index{g}", [P, NBK * SLOTS], I32) for g in range(2)]
        local = [s.sb(f"local{g}", [P, NBK * SLOTS]) for g in range(2)]
        places = [nc.dram_tensor(f"places{g}", (SP_ROWS, 2), I32, kind="Internal").ap() for g in range(2)]
        tables = [nc.dram_tensor(f"table{i}", (NP, ROW), F32, kind="Internal").ap() for i in range(2)]
        x2 = nc.dram_tensor("x2", (NP, F), F32, kind="Internal").ap()
        er_table = nc.dram_tensor("er_table", (NP, HEADS), F32, kind="Internal").ap()
        q_table = nc.dram_tensor("q_table", (NP, F), F32, kind="Internal").ap()
        kv_table = nc.dram_tensor("kv_table", (NP, 2 * F), F32, kind="Internal").ap()

        make_constants(nc, k)
        load_weights(nc, k, W, al, ar, b, w_qkv, b_qkv, w_o, b_o)
        distribute(nc, k, [dst, src], [src, dst], places)
        sort_buckets(nc, k, places, index, local)
        by_dst, by_src = (Graph(index[g], local[g]) for g in range(2))
        project(nc, k, "first", x, [(tables[0], ROW, k.w_gat[:, 0], WCOLS, None)], k.er)

        crowded = nc.values_load(k.crowded[0:1, 0:1].bitcast(mybir.dt.uint32), min_val=0, max_val=1)
        dealt = list(k.pool_count)
        with nc.If(crowded == FITS):
            gat_layer(nc, k, by_dst, tables[0], 0, tables[1])
            gat_layer(nc, k, by_dst, tables[1], 1, tables[0])
            last_gat_layer(nc, k, by_dst, tables[0], x, x2)
        if_fit, k.pool_count = k.pool_count, dealt
        with nc.Else():
            for layer in range(3):
                write_er(nc, k, layer, er_table)
                kind = "sum" if layer == 2 else "table"
                any_degrees_layer(nc, k, f"any{layer}", dst, src, tables[layer % 2], er_table,
                                  lambda state: finish_nodes(nc, k, f"end{layer}", state, kind, layer,
                                                             tables[(layer + 1) % 2], x, x2))
        project(nc, k, "qkv", x2, [(q_table, F, k.w_qkv[:, :, 0:F], F, k.b_qkv_row[:, 0:F]),
                                   (kv_table, 2 * F, k.w_qkv[:, :, F:3 * F], 2 * F, k.b_qkv_row[:, F:3 * F])])
        if_crowded, k.pool_count = k.pool_count, if_fit
        with nc.If(crowded == FITS):
            dot_layer(nc, k, by_src, q_table, kv_table, x2, out)
        k.pool_count = if_crowded
        with nc.Else():
            any_degrees_layer(nc, k, "any3", src, dst, kv_table, q_table,
                              lambda state: finish_nodes(nc, k, "end3", state, "product", x_in=x2, x_out=out), SCALE)


def kernel(x, src, dst, L0_gnn_W, L0_gnn_al, L0_gnn_ar, L0_gnn_b, L1_gnn_Wq, L1_gnn_bq, L1_gnn_Wk, L1_gnn_bk,
           L1_gnn_Wv, L1_gnn_bv, L1_gnn_Wo, L1_gnn_bo):
    import numpy as np
    import concourse.bacc as bacc
    from concourse.bass_utils import run_bass_kernel_spmd

    def head_major(a):
        a = np.asarray(a)
        return a.reshape(a.shape[:-1] + (HD, HEADS)).swapaxes(-1, -2).reshape(a.shape)

    w_qkv = np.concatenate([head_major(np.asarray(w).T) for w in (L1_gnn_Wq, L1_gnn_Wk, L1_gnn_Wv)], axis=1)
    b_qkv = np.concatenate([head_major(b) for b in (L1_gnn_bq, L1_gnn_bk, L1_gnn_bv)])
    given = {
        "x": x, "src": src, "dst": dst, "W": L0_gnn_W, "al": L0_gnn_al, "ar": L0_gnn_ar, "b": L0_gnn_b,
        "w_qkv": w_qkv, "b_qkv": b_qkv, "w_o": head_major(L1_gnn_Wo).T, "b_o": L1_gnn_bo,
    }
    nc = bacc.Bacc("TRN2", target_bir_lowering=False, num_devices=1)
    arrays, args = {}, []
    for name, a in given.items():
        a = np.ascontiguousarray(a)
        arrays[f"in_{name}"] = a
        args.append(nc.dram_tensor(f"in_{name}", a.shape, mybir.dt.from_np(a.dtype), kind="ExternalInput").ap())
    out = nc.dram_tensor("out_0", (N, F), F32, kind="ExternalOutput").ap()
    gnn_kernel(nc, *args, out)
    return run_bass_kernel_spmd(nc, [arrays], core_ids=[0]).results[0]["out_0"]
```

```python
import concourse.bass as bass
from concourse import mybir
from contextlib import ExitStack

F32 = mybir.dt.float32
BF16 = mybir.dt.bfloat16
F16 = mybir.dt.float16
I32 = mybir.dt.int32
ALU = mybir.AluOpType
ACT = mybir.ActivationFunctionType
AX = mybir.AxisListType

N = 50000
E = 75000
F = 256
HEADS = 8
HD = F // HEADS
P = 128
BATCH = 7
NBK = 392
NBATCH = NBK // BATCH
ROW = F + HEADS
SLOTS = 2
SP_ROWS = P * NBK * SLOTS
T = 588
U = 7
NO_KEY = P
NO_NODE = N


class Chain:

    def __init__(self, eng, sem, per=0, turn=0, base=0):
        self.eng, self.sem, self.per, self.k = eng, sem, per, 0
        self.at = turn * per + base if per else base

    def done(self, ins):
        self.k += 1
        ins.then_inc(self.sem, 1)
        return self.at + self.k

    def link(self, ins):
        self.eng.wait_ge(self.sem, self.done(ins))

    def close(self):
        assert self.k == self.per, f"a turn has {self.k} increments, not {self.per}"


class Scope:

    def __init__(self, nc, ctx, tag):
        self.nc, self.ctx, self.tag, self.sems = nc, ctx, tag, []
        ctx.callback(self.clear)

    def sb(self, name, shape, dt=F32):
        return self.ctx.enter_context(self.nc.sbuf_tensor(f"{self.tag}_{name}", shape, dt))

    def ps(self, name, shape, dt=F32):
        return self.ctx.enter_context(self.nc.psum_tensor(f"{self.tag}_{name}", shape, dt))

    def sem(self, name):
        self.sems.append(self.ctx.enter_context(self.nc.semaphore(f"{self.tag}_{name}")))
        return self.sems[-1]

    def clear(self):
        if self.sems:
            with self.nc.Block() as block:

                @block.sync
                def _(sp):
                    for sem in self.sems:
                        sp.sem_clear(sem)


def make_constants(nc, k):
    with ExitStack() as ctx:
        s = Scope(nc, ctx, "const")
        filled, cast = s.sem("filled"), s.sem("cast")
        block = ctx.enter_context(nc.Block())

        @block.gpsimd
        def _(pool):
            pool.memset(k.ones[:], 1.0).then_inc(filled, 1)
            pool.iota(k.iota_f[:], pattern=[[1, NBK]], base=0, channel_multiplier=0,
                      allow_small_or_imprecise_dtypes=True).then_inc(filled, 1)
            pool.iota(k.slot_f[:], pattern=[[P, SLOTS]], base=0, channel_multiplier=1,
                      allow_small_or_imprecise_dtypes=True).then_inc(filled, 1)
            pool.wait_ge(filled, 3)
            pool.affine_select(out=k.ident[:], in_=k.ones[:], compare_op=ALU.is_equal, fill=0.0,
                               base=0, pattern=[[1, P]], channel_multiplier=-1).then_inc(filled, 1)
            pool.affine_select(out=k.tri_f[:], in_=k.ones[:], compare_op=ALU.is_gt, fill=0.0,
                               base=0, pattern=[[1, P]], channel_multiplier=-1).then_inc(filled, 1)

        @block.vector
        def _(dve):
            dve.wait_ge(filled, 5)
            ch = Chain(dve, cast)
            dve.tensor_copy(k.iota_h[:], k.iota_f[:])
            dve.tensor_scalar(k.balance_b[:], k.iota_f[:, 0:SLOTS * P], 2.0, float(1 - SLOTS * P), ALU.mult, ALU.add)
            dve.tensor_copy(k.ident_b[:], k.ident[:])
            dve.tensor_copy(k.before_b[:], k.tri_f[:])
            dve.tensor_tensor(k.notbefore_b[:], k.ones[:], k.tri_f[:], ALU.subtract)
            dve.tensor_scalar(k.all256_b[:], k.ones[:], 256.0, None, ALU.mult)
            dve.tensor_scalar(k.ones_b[:], k.ones[:], 1.0, None, ALU.mult)
            dve.memset(k.zeros_b[:], 0.0)
            ch.link(dve.memset(k.fill_i[:, :, 0:1], NO_NODE))
            ch.link(dve.memset(k.fill_i[:, :, 1:2], NO_KEY))


def distribute(nc, k, keys, others, places):
    NG = 2
    with ExitStack() as ctx:
        s = Scope(nc, ctx, "deal")
        key_i = [s.sb(f"key{g}", [P, T], I32) for g in range(NG)]
        oth_i = [s.sb(f"oth{g}", [P, T], I32) for g in range(NG)]
        tmp_i = s.sb("tmp", [P, T], I32)
        bucket = [s.sb(f"bucket{g}", [P, T + 1]) for g in range(NG)]
        pair = [s.sb(f"pair{g}", [P, T, 2], I32) for g in range(NG)]
        onehot = [s.sb(f"onehot{g}", [P, 2, NBK], BF16) for g in range(NG)]
        most = s.sb("most", [P, NG])
        junk = [s.sb(f"junk{g}", [P, 2, NBK], BF16) for g in range(NG)]
        rank = [s.sb(f"rank{g}", [P, U]) for g in range(NG)]
        wrap = [s.sb(f"wrap{g}", [P, U]) for g in range(NG)]
        lin = [s.sb(f"lin{g}", [P, U]) for g in range(NG)]
        place = [s.sb(f"place{g}", [P, 2, U], I32) for g in range(NG)]
        payload = [s.sb(f"payload{g}", [P, 2, U, 2], I32) for g in range(NG)]
        earlier = [s.ps(f"earlier{g}", [P, 512]) for g in range(NG)]
        loaded, filled, padded = s.sem("loaded"), s.sem("filled"), s.sem("padded")
        chain = s.sem("chain")
        keyed = s.sem("keyed")
        hot = [s.sem(f"hot{g}") for g in range(NG)]
        counted = [s.sem(f"counted{g}") for g in range(NG)]
        ranked = [s.sem(f"ranked{g}") for g in range(NG)]
        placed = [s.sem(f"placed{g}") for g in range(NG)]
        passed = s.sem("passed")
        scattered = [[k.pool_dma[2 * g + h] for h in range(2)] for g in range(NG)]
        block = ctx.enter_context(nc.Block())
        full, rest = E // T, E % T
        turns = T // (2 * U)

        @block.sync
        def _(sp):
            for g in range(NG):
                sp.dma_start(places[g].rearrange("(p r) c -> p (r c)", p=P),
                             k.fill_i[:].rearrange("p r c -> p (r c)")).then_inc(filled, 16)
            sp.wait_ge(padded, 1)
            for g in range(NG):
                for to, of in ((key_i[g], keys[g]), (oth_i[g], others[g])):
                    for lo, hi in ((0, 112), (112, full)):
                        sp.dma_start(to[lo:hi, :],
                                     of[lo * T:hi * T].rearrange("(p t) -> p t", t=T)).then_inc(loaded, 16)
                    sp.dma_start(to[full:full + 1, 0:rest],
                                 of[full * T:E].rearrange("(p t) -> p t", p=1)).then_inc(loaded, 16)

        @block.vector
        def _(dve):
            ch = Chain(dve, chain)
            for g in range(NG):
                dve.memset(key_i[g][:], (NBK - 1) * P)
                ch.link(dve.memset(oth_i[g][:], 0))
            dve.sem_inc(padded, 1)
            dve.wait_ge(loaded, 16 * 3 * 2 * NG)
            for g in range(NG):
                dve.tensor_copy(pair[g][:, :, 0], oth_i[g][:])
                ch.link(dve.tensor_scalar(pair[g][:, :, 1], key_i[g][:], P - 1, None, ALU.bitwise_and))
                ch.link(dve.tensor_scalar(tmp_i[:], key_i[g][:], 7, None, ALU.logical_shift_right))
                dve.memset(bucket[g][:, T:T + 1], -1.0)
                ch.link(dve.tensor_copy(bucket[g][:, 0:T], tmp_i[:]))
            base = ch.k

            def make_onehot(g, slot, t):
                dve.tensor_scalar(onehot[g][:, slot, :], k.iota_h[:], bucket[g][:, bass.ds(t, 1)],
                                  None, ALU.is_equal).then_inc(hot[g], 1)

            for g in range(NG):
                make_onehot(g, 0, 0)
            with dve.Fori(0, turns) as turn:
                ch = Chain(dve, chain, per=4 * NG, turn=turn, base=base)
                for half in range(2):
                    for u in range(U):
                        t = turn * (2 * U) + (half * U + u)
                        slot = (half * U + u) % 2
                        for g in range(NG):
                            dve.wait_ge(counted[g], 2 * t + 1)
                            dve.wait_ge(hot[g], t + 1)
                            dve.tensor_tensor_reduce(out=junk[g][:, slot, :], in0=earlier[g][:, 0:NBK],
                                                     in1=onehot[g][:, slot, :], scale=1.0, scalar=0.0,
                                                     op0=ALU.mult, op1=ALU.add,
                                                     accum_out=rank[g][:, u:u + 1]).then_inc(ranked[g], 1)
                            make_onehot(g, 1 - slot, t + 1)
                    t0 = turn * (2 * U) + half * U
                    for g in range(NG):
                        dve.wait_ge(ranked[g], t0 + U)
                        dve.tensor_scalar(wrap[g][:], rank[g][:], float(P), float(1 - P * NBK * SLOTS),
                                          ALU.is_ge, ALU.mult)
                        ch.link(dve.tensor_scalar(lin[g][:], rank[g][:], float(NBK * SLOTS), None, ALU.mult))
                        ch.link(dve.scalar_tensor_tensor(out=lin[g][:], in0=bucket[g][:, bass.ds(t0, U)],
                                                         scalar=float(SLOTS), in1=lin[g][:],
                                                         op0=ALU.mult, op1=ALU.add))
                        dve.wait_ge(scattered[g][half], turn * (16 * U))
                        dve.tensor_tensor(place[g][:, half, :], lin[g][:], wrap[g][:], ALU.add).then_inc(placed[g], 1)
                        dve.tensor_copy(payload[g][:, half, :, :],
                                        pair[g][:, bass.ds(t0, U), :]).then_inc(placed[g], 1)
                ch.close()
            ch = Chain(dve, chain, base=base + 4 * NG * turns)
            for g in range(NG):
                dve.wait_ge(counted[g], 2 * T + 1)
                ch.link(dve.tensor_reduce(most[:, g:g + 1], earlier[g][:, 0:NBK - 1], axis=AX.X, op=ALU.max))
            ch.link(dve.tensor_tensor(most[:, 0:1], most[:, 0:1], most[:, 1:2], ALU.max))
            ch.link(dve.tensor_scalar(k.crowded[:], most[:, 0:1], float(P * SLOTS), None, ALU.is_gt))

        @block.tensor
        def _(pe):
            for g in range(NG):
                nc.tensor.matmul(earlier[g][:, 0:NBK], k.zeros_b[:, 0:P], k.zeros_b[:], start=True, stop=True,
                                 skip_group_check=True)

            def count(g, edges, v, ready, n):
                pe.wait_ge(ready, n)
                nc.tensor.matmul(earlier[g][:, 0:NBK], edges[:], onehot[g][:, v % 2, :],
                                 start=False, stop=True, skip_group_check=True).then_inc(counted[g], 1)

            for g in range(NG):
                count(g, k.before_b, 0, hot[g], 1)
            with pe.Fori(0, turns) as turn:
                for v in range(2 * U):
                    t = turn * (2 * U) + v
                    for g in range(NG):
                        count(g, k.notbefore_b, v, ranked[g], t + 1)
                        count(g, k.before_b, v + 1, hot[g], t + 2)

        @block.gpsimd
        def _(pool):
            pool.wait_ge(filled, 16 * NG)
            with pool.Fori(0, turns) as turn:
                for half in range(2):
                    for g in range(NG):
                        pool.wait_ge(placed[g], (turn * 2 + half + 1) * 2)
                        pool.sem_inc(passed, 1)
                        for u in range(U):
                            pool.indirect_dma_start(
                                places[g], bass.IndirectOffsetOnAxis(place[g][:, half, u:u + 1], 0),
                                payload[g][:, half, u, :], None,
                                bounds_check=SP_ROWS - 1, oob_is_err=False).then_inc(scattered[g][half], 16)
            for g in range(NG):
                for half in range(2):
                    pool.wait_ge(scattered[g][half], turns * 16 * U)
                    k.pool_count[2 * g + half] += turns * 16 * U


def sort_buckets(nc, k, places, index, local):
    G, RING, AHEAD = 14, 7, 3
    with ExitStack() as ctx:
        s = Scope(nc, ctx, "sort")
        raw = s.sb("raw", [P, NBK, SLOTS, 2], I32)
        tmp_i = s.sb("tmp", [P, NBK, SLOTS], I32)
        loc = s.sb("loc", [P, NBK + AHEAD + 1, SLOTS])
        code = s.sb("code", [P, NBK, SLOTS])
        parts = s.sb("parts", [P, NBK, SLOTS, 3], BF16)
        diag = s.sb("diag", [P, RING, SLOTS, P], BF16)
        junk = s.sb("junk", [P, 2, SLOTS, SLOTS * P], BF16)
        balance = s.sb("balance", [P, G, SLOTS])
        perm = s.sb("perm", [P, 2, SLOTS, SLOTS * P], BF16)
        slot_row = s.sb("slotrow", [P, SLOTS, P], BF16)
        codes = [s.ps(f"codes{i}", [P, 512]) for i in range(RING)]
        moved = s.ps("moved", [P, 512])
        took = s.sb("took", [P, G * SLOTS, 3])
        loaded, chain = s.sem("loaded"), s.sem("chain")
        diag_ready, codes_ready = s.sem("diag_ready"), s.sem("codes_ready")
        set_up, balanced = s.sem("set_up"), s.sem("balanced")
        perm_ready, perm_used, moved_read = s.sem("perm_ready"), s.sem("perm_used"), s.sem("moved_read")
        block = ctx.enter_context(nc.Block())
        turns = NBK // G
        NG = len(places)

        @block.sync
        def _(sp):
            for g in range(NG):
                if g:
                    sp.wait_ge(set_up, g)
                sp.dma_start(raw[:].rearrange("p b j c -> p (b j c)"),
                             places[g].rearrange("(p r) c -> p (r c)", p=P)).then_inc(loaded, 16)

        @block.vector
        def _(dve):
            ch = Chain(dve, chain)
            for j in range(SLOTS):
                ch.link(dve.tensor_scalar(slot_row[:, j, :], k.ident[:], k.slot_f[:, j:j + 1], None, ALU.mult))
            base = ch.k
            for g in range(NG):
                dve.wait_ge(loaded, 16 * (g + 1))
                if g:
                    dve.wait_ge(balanced, g * (NBK + AHEAD) + RING)
                    dve.wait_ge(perm_used, g * NBK + 1)
                ch = Chain(dve, chain, base=base)
                dve.memset(loc[:, NBK:NBK + AHEAD + 1, :], 0.0)
                ch.link(dve.tensor_copy(loc[:, 0:NBK, :], raw[:, :, :, 1]))
                dve.tensor_copy(parts[:, :, :, 2], loc[:, 0:NBK, :])
                ch.link(dve.tensor_scalar(tmp_i[:], raw[:, :, :, 0], 8, None, ALU.logical_shift_right))
                ch.link(dve.tensor_copy(parts[:, :, :, 0], tmp_i[:]))
                ch.link(dve.tensor_scalar(tmp_i[:], raw[:, :, :, 0], 255, None, ALU.bitwise_and))
                ch.link(dve.tensor_copy(parts[:, :, :, 1], tmp_i[:]))
                for j in range(SLOTS):
                    last = dve.tensor_scalar(code[:, :, j], loc[:, 0:NBK, j], 256.0, k.slot_f[:, j:j + 1],
                                             ALU.mult, ALU.add)
                ch.link(last)
                dve.sem_inc(set_up, 1)
                base += ch.k
                flat_loc = loc[:].rearrange("p b j -> p (b j)")

                def diagonals(slot, column):
                    for j in range(SLOTS):
                        last = dve.tensor_scalar(diag[:, slot, j, :], k.ident_b[:],
                                                 flat_loc[:, bass.ds(column + j, 1)], None, ALU.mult)
                    last.then_inc(diag_ready, 1)

                for i in range(AHEAD + 1):
                    diagonals(i, i * SLOTS)
                with dve.Fori(0, turns) as turn:
                    ch = Chain(dve, chain, per=1, turn=turn, base=base)
                    n0 = turn * G + g * NBK
                    m0 = turn * G + g * (NBK + AHEAD)
                    for i in range(G):
                        dve.wait_ge(balanced, m0 + i + RING + 1)
                        dve.wait_ge(perm_used, n0 + i)
                        for j in range(SLOTS):
                            last = dve.tensor_scalar(perm[:, i % 2, j, :], k.balance_b[:], balance[:, i, j:j + 1],
                                                     None, ALU.is_equal)
                        last.then_inc(perm_ready, 1)
                        diagonals((i + AHEAD + 1) % RING, turn * (G * SLOTS) + (i + AHEAD + 1) * SLOTS)
                    dve.wait_ge(perm_used, n0 + G + 1)
                    ch.link(dve.tensor_copy(took[:].rearrange("p s c -> p (s c)"), moved[:, 0:G * SLOTS * 3]))
                    at = bass.ds(turn * (G * SLOTS), G * SLOTS)
                    dve.scalar_tensor_tensor(out=index[g][:, at], in0=took[:, :, 0], scalar=256.0, in1=took[:, :, 1],
                                             op0=ALU.mult, op1=ALU.add)
                    dve.tensor_copy(local[g][:, at], took[:, :, 2]).then_inc(moved_read, 1)
                    ch.close()
                base += turns

        @block.scalar
        def _(act):
            act.sem_inc(balanced, RING)
            flat_code = code[:].rearrange("p b j -> p (b j)")
            for g in range(NG):
                act.wait_ge(set_up, g + 1)
                with act.Fori(0, turns) as turn:
                    m0 = turn * G + g * (NBK + AHEAD)
                    for i in range(G):
                        act.wait_ge(codes_ready, m0 + i + 1)
                        act.wait_ge(balanced, m0 + i + RING - 1)
                        for j in range(SLOTS):
                            last = nc.scalar.activation(
                                junk[:, i % 2, j, :], codes[i % RING][:, 0:SLOTS * P], ACT.Sign,
                                bias=flat_code[:, bass.ds(turn * (G * SLOTS) + (i * SLOTS + j), 1)], scale=-1.0,
                                accum_out=balance[:, i, j:j + 1])
                        last.then_inc(balanced, 1)
                act.wait_ge(codes_ready, (g + 1) * (NBK + AHEAD))
                act.wait_ge(balanced, (g + 1) * (NBK + AHEAD) + RING - AHEAD)
                act.sem_inc(balanced, AHEAD)

        @block.tensor
        def _(pe):
            pe.sem_inc(perm_used, 1)
            for g in range(NG):
                m0 = g * (NBK + AHEAD)

                def spread(slot, m):
                    pe.wait_ge(diag_ready, m + g + 1)
                    pe.wait_ge(balanced, m + 1)
                    to = codes[slot][:, 0:SLOTS * P]
                    nc.tensor.matmul(to, k.all256_b[:], diag[:, slot, :, :], start=True, stop=False)
                    nc.tensor.matmul(to, k.ones_b[:], slot_row[:], start=False, stop=True).then_inc(codes_ready, 1)

                for i in range(AHEAD):
                    spread(i, m0 + i)
                with pe.Fori(0, turns) as turn:
                    n0 = turn * G + g * NBK
                    for i in range(G):
                        spread((i + AHEAD) % RING, turn * G + (i + AHEAD + m0))
                        pe.wait_ge(perm_ready, n0 + i + 1)
                        if i == 0:
                            pe.wait_ge(moved_read, turn + g * turns)
                        for hi in range(SLOTS):
                            c0 = (i * SLOTS + hi) * 3
                            for j in range(SLOTS):
                                last = nc.tensor.matmul(
                                    moved[:, c0:c0 + 3], perm[:, i % 2, j, hi * P:(hi + 1) * P],
                                    parts[:].rearrange("p b j c -> p (b j c)")[
                                        :, bass.ds(turn * (G * SLOTS * 3) + (i * SLOTS + j) * 3, 3)],
                                    start=(j == 0), stop=(j == SLOTS - 1))
                        last.then_inc(perm_used, 1)


class Constants:
    def __init__(self, s):
        self.pool_dma = [s.sem(f"pool_dma{i}") for i in range(4)]
        self.pool_count = [0] * 4
        self.crowded = s.sb("crowded", [P, 1], I32)
        self.ones = s.sb("ones", [P, P])
        self.ident = s.sb("ident", [P, P])
        self.tri_f = s.sb("tri", [P, P])
        self.iota_f = s.sb("iota", [P, NBK])
        self.slot_f = s.sb("slot", [P, SLOTS])
        self.iota_h = s.sb("iota_h", [P, NBK], F16)
        self.balance_b = s.sb("balance_b", [P, SLOTS * P], BF16)
        self.ident_b = s.sb("ident_b", [P, P], BF16)
        self.before_b = s.sb("before_b", [P, P], BF16)
        self.notbefore_b = s.sb("notbefore_b", [P, P], BF16)
        self.all256_b = s.sb("all256_b", [P, P], BF16)
        self.ones_b = s.sb("ones_b", [P, P], BF16)
        self.zeros_b = s.sb("zeros_b", [P, NBK], BF16)
        self.fill_i = s.sb("fill", [P, NBK * SLOTS, 2], I32)


NP = NBK * P
WCOLS = F + 2 * HEADS
EPS = 1e-5
SLOPE_ATTN = 0.2
SLOPE_ACT = 0.01
FAR = 1e30
TINY = 1e-30
TAIL = N - (NBK - BATCH) * P
TAIL_FULL = TAIL // P
TAIL_REST = TAIL % P


class Graph:

    def __init__(self, index, local):
        self.index, self.local = index, local


def load_weights(nc, k, W, al, ar, b, w_qkv, b_qkv, w_o, b_o):
    L = 3
    with ExitStack() as ctx:
        s = Scope(nc, ctx, "weights")
        a_rows = s.sb("a_rows", [P, 2, L, F])
        prod = s.sb("prod", [P, 2, F])
        rest = s.sb("rest", [1, F])
        part = s.sb("part", [1, 3, F], BF16)
        loaded, chain, moved = s.sem("loaded"), s.sem("chain"), s.sem("moved")
        split = s.sem("split")
        block = ctx.enter_context(nc.Block())

        @block.sync
        def _(sp):
            for l in range(L):
                sp.dma_start(k.w_gat[:, l, :, 0:F], W[l].rearrange("(c p) n -> p c n", p=P)).then_inc(loaded, 16)
                for i, a in enumerate((al, ar)):
                    sp.dma_start(a_rows[:, i, l, :], a[l:l + 1].rearrange("o h d -> o (h d)").to_broadcast([P, F])
                                 ).then_inc(loaded, 16)
            with nc.allow_non_contiguous_dma(reason="256 words of a bias, once"):
                sp.dma_start(k.b_col[:], b.rearrange("l (c p) -> p l c", p=P)).then_inc(loaded, 16)
            sp.dma_start(k.b2_row[:], b[2:3].to_broadcast([P, F])).then_inc(loaded, 16)
            sp.dma_start(k.w_qkv[:], w_qkv.rearrange("(c p) n -> p c n", p=P)).then_inc(loaded, 16)
            sp.dma_start(k.w_o[:], w_o.rearrange("(c p) n -> p c n", p=P)).then_inc(loaded, 16)
            sp.dma_start(k.b_qkv_row[:], b_qkv.rearrange("(o n) -> o n", o=1).to_broadcast([P, 3 * F])).then_inc(loaded, 16)
            sp.dma_start(rest[:], b_o.rearrange("(o n) -> o n", o=1)).then_inc(loaded, 16)
            sp.wait_ge(split, 1)
            for i in range(3):
                sp.dma_start(k.bias_parts[i:i + 1, :], part[:, i, :]).then_inc(moved, 16)
            sp.wait_ge(moved, 48)

        @block.vector
        def _(dve):
            dve.wait_ge(loaded, 16 * (3 * L + 6))
            ch = Chain(dve, chain)
            for l in range(L):
                for i in range(2):
                    for c in range(2):
                        ch.link(dve.tensor_tensor(prod[:, c, :], k.w_gat[:, l, c, 0:F], a_rows[:, i, l, :], ALU.mult))
                        ch.link(dve.tensor_reduce(k.w_gat[:, l, c, F + i * HEADS:F + (i + 1) * HEADS],
                                                  prod[:, c, :].rearrange("p (h d) -> p h d", h=HEADS),
                                                  axis=AX.X, op=ALU.add))
            r = rest[:]
            for i in range(3):
                ch.link(dve.tensor_copy(part[:, i, :], r))
                if i < 2:
                    ch.link(dve.tensor_tensor(r, r, part[:, i, :], ALU.subtract))
            dve.sem_inc(split, 1)


def load_nodes(sp, x, to, i, loaded, last):
    a = TAIL_FULL
    if not last:
        v = x[bass.ds(i * (BATCH * P), BATCH * P), :].rearrange("(b p) f -> p b f", p=P)
        sp.dma_start(to[:, 0:a, :], v[:, 0:a, :]).then_inc(loaded, 16)
        sp.dma_start(to[:, a:BATCH, :], v[:, a:BATCH, :]).then_inc(loaded, 16)
    else:
        n0 = (NBATCH - 1) * BATCH * P
        sp.dma_start(to[:, 0:a, :], x[n0:n0 + a * P, :].rearrange("(b p) f -> p b f", p=P)).then_inc(loaded, 16)
        sp.dma_start(to[0:TAIL_REST, a, :], x[n0 + a * P:N, :]).then_inc(loaded, 16)


RG = 4
BH = BATCH * HEADS
PAIR = SLOTS * P


class Batch:

    def __init__(self, turn, h, i=None, ring=RG, size=BATCH):
        self.turn, self.h, self.ring, self.size = turn, h, ring, size
        self.i = turn * ring + h if i is None else i
        self.s, self.q, self.round = h % ring, h % 2, turn + h // ring
        self.pairs = turn * (ring // 2) + h // 2

    def plus(self, d):
        return Batch(self.turn, self.h + d, self.i + d, self.ring, self.size)

    def n(self, b):
        return self.i * self.size + b, (self.h * self.size + b) % 2


def ahead(one, a, b, d, after):
    if b + d < a.size:
        if after >= 0:
            one(a, b + d)
    elif after >= 1:
        one(a.plus(1), b + d - a.size)


def over_batches(eng, first, batch, batches=NBATCH, ring=RG, size=BATCH):
    first()
    looped = batches // ring - 1
    with eng.Fori(0, looped) as turn, eng.register() as number:
        for h in range(ring):
            eng.reg_mov(number, turn * ring + h)
            i = eng.snap(number, min_val=0, max_val=looped * ring - 1)
            batch(Batch(turn, h, i, ring, size), ring)
    left = batches - looped * ring
    for h in range(left):
        batch(Batch(looped, h, ring=ring, size=size), left - 1 - h)


def gat_layer(nc, k, graph, table_in, layer, table_out):
    with ExitStack() as ctx:
        s = Scope(nc, ctx, f"gat{layer}")
        rows = s.sb("rows", [P, RG, BATCH, SLOTS, ROW])
        place = s.sb("place", [P, RG, BATCH * SLOTS], I32)
        onehot = s.sb("onehot", [P, 2, BATCH * SLOTS, P])
        onehot_t = s.sb("onehot_t", [P, 2, PAIR])
        er_edge = s.sb("er_edge", [P, 2, SLOTS, BH])
        logit = s.sb("logit", [P, 2, SLOTS, BH])
        key_bh = s.sb("key_bh", [P, 2, SLOTS, BH])
        key_t = s.sb("key_t", [BH, PAIR])
        wall = s.sb("wall", [BH, PAIR + 1])
        run_max = s.sb("run_max", [BH, PAIR])
        node_max = s.sb("node_max", [BH, PAIR])
        below_max = s.sb("below_max", [BH, 2, PAIR])
        total = s.sb("total", [P, 2, HEADS])
        mean = s.sb("mean", [P, 2, F])
        mean_t = s.sb("mean_t", [P, 2, 2, P])
        out_rows = s.sb("out_rows", [P, 2, BATCH, ROW])
        p_turn = s.ps("p_turn", [P, 512])
        p_er = s.ps("p_er", [P, 512])
        p_soft = s.ps("p_soft", [P, 512])
        p_sum = [s.ps(f"p_sum{i}", [P, 512]) for i in range(2)]
        p_mean = s.ps("p_mean", [P, 512])
        p_next = [s.ps(f"p_next{i}", [P, 512]) for i in range(2)]
        (placed, hot, hot_turned, hot_copied, er_made, er_taken, keyed, keys_turned, keys_copied, logits, soft_turned, below, soft_back, weights,
         messages, summed, averaged, mean_turned, mean_copied, product, row_done, chain_logit, chain_soft,
         chain_mean, passed, passed_pe, shifted) = (s.sem(n) for n in (
             "placed", "hot", "hot_turned", "hot_copied", "er_made", "er_taken", "keyed", "keys_turned", "keys_copied", "logits", "soft_turned", "below",
             "soft_back", "weights", "messages", "summed", "averaged", "mean_turned", "mean_copied", "product",
             "row_done", "chain_logit", "chain_soft", "chain_mean", "passed", "passed_pe", "shifted"))
        gathered, before = k.pool_dma[0:RG], k.pool_count[0:RG]
        stored = [s.sem(f"stored{i}") for i in range(2)]
        walls_set = s.sem("walls_set")
        rows_clear = s.sem("rows_clear")
        AHEAD = RG * BATCH
        block = ctx.enter_context(nc.Block())
        turns = NBATCH // RG
        flat_local = graph.local[:].rearrange("p (b j) -> p b j", j=SLOTS)

        @block.gpsimd
        def _(pool):
            pool.wait_ge(rows_clear, 1)

            def gather(a):
                pool.wait_ge(placed, a.i + 1)
                for b in range(BATCH):
                    pool.wait_ge(averaged, a.n(b)[0] + 1)
                    pool.sem_inc(passed, 1)
                    for j in range(SLOTS):
                        c = b * SLOTS + j
                        pool.indirect_dma_start(rows[:, a.s, b, j, :], None, table_in,
                                                bass.IndirectOffsetOnAxis(place[:, a.s, c:c + 1], 0),
                                                bounds_check=N - 1, oob_is_err=False).then_inc(gathered[a.s], 16)

            with pool.Fori(0, turns) as turn:
                for h in range(RG):
                    gather(Batch(turn, h))
            for h in range(RG):
                k.pool_count[h] += turns * 16 * BATCH * SLOTS

        @block.sync
        def _(sp):
            with sp.Fori(0, turns) as turn:
                for h in range(RG):
                    a = Batch(turn, h)
                    sp.wait_ge(row_done, (a.i + 1) * BATCH + 1)
                    sp.dma_start(table_out[bass.ds(a.i * (BATCH * P), BATCH * P), :].rearrange("(b p) f -> p b f", p=P),
                                 out_rows[:, a.q]).then_inc(stored[a.q], 16)
            for q in range(2):
                sp.wait_ge(stored[q], 16 * (NBATCH // 2))

        @block.vector
        def _(dve):
            def make_place(a):
                dve.wait_ge(gathered[a.s], a.round * (16 * BATCH * SLOTS) + before[a.s])
                dve.tensor_copy(place[:, a.s, :], graph.index[:, bass.ds(a.i * (BATCH * SLOTS), BATCH * SLOTS)]
                                ).then_inc(placed, 1)

            def make_onehot(a, b):
                node = graph.local[:, bass.ds((a.i * BATCH + b) * SLOTS, SLOTS)]
                dve.tensor_tensor(onehot[:, a.q, b * SLOTS:(b + 1) * SLOTS, :],
                                  k.iota_f[:, 0:P].unsqueeze(1).to_broadcast([P, SLOTS, P]),
                                  node.unsqueeze(2).to_broadcast([P, SLOTS, P]), ALU.is_equal).then_inc(hot, 1)

            def take_er(a):
                dve.wait_ge(er_made, (a.i + 1) * BATCH + 1)
                dve.tensor_copy(er_edge[:, a.q].rearrange("p j c -> p (j c)"), p_er[:, 0:SLOTS * BH]).then_inc(er_taken, 1)

            def copy_keys(a):
                for j in range(SLOTS):
                    last = dve.tensor_copy(
                        key_bh[:, a.q, j, :].rearrange("p (b h) -> p b h", h=HEADS),
                        flat_local[:, bass.ds(a.i * BATCH, BATCH), j:j + 1].to_broadcast([P, BATCH, HEADS]))
                last.then_inc(keyed, 1)

            def add_logits(a):
                dve.wait_ge(gathered[a.s], (a.round + 1) * (16 * BATCH * SLOTS) + before[a.s])
                dve.wait_ge(er_taken, a.i + 1)
                for j in range(SLOTS):
                    last = dve.tensor_tensor(logit[:, a.q, j, :].rearrange("p (b h) -> p b h", h=HEADS),
                                             rows[:, a.s, :, j, F:ROW],
                                             er_edge[:, a.q, j, :].rearrange("p (b h) -> p b h", h=HEADS), ALU.add)
                last.then_inc(chain_logit, 1)

            def leak_logits(a):
                dve.wait_ge(chain_logit, a.i + 1)
                dve.scalar_tensor_tensor(out=logit[:, a.q], in0=logit[:, a.q], scalar=SLOPE_ATTN, in1=logit[:, a.q],
                                         op0=ALU.mult, op1=ALU.max).then_inc(logits, 1)

            def take_keys(a):
                dve.wait_ge(keys_turned, a.i + 1)
                dve.tensor_copy(key_t[:], p_soft[0:BH, PAIR:2 * PAIR]).then_inc(keys_copied, 1)

            def compare_keys(a):
                dve.wait_ge(keys_copied, a.i + 1)
                dve.tensor_tensor(wall[:, 1:PAIR], key_t[:, 1:PAIR], key_t[:, 0:PAIR - 1],
                                  ALU.is_equal).then_inc(chain_soft, 1)

            def set_walls(a):
                dve.wait_ge(chain_soft, a.i * SOFT + 1)
                dve.tensor_scalar(wall[:, 1:PAIR], wall[:, 1:PAIR], 1.0, FAR, ALU.subtract,
                                  ALU.mult).then_inc(chain_soft, 1)

            def scan_forward(a):
                dve.wait_ge(soft_turned, a.i + 1)
                dve.wait_ge(chain_soft, a.i * SOFT + 2)
                dve.tensor_tensor_scan(run_max[:], wall[:, 0:PAIR], p_soft[0:BH, 0:PAIR], 0.0,
                                       ALU.add, ALU.max).then_inc(chain_soft, 1)

            def scan_back(a):
                dve.wait_ge(chain_soft, a.i * SOFT + 3)
                dve.tensor_tensor_scan(node_max[:, ::-1], wall[:, PAIR:0:-1], run_max[:, ::-1], 0.0,
                                       ALU.add, ALU.max).then_inc(chain_soft, 1)

            def subtract_max(a):
                dve.wait_ge(chain_soft, a.i * SOFT + 4)
                dve.tensor_tensor(below_max[:, a.q], p_soft[0:BH, 0:PAIR], node_max[:], ALU.subtract).then_inc(below, 1)

            def weigh(a, b):
                if b == 0:
                    dve.wait_ge(weights, a.i + 1)
                v = rows[:, a.s, b, :, 0:F].rearrange("p j (h d) -> p j h d", h=HEADS)
                w = rows[:, a.s, b, :, F:ROW]
                dve.tensor_tensor(v, v, w.unsqueeze(3).to_broadcast([P, SLOTS, HEADS, HD]), ALU.mult).then_inc(messages, 1)

            def take_total(a, b):
                n, q = a.n(b)
                dve.wait_ge(summed, n + 1)
                dve.tensor_scalar(total[:, q], p_sum[q][:, F:ROW], TINY, None, ALU.max).then_inc(chain_mean, 1)

            def invert_total(a, b):
                n, q = a.n(b)
                dve.wait_ge(chain_mean, n * 2 + 1)
                dve.reciprocal(total[:, q], total[:, q]).then_inc(chain_mean, 1)

            def divide(a, b):
                n, q = a.n(b)
                dve.wait_ge(chain_mean, n * 2 + 2)
                dve.wait_ge(mean_turned, n)
                dve.tensor_tensor(mean[:, q].rearrange("p (h d) -> p h d", h=HEADS),
                                  p_sum[q][:, 0:F].rearrange("p (h d) -> p h d", h=HEADS),
                                  total[:, q].unsqueeze(2).to_broadcast([P, HEADS, HD]), ALU.mult).then_inc(averaged, 1)

            def leak(a, b):
                n, q = a.n(b)
                dve.wait_ge(shifted, n + 1)
                v = mean_t[:, q].rearrange("p c n -> p (c n)")
                dve.scalar_tensor_tensor(out=v, in0=v, scalar=SLOPE_ACT, in1=v,
                                         op0=ALU.mult, op1=ALU.max).then_inc(mean_copied, 1)

            SOFT = 4

            def first():
                dve.memset(rows[:], 0.0).then_inc(rows_clear, 1)
                dve.wait_ge(rows_clear, 1)
                dve.memset(wall[:, 0:1], -FAR).then_inc(walls_set, 1)
                dve.memset(wall[:, PAIR:PAIR + 1], -FAR).then_inc(walls_set, 1)
                dve.wait_ge(walls_set, 2)
                dve.sem_inc(averaged, AHEAD)
                for h in range(RG):
                    make_place(Batch(0, h))
                for h in range(2):
                    for b in range(BATCH):
                        make_onehot(Batch(0, h), b)
                    copy_keys(Batch(0, h))
                a = Batch(0, 0)
                take_er(a)
                add_logits(a)
                leak_logits(a)
                take_keys(a)
                compare_keys(a)
                set_walls(a)
                scan_forward(a)
                scan_back(a)
                subtract_max(a)
                for b in range(2):
                    weigh(a, b)
                take_total(a, 0)
                invert_total(a, 0)
                divide(a, 0)
                make_onehot(a.plus(2), 0)

            def batch(a, after):
                for b in range(BATCH):
                    if b == 0 and after >= RG:
                        make_place(a.plus(RG))
                    ahead(weigh, a, b, 2, after)
                    ahead(take_total, a, b, 1, after)
                    if b == 0 and after >= 1:
                        take_er(a.plus(1))
                    if b == 1 and after >= 1:
                        take_keys(a.plus(1))
                    if b == 3 and after >= 1:
                        scan_forward(a.plus(1))
                    ahead(make_onehot, a.plus(2), b, 1, after - 2)
                    ahead(invert_total, a, b, 1, after)
                    if b == 1 and after >= 1:
                        compare_keys(a.plus(1))
                    if b == 0 and after >= 1:
                        add_logits(a.plus(1))
                    if b == 3 and after >= 1:
                        scan_back(a.plus(1))
                    ahead(divide, a, b, 1, after)
                    if b == 0 and after >= 1:
                        leak_logits(a.plus(1))
                    if b == 1 and after >= 1:
                        set_walls(a.plus(1))
                    if b == 3 and after >= 1:
                        subtract_max(a.plus(1))
                    if b == BATCH - 1 and after >= 2:
                        copy_keys(a.plus(2))
                    leak(a, b)

            over_batches(dve, first, batch)

        @block.tensor
        def _(pe):
            def turn_onehot(a, b):
                n, q = a.n(b)
                pe.wait_ge(hot, n + 1)
                pe.wait_ge(hot_copied, n)
                for j in range(SLOTS):
                    last = nc.tensor.transpose(p_turn[:, j * P:(j + 1) * P], onehot[:, a.q, b * SLOTS + j, :], k.ident[:])
                last.then_inc(hot_turned, 1)

            def make_er(a, b):
                n, q = a.n(b)
                pe.wait_ge(hot_copied, n + 1)
                if b == 0:
                    pe.wait_ge(er_taken, a.i)
                for j in range(SLOTS):
                    c = j * BH + b * HEADS
                    last = nc.tensor.matmul(p_er[:, c:c + HEADS], onehot_t[:, q, j * P:(j + 1) * P],
                                            k.er[:, bass.ds(n * HEADS, HEADS)], start=True, stop=True)
                last.then_inc(er_made, 1)

            def turn_keys(a):
                pe.wait_ge(keyed, a.i + 1)
                pe.wait_ge(weights, a.i)
                pe.sem_inc(passed_pe, 1)
                for j in range(SLOTS):
                    last = nc.tensor.transpose(p_soft[0:BH, PAIR + j * P:PAIR + (j + 1) * P], key_bh[:, a.q, j, :], k.ident[:])
                last.then_inc(keys_turned, 1)

            def turn_logits(a):
                pe.wait_ge(logits, a.i + 1)
                pe.wait_ge(keys_copied, a.i + 1)
                pe.sem_inc(passed_pe, 1)
                for j in range(SLOTS):
                    last = nc.tensor.transpose(p_soft[0:BH, j * P:(j + 1) * P], logit[:, a.q, j, :], k.ident[:])
                last.then_inc(soft_turned, 1)

            def turn_back(a):
                pe.wait_ge(below, a.i + 1)
                pe.sem_inc(passed_pe, 1)
                for j in range(SLOTS):
                    last = nc.tensor.transpose(p_soft[:, j * BH:(j + 1) * BH], below_max[:, a.q, j * P:(j + 1) * P],
                                               k.ident[0:BH, 0:BH])
                last.then_inc(soft_back, 1)

            def add_up(a, b):
                n, q = a.n(b)
                pe.wait_ge(messages, n + 1)
                pe.wait_ge(averaged, n + (AHEAD - 1))
                for j in range(SLOTS):
                    last = nc.tensor.matmul(p_sum[q][:, 0:ROW], onehot[:, a.q, b * SLOTS + j, :], rows[:, a.s, b, j, :],
                                            start=(j == 0), stop=(j == SLOTS - 1))
                last.then_inc(summed, 1)

            def turn_mean(a, b):
                n, q = a.n(b)
                pe.wait_ge(averaged, n + (AHEAD + 1))
                pe.wait_ge(shifted, n)
                for c in range(2):
                    last = nc.tensor.transpose(p_mean[:, c * P:(c + 1) * P], mean[:, q, c * P:(c + 1) * P], k.ident[:])
                last.then_inc(mean_turned, 1)

            def multiply(a, b):
                n, q = a.n(b)
                pe.wait_ge(mean_copied, n + 1)
                pe.wait_ge(row_done, n)
                for c in range(2):
                    last = nc.tensor.matmul(p_next[q][:, 0:WCOLS], mean_t[:, q, c, :], k.w_gat[:, layer + 1, c, :],
                                            start=(c == 0), stop=(c == 1))
                last.then_inc(product, 1)

            def first():
                for x in (mean_turned, product, er_made):
                    pe.sem_inc(x, 1)
                for h in range(2):
                    for b in range(BATCH + 1):
                        if b:
                            make_er(Batch(0, h), b - 1)
                        if b < BATCH:
                            turn_onehot(Batch(0, h), b)
                turn_keys(Batch(0, 0))
                turn_logits(Batch(0, 0))
                a = Batch(0, 0)
                turn_back(a)
                for b in range(2):
                    add_up(a, b)
                turn_onehot(a.plus(2), 0)
                turn_mean(a, 0)

            def batch(a, after):
                for b in range(BATCH):
                    ahead(add_up, a, b, 2, after)
                    if b == 0 and after >= 1:
                        turn_keys(a.plus(1))
                    if b == 2 and after >= 1:
                        turn_logits(a.plus(1))
                    if b == 4 and after >= 1:
                        turn_back(a.plus(1))
                    if after >= 2:
                        make_er(a.plus(2), b)
                    ahead(turn_onehot, a.plus(2), b, 1, after - 2)
                    ahead(turn_mean, a, b, 1, after)
                    multiply(a, b)

            over_batches(pe, first, batch)

        @block.scalar
        def _(act):
            def copy_onehot(a, b):
                n, q = a.n(b)
                act.wait_ge(hot_turned, n + 1)
                act.wait_ge(er_made, n)
                nc.scalar.copy(onehot_t[:, q, :], p_turn[:, 0:PAIR]).then_inc(hot_copied, 1)

            def exponentiate(a):
                act.wait_ge(soft_back, a.i + 1)
                for j in range(SLOTS):
                    last = nc.scalar.activation(
                        rows[:, a.s, :, j, F:ROW],
                        p_soft[:, j * BH:(j + 1) * BH].rearrange("p (b h) -> p b h", h=HEADS), ACT.Exp)
                last.then_inc(weights, 1)

            def activate(a, b):
                n, q = a.n(b)
                act.wait_ge(mean_turned, n + 2)
                act.wait_ge(product, n)
                for c in range(2):
                    last = nc.scalar.activation(mean_t[:, q, c, :], p_mean[:, c * P:(c + 1) * P], ACT.Identity,
                                                bias=k.b_col[:, layer, c:c + 1])
                last.then_inc(shifted, 1)

            def finish(a, b):
                n, q = a.n(b)
                act.wait_ge(product, n + 2)
                if b == 0:
                    act.wait_ge(stored[a.q], a.pairs * 16)
                nc.scalar.copy(out_rows[:, a.q, b, :], p_next[q][:, 0:ROW])
                nc.scalar.copy(k.er[:, bass.ds(n * HEADS, HEADS)], p_next[q][:, ROW:WCOLS]).then_inc(row_done, 1)

            def first():
                act.sem_inc(row_done, 1)
                for h in range(2):
                    for b in range(BATCH):
                        copy_onehot(Batch(0, h), b)
                exponentiate(Batch(0, 0))
                copy_onehot(Batch(0, 2), 0)
                activate(Batch(0, 0), 0)

            def batch(a, after):
                for b in range(BATCH):
                    if b == 4 and after >= 1:
                        exponentiate(a.plus(1))
                    ahead(copy_onehot, a.plus(2), b, 1, after - 2)
                    ahead(activate, a, b, 1, after)
                    finish(a, b)

            over_batches(act, first, batch)


def last_gat_layer(nc, k, graph, table_in, x, x_out):
    with ExitStack() as ctx:
        s = Scope(nc, ctx, "gat2")
        rows = s.sb("rows", [P, RG, BATCH, SLOTS, ROW])
        place = s.sb("place", [P, RG, BATCH * SLOTS], I32)
        onehot = s.sb("onehot", [P, 2, BATCH * SLOTS, P])
        apart = s.sb("apart", [P, 2, PAIR])
        onehot_t = s.sb("onehot_t", [P, 2, PAIR])
        er_edge = s.sb("er_edge", [P, 2, SLOTS, BH])
        logit = s.sb("logit", [P, 2, SLOTS, BH])
        key_bh = s.sb("key_bh", [P, 2, SLOTS, BH])
        key_t = s.sb("key_t", [BH, PAIR])
        wall = s.sb("wall", [BH, PAIR + 1])
        run_max = s.sb("run_max", [BH, PAIR])
        node_max = s.sb("node_max", [BH, PAIR])
        below_max = s.sb("below_max", [BH, 2, PAIR])
        total = s.sb("total", [P, 2, HEADS])
        mean = s.sb("mean", [P, 2, F])
        x_rows = s.sb("x_rows", [P, 2, BATCH, F])
        p_turn = s.ps("p_turn", [P, 512])
        p_er = s.ps("p_er", [P, 512])
        p_soft = s.ps("p_soft", [P, 512])
        p_sum = [s.ps(f"p_sum{i}", [P, 512]) for i in range(2)]
        (placed, chain_hot, hot, hot_turned, hot_copied, er_made, er_taken, keyed, keys_turned, keys_copied, logits, soft_turned, below, soft_back, weights,
         messages, summed, averaged, row_done, chain_logit, chain_soft,
         chain_mean, passed, passed_pe, biased) = (s.sem(n) for n in (
             "placed", "chain_hot", "hot", "hot_turned", "hot_copied", "er_made", "er_taken", "keyed", "keys_turned", "keys_copied", "logits", "soft_turned", "below",
             "soft_back", "weights", "messages", "summed", "averaged", "row_done",
             "chain_logit", "chain_soft", "chain_mean", "passed", "passed_pe", "biased"))
        gathered, before = k.pool_dma[0:RG], k.pool_count[0:RG]
        loaded = [s.sem(f"loaded{i}") for i in range(2)]
        stored = [s.sem(f"stored{i}") for i in range(2)]
        walls_set = s.sem("walls_set")
        rows_clear = s.sem("rows_clear")
        AHEAD = RG * BATCH
        KEPT = 2 * BATCH
        block = ctx.enter_context(nc.Block())
        turns = NBATCH // RG
        flat_local = graph.local[:].rearrange("p (b j) -> p b j", j=SLOTS)

        @block.gpsimd
        def _(pool):
            pool.wait_ge(rows_clear, 1)

            def gather(a):
                pool.wait_ge(placed, a.i + 1)
                for b in range(BATCH):
                    pool.wait_ge(averaged, a.n(b)[0] + 1)
                    pool.sem_inc(passed, 1)
                    for j in range(SLOTS):
                        c = b * SLOTS + j
                        pool.indirect_dma_start(rows[:, a.s, b, j, :], None, table_in,
                                                bass.IndirectOffsetOnAxis(place[:, a.s, c:c + 1], 0),
                                                bounds_check=N - 1, oob_is_err=False).then_inc(gathered[a.s], 16)

            with pool.Fori(0, turns) as turn:
                for h in range(RG):
                    gather(Batch(turn, h))
            for h in range(RG):
                k.pool_count[h] += turns * 16 * BATCH * SLOTS

        @block.sync
        def _(sp):
            sp.wait_ge(rows_clear, 1)

            def load(a, last):
                sp.wait_ge(stored[a.q], a.pairs * 16)
                load_nodes(sp, x, x_rows[:, a.q], a.i, loaded[a.q], last)

            def store(a):
                sp.wait_ge(row_done, (a.i + 1) * BATCH)
                sp.dma_start(x_out[bass.ds(a.i * (BATCH * P), BATCH * P), :].rearrange("(b p) f -> p b f", p=P),
                             x_rows[:, a.q]).then_inc(stored[a.q], 16)

            load(Batch(0, 0), False)
            with sp.Fori(0, turns - 1) as turn:
                for h in range(RG):
                    load(Batch(turn, h + 1), False)
                    store(Batch(turn, h))
            for h in range(RG):
                if h + 1 < RG:
                    load(Batch(turns - 1, h + 1), h + 1 == RG - 1)
                store(Batch(turns - 1, h))
            for q in range(2):
                sp.wait_ge(stored[q], 16 * (NBATCH // 2))

        @block.vector
        def _(dve):
            def make_place(a):
                dve.wait_ge(gathered[a.s], a.round * (16 * BATCH * SLOTS) + before[a.s])
                dve.tensor_copy(place[:, a.s, :], graph.index[:, bass.ds(a.i * (BATCH * SLOTS), BATCH * SLOTS)]
                                ).then_inc(placed, 1)

            def take_er(a):
                dve.wait_ge(er_made, (a.i + 1) * BATCH + 1)
                dve.tensor_copy(er_edge[:, a.q].rearrange("p j c -> p (j c)"), p_er[:, 0:SLOTS * BH]).then_inc(er_taken, 1)

            def copy_keys(a):
                for j in range(SLOTS):
                    last = dve.tensor_copy(
                        key_bh[:, a.q, j, :].rearrange("p (b h) -> p b h", h=HEADS),
                        flat_local[:, bass.ds(a.i * BATCH, BATCH), j:j + 1].to_broadcast([P, BATCH, HEADS]))
                last.then_inc(keyed, 1)

            def add_logits(a):
                dve.wait_ge(gathered[a.s], (a.round + 1) * (16 * BATCH * SLOTS) + before[a.s])
                dve.wait_ge(er_taken, a.i + 1)
                for j in range(SLOTS):
                    last = dve.tensor_tensor(logit[:, a.q, j, :].rearrange("p (b h) -> p b h", h=HEADS),
                                             rows[:, a.s, :, j, F:ROW],
                                             er_edge[:, a.q, j, :].rearrange("p (b h) -> p b h", h=HEADS), ALU.add)
                last.then_inc(chain_logit, 1)

            def leak_logits(a):
                dve.wait_ge(chain_logit, a.i + 1)
                dve.scalar_tensor_tensor(out=logit[:, a.q], in0=logit[:, a.q], scalar=SLOPE_ATTN, in1=logit[:, a.q],
                                         op0=ALU.mult, op1=ALU.max).then_inc(logits, 1)

            def take_keys(a):
                dve.wait_ge(keys_turned, a.i + 1)
                dve.tensor_copy(key_t[:], p_soft[0:BH, PAIR:2 * PAIR]).then_inc(keys_copied, 1)

            def compare_keys(a):
                dve.wait_ge(keys_copied, a.i + 1)
                dve.tensor_tensor(wall[:, 1:PAIR], key_t[:, 1:PAIR], key_t[:, 0:PAIR - 1],
                                  ALU.is_equal).then_inc(chain_soft, 1)

            def set_walls(a):
                dve.wait_ge(chain_soft, a.i * SOFT + 1)
                dve.tensor_scalar(wall[:, 1:PAIR], wall[:, 1:PAIR], 1.0, FAR, ALU.subtract,
                                  ALU.mult).then_inc(chain_soft, 1)

            def scan_forward(a):
                dve.wait_ge(soft_turned, a.i + 1)
                dve.wait_ge(chain_soft, a.i * SOFT + 2)
                dve.tensor_tensor_scan(run_max[:], wall[:, 0:PAIR], p_soft[0:BH, 0:PAIR], 0.0,
                                       ALU.add, ALU.max).then_inc(chain_soft, 1)

            def scan_back(a):
                dve.wait_ge(chain_soft, a.i * SOFT + 3)
                dve.tensor_tensor_scan(node_max[:, ::-1], wall[:, PAIR:0:-1], run_max[:, ::-1], 0.0,
                                       ALU.add, ALU.max).then_inc(chain_soft, 1)

            def subtract_max(a):
                dve.wait_ge(chain_soft, a.i * SOFT + 4)
                dve.tensor_tensor(below_max[:, a.q], p_soft[0:BH, 0:PAIR], node_max[:], ALU.subtract).then_inc(below, 1)

            def weigh(a, b):
                if b == 0:
                    dve.wait_ge(weights, a.i + 1)
                v = rows[:, a.s, b, :, 0:F].rearrange("p j (h d) -> p j h d", h=HEADS)
                w = rows[:, a.s, b, :, F:ROW]
                dve.tensor_tensor(v, v, w.unsqueeze(3).to_broadcast([P, SLOTS, HEADS, HD]), ALU.mult).then_inc(messages, 1)

            def take_total(a, b):
                n, q = a.n(b)
                dve.wait_ge(summed, n + (KEPT + 1))
                dve.tensor_scalar(total[:, q], p_sum[q][:, F:ROW], TINY, None, ALU.max).then_inc(chain_mean, 1)

            def invert_total(a, b):
                n, q = a.n(b)
                dve.wait_ge(chain_mean, n * 2 + 1)
                dve.reciprocal(total[:, q], total[:, q]).then_inc(chain_mean, 1)

            def divide(a, b):
                n, q = a.n(b)
                dve.wait_ge(chain_mean, n * 2 + 2)
                dve.tensor_tensor(mean[:, q].rearrange("p (h d) -> p h d", h=HEADS),
                                  p_sum[q][:, 0:F].rearrange("p (h d) -> p h d", h=HEADS),
                                  total[:, q].unsqueeze(2).to_broadcast([P, HEADS, HD]), ALU.mult).then_inc(averaged, 1)

            def add_bias(a, b):
                if b == 0:
                    dve.wait_ge(loaded[a.q], (a.pairs + 1) * 32)
                v = x_rows[:, a.q, b, :]
                dve.tensor_tensor(v, v, k.b2_row[:], ALU.add).then_inc(biased, 1)

            def finish(a, b):
                n, q = a.n(b)
                dve.wait_ge(averaged, n + (AHEAD + 1))
                dve.wait_ge(biased, n + 1)
                v = x_rows[:, a.q, b, :]
                dve.tensor_tensor(v, v, mean[:, q], ALU.add).then_inc(row_done, 1)

            SOFT = 4

            def first():
                dve.memset(x_rows[:], 0.0)
                dve.memset(rows[:], 0.0).then_inc(rows_clear, 1)
                dve.wait_ge(rows_clear, 1)
                dve.memset(wall[:, 0:1], -FAR).then_inc(walls_set, 1)
                dve.memset(wall[:, PAIR:PAIR + 1], -FAR).then_inc(walls_set, 1)
                dve.wait_ge(walls_set, 2)
                dve.sem_inc(averaged, AHEAD)
                for h in range(RG):
                    make_place(Batch(0, h))
                for h in range(2):
                    copy_keys(Batch(0, h))
                a = Batch(0, 0)
                take_er(a)
                add_logits(a)
                leak_logits(a)
                take_keys(a)
                compare_keys(a)
                set_walls(a)
                scan_forward(a)
                scan_back(a)
                subtract_max(a)
                for b in range(2):
                    weigh(a, b)
                take_total(a, 0)
                invert_total(a, 0)
                divide(a, 0)
                add_bias(a, 0)

            def batch(a, after):
                for b in range(BATCH):
                    if b == 0 and after >= RG:
                        make_place(a.plus(RG))
                    ahead(weigh, a, b, 2, after)
                    ahead(take_total, a, b, 1, after)
                    if b == 0 and after >= 1:
                        take_er(a.plus(1))
                    if b == 1 and after >= 1:
                        take_keys(a.plus(1))
                    if b == 3 and after >= 1:
                        scan_forward(a.plus(1))
                    ahead(add_bias, a, b, 1, after)
                    ahead(invert_total, a, b, 1, after)
                    if b == 1 and after >= 1:
                        compare_keys(a.plus(1))
                    if b == 0 and after >= 1:
                        add_logits(a.plus(1))
                    if b == 3 and after >= 1:
                        scan_back(a.plus(1))
                    finish(a, b)
                    ahead(divide, a, b, 1, after)
                    if b == 0 and after >= 1:
                        leak_logits(a.plus(1))
                    if b == 1 and after >= 1:
                        set_walls(a.plus(1))
                    if b == 3 and after >= 1:
                        subtract_max(a.plus(1))
                    if b == BATCH - 1 and after >= 2:
                        copy_keys(a.plus(2))

            over_batches(dve, first, batch)

        @block.tensor
        def _(pe):
            def turn_onehot(a, b):
                n, q = a.n(b)
                pe.wait_ge(hot, n + 1)
                pe.wait_ge(hot_copied, n)
                for j in range(SLOTS):
                    last = nc.tensor.transpose(p_turn[:, j * P:(j + 1) * P], onehot[:, a.q, b * SLOTS + j, :], k.ident[:])
                last.then_inc(hot_turned, 1)

            def make_er(a, b):
                n, q = a.n(b)
                pe.wait_ge(hot_copied, n + 1)
                if b == 0:
                    pe.wait_ge(er_taken, a.i)
                for j in range(SLOTS):
                    c = j * BH + b * HEADS
                    last = nc.tensor.matmul(p_er[:, c:c + HEADS], onehot_t[:, q, j * P:(j + 1) * P],
                                            k.er[:, bass.ds(n * HEADS, HEADS)], start=True, stop=True)
                last.then_inc(er_made, 1)

            def turn_keys(a):
                pe.wait_ge(keyed, a.i + 1)
                pe.wait_ge(weights, a.i)
                pe.sem_inc(passed_pe, 1)
                for j in range(SLOTS):
                    last = nc.tensor.transpose(p_soft[0:BH, PAIR + j * P:PAIR + (j + 1) * P], key_bh[:, a.q, j, :], k.ident[:])
                last.then_inc(keys_turned, 1)

            def turn_logits(a):
                pe.wait_ge(logits, a.i + 1)
                pe.wait_ge(keys_copied, a.i + 1)
                pe.sem_inc(passed_pe, 1)
                for j in range(SLOTS):
                    last = nc.tensor.transpose(p_soft[0:BH, j * P:(j + 1) * P], logit[:, a.q, j, :], k.ident[:])
                last.then_inc(soft_turned, 1)

            def turn_back(a):
                pe.wait_ge(below, a.i + 1)
                pe.sem_inc(passed_pe, 1)
                for j in range(SLOTS):
                    last = nc.tensor.transpose(p_soft[:, j * BH:(j + 1) * BH], below_max[:, a.q, j * P:(j + 1) * P],
                                               k.ident[0:BH, 0:BH])
                last.then_inc(soft_back, 1)

            def add_up(a, b):
                n, q = a.n(b)
                pe.wait_ge(messages, n + 1)
                pe.wait_ge(averaged, n + (AHEAD - 1))
                for j in range(SLOTS):
                    last = nc.tensor.matmul(p_sum[q][:, 0:ROW], onehot[:, a.q, b * SLOTS + j, :], rows[:, a.s, b, j, :],
                                            start=(j == 0), stop=(j == SLOTS - 1))
                last.then_inc(summed, 1)

            def first():
                pe.sem_inc(summed, KEPT)
                pe.sem_inc(er_made, 1)
                for h in range(2):
                    for b in range(BATCH + 1):
                        if b:
                            make_er(Batch(0, h), b - 1)
                        if b < BATCH:
                            turn_onehot(Batch(0, h), b)
                turn_keys(Batch(0, 0))
                turn_logits(Batch(0, 0))
                a = Batch(0, 0)
                turn_back(a)
                for b in range(2):
                    add_up(a, b)
                turn_onehot(a.plus(2), 0)

            def batch(a, after):
                for b in range(BATCH):
                    ahead(add_up, a, b, 2, after)
                    if b == 0 and after >= 1:
                        turn_keys(a.plus(1))
                    if b == 2 and after >= 1:
                        turn_logits(a.plus(1))
                    if b == 4 and after >= 1:
                        turn_back(a.plus(1))
                    if after >= 2:
                        make_er(a.plus(2), b)
                    ahead(turn_onehot, a.plus(2), b, 1, after - 2)

            over_batches(pe, first, batch)

        @block.scalar
        def _(act):
            def compare(a, b):
                n, q = a.n(b)
                for j in range(SLOTS):
                    last = nc.scalar.activation(apart[:, q, j * P:(j + 1) * P], k.iota_f[:, 0:P], ACT.Abs,
                                                bias=graph.local[:, bass.ds((a.i * BATCH + b) * SLOTS + j, 1)], scale=-1.0)
                last.then_inc(chain_hot, 1)

            def make_onehot(a, b):
                n, q = a.n(b)
                act.wait_ge(chain_hot, n + 1)
                act.wait_ge(summed, n + 1)
                nc.scalar.activation(onehot[:, a.q, b * SLOTS:(b + 1) * SLOTS, :].rearrange("p j n -> p (j n)"),
                                     apart[:, q, :], ACT.Relu, bias=k.ones[:, 0:1], scale=-1.0).then_inc(hot, 1)

            def copy_onehot(a, b):
                n, q = a.n(b)
                act.wait_ge(hot_turned, n + 1)
                act.wait_ge(er_made, n)
                nc.scalar.copy(onehot_t[:, q, :], p_turn[:, 0:PAIR]).then_inc(hot_copied, 1)

            def exponentiate(a):
                act.wait_ge(soft_back, a.i + 1)
                for j in range(SLOTS):
                    last = nc.scalar.activation(
                        rows[:, a.s, :, j, F:ROW],
                        p_soft[:, j * BH:(j + 1) * BH].rearrange("p (b h) -> p b h", h=HEADS), ACT.Exp)
                last.then_inc(weights, 1)

            def first():
                for h in range(2):
                    for b in range(BATCH):
                        compare(Batch(0, h), b)
                        make_onehot(Batch(0, h), b)
                        copy_onehot(Batch(0, h), b)
                exponentiate(Batch(0, 0))
                compare(Batch(0, 2), 0)
                make_onehot(Batch(0, 2), 0)
                copy_onehot(Batch(0, 2), 0)
                compare(Batch(0, 2), 1)

            def batch(a, after):
                for b in range(BATCH):
                    if b == 4 and after >= 1:
                        exponentiate(a.plus(1))
                    ahead(compare, a.plus(2), b, 2, after - 2)
                    ahead(make_onehot, a.plus(2), b, 1, after - 2)
                    ahead(copy_onehot, a.plus(2), b, 1, after - 2)

            over_batches(act, first, batch)


RP = 4


def project(nc, k, tag, x, parts, er=None):
    padded = x.shape[0] == NP
    two = len(parts) > 1
    products = 2 if two else RP
    with ExitStack() as ctx:
        s = Scope(nc, ctx, tag)
        xin = s.sb("xin", [P, RP, BATCH, F])
        stats = s.sb("stats", [P, RP, BATCH, 6])
        mv = s.sb("mv", [P, RP, BATCH, 2])
        rstd = s.sb("rstd", [P, RP, BATCH])
        shift = s.sb("shift", [P, RP, BATCH])
        hidden = s.sb("hidden", [P, RP, F])
        hidden_t = s.sb("hidden_t", [P, RP, 2, P])
        rows = [s.sb(f"rows{m}", [P, 2, BATCH, part[1]]) for m, part in enumerate(parts)]
        turned = [s.ps(f"turned{i}", [P, 512]) for i in range(RP)]
        product = [[s.ps(f"product{m}{i}", [P, 512]) for i in range(products)] for m in range(len(parts))]
        (zeroed, passed, chain, chain_scale, variances, roots, scaled, hid, hid_turned, copied, multiplied, taken) = (
            s.sem(n) for n in (
                "zeroed", "passed", "chain", "chain_scale", "variances", "roots", "scaled", "hidden_ready",
                "hidden_turned", "copied", "multiplied", "taken"))
        loaded = [s.sem(f"loaded{i}") for i in range(RP)]
        stored = [s.sem(f"stored{i}") for i in range(2)]
        block = ctx.enter_context(nc.Block())
        turns = NBATCH // RP
        HID0, RING0, TAKEN0 = (RP - 1) * BATCH, RP - 1, products - 1

        def batch_of(turn, h):
            return Batch(turn, h, ring=RP)

        def block_of(a, b):
            m = a.h * BATCH + b
            return a.i * BATCH + b, m % RP, m % products

        @block.sync
        def _(sp):
            sp.wait_ge(zeroed, 1)

            def load(a, last=False):
                sp.wait_ge(hid, a.i * BATCH)
                load_nodes(sp, x, xin[:, a.s], a.i, loaded[a.s], last and not padded)

            def store(a):
                sp.wait_ge(taken, (a.i + 1) * BATCH + TAKEN0)
                for m, part in enumerate(parts):
                    sp.dma_start(part[0][bass.ds(a.i * (BATCH * P), BATCH * P), :].rearrange("(b p) f -> p b f", p=P),
                                 rows[m][:, a.q]).then_inc(stored[a.q], 16)

            for h in range(RP):
                load(batch_of(0, h))
            with sp.Fori(0, turns - 2) as turn:
                for h in range(RP):
                    load(batch_of(turn, h + RP))
                    store(batch_of(turn, h))
            for h in range(2 * RP):
                a = batch_of(turns - 2, h)
                if h < RP:
                    load(a.plus(RP), h == RP - 1)
                store(a)
            for q in range(2):
                sp.wait_ge(stored[q], 16 * (NBATCH // 2) * len(parts))

        def copy(eng, a, b):
            n, r, _ = block_of(a, b)
            eng.wait_ge(hid_turned, n + (1 + RING0))
            eng.wait_ge(multiplied, n)
            to = hidden_t[:, r].rearrange("p c n -> p (c n)")
            if two:
                nc.scalar.copy(to, turned[r][:, 0:F]).then_inc(copied, 1)
            else:
                eng.tensor_copy(to, turned[r][:, 0:F]).then_inc(copied, 1)

        @block.vector
        def _(dve):
            def statistics(a, b):
                if b == 0:
                    dve.wait_ge(loaded[a.s], (a.round + 1) * 32)
                last = dve.bn_stats(stats[:, a.s, b, :], xin[:, a.s, b, :])
                if b == BATCH - 1:
                    ch = Chain(dve, chain, per=2, turn=a.i)
                    ch.link(last)
                    dve.sem_inc(passed, 1)
                    for i in range(BATCH):
                        last = dve.bn_aggr(mv[:, a.s, i, :], stats[:, a.s, i, :])
                    ch.link(last)
                    dve.tensor_scalar(rstd[:, a.s], mv[:, a.s, :, 1], EPS, None, ALU.add).then_inc(variances, 1)
                    ch.close()

            def scale(a):
                ch = Chain(dve, chain_scale, per=1, turn=a.i)
                dve.wait_ge(roots, a.i + 1)
                ch.link(dve.reciprocal(rstd[:, a.s], rstd[:, a.s]))
                dve.scalar_tensor_tensor(out=shift[:, a.s], in0=mv[:, a.s, :, 0], scalar=-1.0, in1=rstd[:, a.s],
                                         op0=ALU.mult, op1=ALU.mult).then_inc(scaled, 1)
                ch.close()

            def take(a, b):
                n, _, r = block_of(a, b)
                dve.wait_ge(multiplied, n + (1 + RING0))
                if b == 0:
                    dve.wait_ge(stored[a.q], a.pairs * (16 * len(parts)))
                for m, (_, cols, _, _, bias) in enumerate(parts):
                    last = dve.tensor_tensor(rows[m][:, a.q, b, :], product[m][r][:, 0:cols], bias, ALU.add)
                last.then_inc(taken, 1)

            def first():
                dve.memset(xin[:], 0.0).then_inc(zeroed, 1)
                for h in range(2):
                    for b in range(BATCH):
                        statistics(batch_of(0, h), b)
                scale(batch_of(0, 0))
                if two:
                    dve.sem_inc(taken, TAKEN0)
                else:
                    dve.sem_inc(copied, RING0)
                    copy(dve, batch_of(0, 0), 0)

            def batch(a, after):
                for b in range(BATCH):
                    if not two:
                        ahead(lambda a, b: copy(dve, a, b), a, b, 1, after)
                    if b == 1 and after >= 1:
                        scale(a.plus(1))
                    if two:
                        take(a, b)
                    if after >= 2:
                        statistics(a.plus(2), b)

            over_batches(dve, first, batch, ring=RP)

        @block.scalar
        def _(act):
            def root(a):
                act.wait_ge(variances, a.i + 1)
                nc.scalar.activation(rstd[:, a.s], rstd[:, a.s], ACT.Sqrt).then_inc(roots, 1)

            def relu(a, b):
                n, r, _ = block_of(a, b)
                if b == 0:
                    act.wait_ge(scaled, a.i + 1)
                act.wait_ge(hid_turned, n)
                nc.scalar.activation(hidden[:, r, :], xin[:, a.s, b, :], ACT.Relu,
                                     bias=shift[:, a.s, b:b + 1], scale=rstd[:, a.s, b:b + 1]).then_inc(hid, 1)

            def take(a, b):
                n, _, r = block_of(a, b)
                act.wait_ge(multiplied, n + (1 + RING0))
                if b == 0:
                    act.wait_ge(stored[a.q], a.pairs * (16 * len(parts)))
                last = nc.scalar.copy(rows[0][:, a.q, b, :], product[0][r][:, 0:parts[0][1]])
                if er is not None:
                    last = nc.scalar.copy(er[:, bass.ds(n * HEADS, HEADS)], product[0][r][:, ROW:WCOLS])
                last.then_inc(taken, 1)

            def first():
                act.sem_inc(hid, HID0)
                for h in range(2):
                    root(batch_of(0, h))
                for b in range(3):
                    relu(batch_of(0, 0), b)
                if two:
                    act.sem_inc(copied, RING0)
                    copy(act, batch_of(0, 0), 0)
                else:
                    act.sem_inc(taken, TAKEN0)

            def batch(a, after):
                for b in range(BATCH):
                    ahead(relu, a, b, 3, after)
                    if two:
                        ahead(lambda a, b: copy(act, a, b), a, b, 1, after)
                    else:
                        take(a, b)
                if after >= 2:
                    root(a.plus(2))

            over_batches(act, first, batch, ring=RP)

        @block.tensor
        def _(pe):
            def turn_hidden(a, b):
                n, r, _ = block_of(a, b)
                pe.wait_ge(hid, n + (1 + HID0))
                pe.wait_ge(copied, n)
                for c in range(2):
                    last = nc.tensor.transpose(turned[r][:, c * P:(c + 1) * P], hidden[:, r, c * P:(c + 1) * P], k.ident[:])
                last.then_inc(hid_turned, 1)

            def multiply(a, b):
                n, r, out = block_of(a, b)
                pe.wait_ge(copied, n + (1 + RING0))
                pe.wait_ge(taken, n)
                for m, (_, _, w, cols, _) in enumerate(parts):
                    for c in range(2):
                        last = nc.tensor.matmul(product[m][out][:, 0:cols], hidden_t[:, r, c, :], w[:, c, :],
                                                start=(c == 0), stop=(c == 1))
                last.then_inc(multiplied, 1)

            def first():
                pe.sem_inc(hid_turned, RING0)
                pe.sem_inc(multiplied, RING0)
                for b in range(2):
                    turn_hidden(batch_of(0, 0), b)

            def batch(a, after):
                for b in range(BATCH):
                    ahead(turn_hidden, a, b, 2, after)
                    multiply(a, b)

            over_batches(pe, first, batch, ring=RP)


SCALE = HD ** -0.5
DB = 4
NDB = NBK // DB
DBH = DB * HEADS
DTAIL = N - (NDB - 1) * DB * P


def dot_layer(nc, k, graph, q_table, kv_table, x_in, x_out):
    KV = 2 * F
    with ExitStack() as ctx:
        s = Scope(nc, ctx, "dot")
        rows = s.sb("rows", [P, RG, DB, SLOTS, KV])
        q_rows = s.sb("q_rows", [P, 2, DB, F])
        x_rows = s.sb("x_rows", [P, 2, DB, F])
        place = s.sb("place", [P, RG, DB * SLOTS], I32)
        onehot = s.sb("onehot", [P, RG, DB * SLOTS, P])
        apart = s.sb("apart", [P, 2, PAIR])
        onehot_t = s.sb("onehot_t", [P, 2, PAIR])
        logit = s.sb("logit", [P, 2, SLOTS, DBH])
        key_bh = s.sb("key_bh", [P, 2, SLOTS, DBH])
        key_t = s.sb("key_t", [DBH, PAIR])
        wall = s.sb("wall", [DBH, PAIR + 1])
        run_max = s.sb("run_max", [DBH, PAIR])
        node_max = s.sb("node_max", [DBH, PAIR])
        below_max = s.sb("below_max", [DBH, 2, PAIR])
        total = s.sb("total", [P, 2, HEADS])
        mean = s.sb("mean", [P, 2, F])
        mean_t = s.sb("mean_t", [P, 2, 2, P])
        p_turn = s.ps("p_turn", [P, 512])
        p_q = [s.ps(f"p_q{i}", [P, 512]) for i in range(2)]
        p_soft = s.ps("p_soft", [P, 512])
        p_sum = [s.ps(f"p_sum{i}", [P, 512]) for i in range(2)]
        p_mean = s.ps("p_mean", [P, 512])
        p_next = s.ps("p_next", [P, 512])
        (placed, chain_hot, hot, hot_turned, hot_copied, spread, dotted, keyed, keys_turned, keys_copied, soft_turned, below, soft_back, weights,
         messages, summed, averaged, mean_turned, mean_copied, product, row_done, chain_dot, chain_soft,
         chain_mean, passed, passed_pe) = (s.sem(n) for n in (
             "placed", "chain_hot", "hot", "hot_turned", "hot_copied", "spread", "dotted", "keyed", "keys_turned", "keys_copied", "soft_turned", "below",
             "soft_back", "weights", "messages", "summed", "averaged", "mean_turned", "mean_copied", "product",
             "row_done", "chain_dot", "chain_soft", "chain_mean", "passed", "passed_pe"))
        gathered, before = k.pool_dma[0:RG], k.pool_count[0:RG]
        loaded = [s.sem(f"loaded{i}") for i in range(2)]
        q_loaded = [s.sem(f"q_loaded{i}") for i in range(2)]
        stored = [s.sem(f"stored{i}") for i in range(2)]
        walls_set = s.sem("walls_set")
        rows_clear = s.sem("rows_clear")
        AHEAD = RG * DB
        KEPT = RG * DB
        block = ctx.enter_context(nc.Block())

        def batch_of(i):
            return Batch(i // RG, i % RG, size=DB)

        flat_local = graph.local[:].rearrange("p (b j) -> p b j", j=SLOTS)

        @block.gpsimd
        def _(pool):
            pool.wait_ge(rows_clear, 1)

            def gather(a):
                pool.wait_ge(placed, a.i + 1)
                for b in range(DB):
                    pool.wait_ge(averaged, a.n(b)[0] + 1)
                    pool.sem_inc(passed, 1)
                    for j in range(SLOTS):
                        c = b * SLOTS + j
                        pool.indirect_dma_start(rows[:, a.s, b, j, :], None, kv_table,
                                                bass.IndirectOffsetOnAxis(place[:, a.s, c:c + 1], 0),
                                                bounds_check=N - 1, oob_is_err=False).then_inc(gathered[a.s], 16)

            with pool.Fori(0, NDB // RG) as turn:
                for h in range(RG):
                    gather(Batch(turn, h, size=DB))
            for i in range(NDB // RG * RG, NDB):
                gather(batch_of(i))
            for i in range(NDB):
                k.pool_count[i % RG] += 16 * DB * SLOTS

        @block.sync
        def _(sp):
            def load_q(a, used=None):
                if used:
                    sp.wait_ge(spread, used.i * DB + (DB + 1))
                sp.dma_start(q_rows[:, a.q], q_table[bass.ds(a.i * (DB * P), DB * P), :].rearrange(
                    "(b p) f -> p b f", p=P)).then_inc(q_loaded[a.q], 16)

            def load_x(a):
                sp.wait_ge(stored[a.q], a.pairs * 32)
                sp.dma_start(x_rows[:, a.q], x_in[bass.ds(a.i * (DB * P), DB * P), :].rearrange(
                    "(b p) f -> p b f", p=P)).then_inc(loaded[a.q], 16)

            def store(a, last=False):
                sp.wait_ge(row_done, (a.i + 1) * DB)
                m = DTAIL // P
                if last:
                    n0 = (NDB - 1) * DB * P
                    sp.dma_start(x_out[n0:n0 + m * P, :].rearrange("(b p) f -> p b f", p=P),
                                 x_rows[:, a.q, 0:m, :]).then_inc(stored[a.q], 16)
                    sp.dma_start(x_out[n0 + m * P:N, :], x_rows[0:DTAIL % P, a.q, m, :]).then_inc(stored[a.q], 16)
                else:
                    v = x_out[bass.ds(a.i * (DB * P), DB * P), :].rearrange("(b p) f -> p b f", p=P)
                    sp.dma_start(v[:, 0:m, :], x_rows[:, a.q, 0:m, :]).then_inc(stored[a.q], 16)
                    sp.dma_start(v[:, m:DB, :], x_rows[:, a.q, m:DB, :]).then_inc(stored[a.q], 16)

            def first():
                for h in range(2):
                    load_q(batch_of(h))
                load_x(batch_of(0))
                for h in range(2):
                    load_q(batch_of(h + 2), batch_of(h))

            def batch(a, after):
                if after >= 1:
                    load_x(a.plus(1))
                if after >= 4:
                    load_q(a.plus(4), a.plus(2))
                store(a, after == 0)

            over_batches(sp, first, batch, NDB, size=DB)
            for q in range(2):
                sp.wait_ge(stored[q], 32 * (NDB // 2))

        @block.vector
        def _(dve):
            def make_place(a):
                dve.wait_ge(gathered[a.s], a.round * (16 * DB * SLOTS) + before[a.s])
                dve.tensor_copy(place[:, a.s, :], graph.index[:, bass.ds(a.i * (DB * SLOTS), DB * SLOTS)]
                                ).then_inc(placed, 1)

            def multiply_q(a, b):
                n, q = a.n(b)
                if b == 0:
                    dve.wait_ge(gathered[a.s], (a.round + 1) * (16 * DB * SLOTS) + before[a.s])
                dve.wait_ge(spread, n + 2)
                kq = rows[:, a.s, b, :, 0:F]
                dve.tensor_tensor(kq, kq, p_q[q][:].rearrange("p (j f) -> p j f", j=SLOTS),
                                  ALU.mult).then_inc(chain_dot, 1)

            def sum_heads(a, b):
                n, q = a.n(b)
                dve.wait_ge(chain_dot, n + 1)
                dve.tensor_reduce(logit[:, a.q, :, b * HEADS:(b + 1) * HEADS],
                                  rows[:, a.s, b, :, 0:F].rearrange("p j (h d) -> p j h d", h=HEADS),
                                  axis=AX.X, op=ALU.add).then_inc(dotted, 1)

            def copy_keys(a):
                for j in range(SLOTS):
                    last = dve.tensor_copy(
                        key_bh[:, a.q, j, :].rearrange("p (b h) -> p b h", h=HEADS),
                        flat_local[:, bass.ds(a.i * DB, DB), j:j + 1].to_broadcast([P, DB, HEADS]))
                last.then_inc(keyed, 1)

            def take_keys(a):
                dve.wait_ge(keys_turned, a.i + 1)
                dve.tensor_copy(key_t[:], p_soft[0:DBH, PAIR:2 * PAIR]).then_inc(keys_copied, 1)

            def compare_keys(a):
                dve.wait_ge(keys_copied, a.i + 1)
                dve.tensor_tensor(wall[:, 1:PAIR], key_t[:, 1:PAIR], key_t[:, 0:PAIR - 1],
                                  ALU.is_equal).then_inc(chain_soft, 1)

            def set_walls(a):
                dve.wait_ge(chain_soft, a.i * SOFT + 1)
                dve.tensor_scalar(wall[:, 1:PAIR], wall[:, 1:PAIR], 1.0, FAR, ALU.subtract,
                                  ALU.mult).then_inc(chain_soft, 1)

            def scan_forward(a):
                dve.wait_ge(soft_turned, a.i + 1)
                dve.wait_ge(chain_soft, a.i * SOFT + 2)
                dve.tensor_tensor_scan(run_max[:], wall[:, 0:PAIR], p_soft[0:DBH, 0:PAIR], 0.0,
                                       ALU.add, ALU.max).then_inc(chain_soft, 1)

            def scan_back(a):
                dve.wait_ge(chain_soft, a.i * SOFT + 3)
                dve.tensor_tensor_scan(node_max[:, ::-1], wall[:, PAIR:0:-1], run_max[:, ::-1], 0.0,
                                       ALU.add, ALU.max).then_inc(chain_soft, 1)

            def subtract_max(a):
                dve.wait_ge(chain_soft, a.i * SOFT + 4)
                dve.tensor_tensor(below_max[:, a.q], p_soft[0:DBH, 0:PAIR], node_max[:],
                                  ALU.subtract).then_inc(below, 1)

            def weigh(a, b):
                if b == 0:
                    dve.wait_ge(weights, a.i + 1)
                v = rows[:, a.s, b, :, F:KV].rearrange("p j (h d) -> p j h d", h=HEADS)
                w = rows[:, a.s, b, :, F - HEADS:F]
                dve.tensor_tensor(v, v, w.unsqueeze(3).to_broadcast([P, SLOTS, HEADS, HD]), ALU.mult).then_inc(messages, 1)

            def take_total(a, b):
                n, q = a.n(b)
                dve.wait_ge(summed, n + (KEPT + 1))
                dve.tensor_scalar(total[:, q], p_sum[q][:, 0:HEADS], TINY, None, ALU.max).then_inc(chain_mean, 1)

            def invert_total(a, b):
                n, q = a.n(b)
                dve.wait_ge(chain_mean, n * 2 + 1)
                dve.reciprocal(total[:, q], total[:, q]).then_inc(chain_mean, 1)

            def divide(a, b):
                n, q = a.n(b)
                dve.wait_ge(chain_mean, n * 2 + 2)
                dve.wait_ge(mean_turned, n)
                dve.tensor_tensor(mean[:, q].rearrange("p (h d) -> p h d", h=HEADS),
                                  p_sum[q][:, HEADS:ROW].rearrange("p (h d) -> p h d", h=HEADS),
                                  total[:, q].unsqueeze(2).to_broadcast([P, HEADS, HD]), ALU.mult).then_inc(averaged, 1)

            def finish(a, b):
                n, q = a.n(b)
                dve.wait_ge(product, n + 2)
                if b == 0:
                    dve.wait_ge(loaded[a.q], (a.pairs + 1) * 16)
                v = x_rows[:, a.q, b, :]
                dve.tensor_tensor(v, p_next[:, 0:F], v, ALU.add).then_inc(row_done, 1)

            SOFT = 4

            def first():
                dve.memset(rows[:], 0.0).then_inc(rows_clear, 1)
                dve.wait_ge(rows_clear, 1)
                dve.memset(wall[:, 0:1], -FAR).then_inc(walls_set, 1)
                dve.memset(wall[:, PAIR:PAIR + 1], -FAR).then_inc(walls_set, 1)
                dve.wait_ge(walls_set, 2)
                dve.sem_inc(averaged, AHEAD)
                dve.sem_inc(dotted, 1)
                for h in range(RG):
                    make_place(batch_of(h))
                for h in range(2):
                    copy_keys(batch_of(h))
                for h in range(2):
                    for b in range(DB):
                        multiply_q(batch_of(h), b)
                        sum_heads(batch_of(h), b)
                a = batch_of(0)
                take_keys(a)
                compare_keys(a)
                set_walls(a)
                scan_forward(a)
                scan_back(a)
                subtract_max(a)
                take_keys(a.plus(1))
                compare_keys(a.plus(1))
                set_walls(a.plus(1))
                for b in range(2):
                    weigh(a, b)
                take_total(a, 0)
                invert_total(a, 0)
                divide(a, 0)

            def batch(a, after):
                for b in range(DB):
                    if b == 0 and after >= RG:
                        make_place(a.plus(RG))
                    if b == 1 and after >= 1:
                        subtract_max(a.plus(1))
                    ahead(weigh, a, b, 2, after)
                    ahead(take_total, a, b, 1, after)
                    if b == 0 and after >= 1:
                        scan_forward(a.plus(1))
                    if b == 1 and after >= 2:
                        copy_keys(a.plus(2))
                    if after >= 2:
                        multiply_q(a.plus(2), b)
                    if b == 3 and after >= 2:
                        take_keys(a.plus(2))
                    ahead(invert_total, a, b, 1, after)
                    if b == 0 and after >= 1:
                        scan_back(a.plus(1))
                    if b == 3 and after >= 2:
                        compare_keys(a.plus(2))
                    if after >= 2:
                        sum_heads(a.plus(2), b)
                    ahead(divide, a, b, 1, after)
                    if b == 3 and after >= 2:
                        set_walls(a.plus(2))
                    finish(a, b)

            over_batches(dve, first, batch, NDB, size=DB)

        @block.tensor
        def _(pe):
            def turn_onehot(a, b):
                n, q = a.n(b)
                pe.wait_ge(hot, n + 1)
                pe.wait_ge(hot_copied, n)
                for j in range(SLOTS):
                    last = nc.tensor.transpose(p_turn[:, j * P:(j + 1) * P], onehot[:, a.s, b * SLOTS + j, :], k.ident[:])
                last.then_inc(hot_turned, 1)

            def spread_q(a, b):
                n, q = a.n(b)
                pe.wait_ge(hot_copied, n + 1)
                pe.wait_ge(dotted, n)
                if b == 0:
                    pe.wait_ge(q_loaded[a.q], (a.pairs + 1) * 16)
                for j in range(SLOTS):
                    last = nc.tensor.matmul(p_q[q][:, j * F:(j + 1) * F], onehot_t[:, q, j * P:(j + 1) * P],
                                            q_rows[:, a.q, b, :], start=True, stop=True)
                last.then_inc(spread, 1)

            def turn_keys(a):
                pe.wait_ge(keyed, a.i + 1)
                pe.wait_ge(weights, a.i)
                pe.sem_inc(passed_pe, 1)
                for j in range(SLOTS):
                    last = nc.tensor.transpose(p_soft[0:DBH, PAIR + j * P:PAIR + (j + 1) * P], key_bh[:, a.q, j, :], k.ident[:])
                last.then_inc(keys_turned, 1)

            def turn_logits(a):
                pe.wait_ge(dotted, (a.i + 1) * DB + 1)
                pe.wait_ge(keys_copied, a.i + 1)
                pe.sem_inc(passed_pe, 1)
                for j in range(SLOTS):
                    last = nc.tensor.transpose(p_soft[0:DBH, j * P:(j + 1) * P], logit[:, a.q, j, :], k.ident[:])
                last.then_inc(soft_turned, 1)

            def turn_back(a):
                pe.wait_ge(below, a.i + 1)
                pe.sem_inc(passed_pe, 1)
                for j in range(SLOTS):
                    last = nc.tensor.transpose(p_soft[:, j * DBH:(j + 1) * DBH], below_max[:, a.q, j * P:(j + 1) * P],
                                               k.ident[0:DBH, 0:DBH])
                last.then_inc(soft_back, 1)

            def add_up(a, b):
                n, q = a.n(b)
                pe.wait_ge(messages, n + 1)
                pe.wait_ge(averaged, n + (AHEAD - 1))
                for j in range(SLOTS):
                    last = nc.tensor.matmul(p_sum[q][:, 0:ROW], onehot[:, a.s, b * SLOTS + j, :], rows[:, a.s, b, j, F - HEADS:KV],
                                            start=(j == 0), stop=(j == SLOTS - 1))
                last.then_inc(summed, 1)

            def turn_mean(a, b):
                n, q = a.n(b)
                pe.wait_ge(averaged, n + (AHEAD + 1))
                pe.wait_ge(mean_copied, n)
                for c in range(2):
                    last = nc.tensor.transpose(p_mean[:, c * P:(c + 1) * P], mean[:, q, c * P:(c + 1) * P], k.ident[:])
                last.then_inc(mean_turned, 1)

            def multiply(a, b):
                n, q = a.n(b)
                pe.wait_ge(mean_copied, n + 1)
                pe.wait_ge(row_done, n)
                for c in range(2):
                    nc.tensor.matmul(p_next[:, 0:F], mean_t[:, q, c, :], k.w_o[:, c, :], start=(c == 0), stop=False)
                nc.tensor.matmul(p_next[:, 0:F], k.ones_b[0:3, :], k.bias_parts[:],
                                 start=False, stop=True).then_inc(product, 1)

            def first():
                pe.sem_inc(summed, KEPT)
                for x in (mean_turned, product, spread):
                    pe.sem_inc(x, 1)
                for m in range(2 * DB + 1):
                    if m < 2 * DB:
                        turn_onehot(batch_of(m // DB), m % DB)
                    if m:
                        spread_q(batch_of((m - 1) // DB), (m - 1) % DB)
                a = batch_of(0)
                turn_keys(a)
                turn_logits(a)
                turn_back(a)
                turn_keys(a.plus(1))
                for b in range(2):
                    add_up(a, b)
                turn_onehot(a.plus(2), 0)
                spread_q(a.plus(2), 0)
                turn_onehot(a.plus(2), 1)

            def batch(a, after):
                for b in range(DB):
                    if b == 0 and after >= 1:
                        turn_logits(a.plus(1))
                    turn_mean(a, b)
                    if b == 1 and after >= 1:
                        turn_back(a.plus(1))
                    ahead(add_up, a, b, 2, after)
                    if b == 2 and after >= 2:
                        turn_keys(a.plus(2))
                    multiply(a, b)
                    ahead(spread_q, a.plus(2), b, 1, after - 2)
                    ahead(turn_onehot, a.plus(2), b, 2, after - 2)

            over_batches(pe, first, batch, NDB, size=DB)

        @block.scalar
        def _(act):
            def compare(a, b):
                n, q = a.n(b)
                for j in range(SLOTS):
                    last = nc.scalar.activation(apart[:, q, j * P:(j + 1) * P], k.iota_f[:, 0:P], ACT.Abs,
                                                bias=graph.local[:, bass.ds((a.i * DB + b) * SLOTS + j, 1)], scale=-1.0)
                last.then_inc(chain_hot, 1)

            def make_onehot(a, b):
                n, q = a.n(b)
                act.wait_ge(chain_hot, n + 1)
                act.wait_ge(summed, n + 1)
                nc.scalar.activation(onehot[:, a.s, b * SLOTS:(b + 1) * SLOTS, :].rearrange("p j n -> p (j n)"),
                                     apart[:, q, :], ACT.Relu, bias=k.ones[:, 0:1], scale=-1.0).then_inc(hot, 1)

            def copy_onehot(a, b):
                n, q = a.n(b)
                act.wait_ge(hot_turned, n + 1)
                act.wait_ge(spread, n)
                nc.scalar.copy(onehot_t[:, q, :], p_turn[:, 0:PAIR]).then_inc(hot_copied, 1)

            def exponentiate(a):
                act.wait_ge(soft_back, a.i + 1)
                for j in range(SLOTS):
                    last = nc.scalar.activation(
                        rows[:, a.s, :, j, F - HEADS:F],
                        p_soft[:, j * DBH:(j + 1) * DBH].rearrange("p (b h) -> p b h", h=HEADS), ACT.Exp, scale=SCALE)
                last.then_inc(weights, 1)

            def copy_mean(a, b):
                n, q = a.n(b)
                act.wait_ge(mean_turned, n + 2)
                act.wait_ge(product, n)
                nc.scalar.copy(mean_t[:, q].rearrange("p c n -> p (c n)"), p_mean[:, 0:F]).then_inc(mean_copied, 1)

            def first():
                for m in range(2 * DB):
                    compare(batch_of(m // DB), m % DB)
                    make_onehot(batch_of(m // DB), m % DB)
                    copy_onehot(batch_of(m // DB), m % DB)
                exponentiate(batch_of(0))
                for b in range(2):
                    compare(batch_of(2), b)
                    make_onehot(batch_of(2), b)
                    copy_onehot(batch_of(2), b)
                compare(batch_of(2), 2)

            def batch(a, after):
                for b in range(DB):
                    copy_mean(a, b)
                    if b == 1 and after >= 1:
                        exponentiate(a.plus(1))
                    ahead(compare, a.plus(2), b, 3, after - 2)
                    ahead(make_onehot, a.plus(2), b, 2, after - 2)
                    ahead(copy_onehot, a.plus(2), b, 2, after - 2)

            over_batches(act, first, batch, NDB, size=DB)


STATE = ROW + HEADS


def any_degrees_layer(nc, k, tag, keys, others, table, side, finish, scale=None):
    dot = scale is not None
    cols, side_cols, at = (2 * F, F, F) if dot else (ROW, HEADS, 0)
    state = nc.dram_tensor(f"{tag}_state", (NP, STATE), F32, kind="Internal").ap()
    with ExitStack() as ctx:
        s = Scope(nc, ctx, tag)
        key_i = s.sb("key", [P, T], I32)
        oth_i = s.sb("oth", [P, T], I32)
        ask = s.sb("ask", [P, 3], I32)
        key_f = s.sb("key_f", [P, 1])
        later = s.sb("later", [P, P])
        empty = s.sb("empty", [P, BATCH, STATE])
        rows = s.sb("rows", [P, cols])
        mine = s.sb("mine", [P, side_cols])
        old = s.sb("old", [P, STATE])
        new = s.sb("new", [P, STATE])
        diag = s.sb("diag", [P, P])
        diags = s.sb("diags", [P, HEADS, P])
        same = s.sb("same", [P, P])
        apart = s.sb("apart", [P, P])
        masked = s.sb("masked", [P, HEADS, P])
        count = s.sb("count", [P, 1])
        logit = s.sb("logit", [P, HEADS])
        diffs = s.sb("diffs", [P, 2, HEADS])
        powers = s.sb("powers", [P, HEADS])
        message = s.sb("message", [P, ROW])
        p_key = s.ps("p_key", [P, 512])
        p_logit = [s.ps(f"p_logit{i}", [P, 512]) for i in range(2)]
        p_sum = s.ps("p_sum", [P, 512])
        (loaded, cleared, emptied, chain, asked, diag_ready, key_spread, logits, logits_spread, maxima, powered,
         messages, summed, updated, passed) = (s.sem(n) for n in (
             "loaded", "cleared", "emptied", "chain", "asked", "diag_ready", "key_spread", "logits",
             "logits_spread", "maxima", "powered", "messages", "summed", "updated", "passed"))
        arrived, before = k.pool_dma, list(k.pool_count)
        block = ctx.enter_context(nc.Block())
        full, rest = E // T, E % T

        @block.sync
        def _(sp):
            sp.wait_ge(cleared, 1)
            for to, of in ((key_i, keys), (oth_i, others)):
                for lo, hi in ((0, 112), (112, full)):
                    sp.dma_start(to[lo:hi, :], of[lo * T:hi * T].rearrange("(p t) -> p t", t=T)).then_inc(loaded, 16)
                sp.dma_start(to[full:full + 1, 0:rest],
                             of[full * T:E].rearrange("(p t) -> p t", p=1)).then_inc(loaded, 16)
            for i in range(NBATCH):
                sp.dma_start(state[i * BATCH * P:(i + 1) * BATCH * P, :].rearrange("(b p) c -> p b c", p=P),
                             empty[:]).then_inc(emptied, 16)
            sp.wait_ge(emptied, 16 * NBATCH)

        @block.gpsimd
        def _(pool):
            pool.wait_ge(emptied, 16 * NBATCH)
            with pool.Fori(0, T) as t:
                pool.wait_ge(arrived[3], t * 16 + before[3])
                pool.wait_ge(asked, t + 1)
                pool.sem_inc(passed, 1)
                for i, (to, of, c, bound) in enumerate(((old, state, 0, NP), (rows, table, 1, N), (mine, side, 0, NP))):
                    pool.indirect_dma_start(to[:], None, of, bass.IndirectOffsetOnAxis(ask[:, c:c + 1], 0),
                                            bounds_check=bound - 1, oob_is_err=False).then_inc(arrived[i], 16)
                pool.wait_ge(updated, t + 1)
                pool.sem_inc(passed, 1)
                pool.indirect_dma_start(state, bass.IndirectOffsetOnAxis(ask[:, 2:3], 0), new[:], None,
                                        bounds_check=NP - 1, oob_is_err=False).then_inc(arrived[3], 16)
            pool.wait_ge(arrived[3], T * 16 + before[3])
            for i in range(4):
                k.pool_count[i] += T * 16

        @block.vector
        def _(dve):
            ch = Chain(dve, chain)
            dve.memset(key_i[:], (NBK - 1) * P)
            dve.memset(oth_i[:], 0)
            ch.link(dve.memset(empty[:, :, 0:ROW], 0.0))
            ch.link(dve.memset(empty[:, :, ROW:STATE], -FAR))
            dve.sem_inc(cleared, 1)
            ch.link(dve.tensor_tensor(later[:], k.ones[:], k.tri_f[:], ALU.subtract))
            ch.link(dve.tensor_tensor(later[:], later[:], k.ident[:], ALU.subtract))
            dve.wait_ge(loaded, 16 * 6)
            base, PER = ch.k, (15 if dot else 14)
            with dve.Fori(0, T) as t:
                ch = Chain(dve, chain, per=PER, turn=t, base=base)
                dve.wait_ge(arrived[3], t * 16 + before[3])
                dve.tensor_copy(ask[:, 0:1], key_i[:, bass.ds(t, 1)])
                dve.tensor_copy(ask[:, 1:2], oth_i[:, bass.ds(t, 1)]).then_inc(asked, 1)
                ch.link(dve.tensor_copy(key_f[:], key_i[:, bass.ds(t, 1)]))
                dve.tensor_scalar(diag[:], k.ident[:], key_f[:], None, ALU.mult).then_inc(diag_ready, 1)
                dve.wait_ge(key_spread, t + 1)
                ch.link(dve.tensor_scalar(same[:], p_key[:, 0:P], key_f[:], None, ALU.is_equal))
                ch.link(dve.tensor_scalar(apart[:], same[:], 1.0, FAR, ALU.subtract, ALU.mult))
                ch.link(dve.tensor_tensor(diag[:], same[:], later[:], ALU.mult))
                ch.link(dve.tensor_reduce(count[:], diag[:], axis=AX.X, op=ALU.add))
                ch.link(dve.tensor_scalar(count[:], count[:], 0.5, float(1 << 20), ALU.is_ge, ALU.mult))
                ch.link(dve.tensor_tensor(ask[:, 2:3], count[:], key_f[:], ALU.add))
                for i in range(3):
                    dve.wait_ge(arrived[i], (t + 1) * 16 + before[i])
                if dot:
                    ch.link(dve.tensor_tensor(rows[:, 0:F], rows[:, 0:F], mine[:], ALU.mult))
                    ch.link(dve.tensor_reduce(logit[:], rows[:, 0:F].rearrange("p (h d) -> p h d", h=HEADS),
                                              axis=AX.X, op=ALU.add))
                    ch.link(dve.tensor_scalar(logit[:], logit[:], scale, None, ALU.mult))
                else:
                    ch.link(dve.tensor_tensor(logit[:], rows[:, F:ROW], mine[:], ALU.add))
                    ch.link(dve.scalar_tensor_tensor(out=logit[:], in0=logit[:], scalar=SLOPE_ATTN, in1=logit[:],
                                                     op0=ALU.mult, op1=ALU.max))
                dve.tensor_tensor(diags[:], k.ident[:].unsqueeze(1).to_broadcast([P, HEADS, P]),
                                  logit[:].unsqueeze(2).to_broadcast([P, HEADS, P]), ALU.mult).then_inc(logits, 1)
                dve.wait_ge(logits_spread, t + 1)
                half = HEADS // 2
                for i in range(2):
                    last = dve.tensor_tensor(masked[:, i * half:(i + 1) * half, :],
                                             p_logit[i][:].rearrange("p (h e) -> p h e", h=half),
                                             apart[:].unsqueeze(1).to_broadcast([P, half, P]), ALU.add)
                ch.link(last)
                ch.link(dve.tensor_reduce(powers[:], masked[:], axis=AX.X, op=ALU.max))
                ch.link(dve.tensor_tensor(new[:, ROW:STATE], powers[:], old[:, ROW:STATE], ALU.max))
                dve.tensor_tensor(diffs[:, 0], old[:, ROW:STATE], new[:, ROW:STATE], ALU.subtract)
                dve.tensor_tensor(diffs[:, 1], logit[:], new[:, ROW:STATE], ALU.subtract).then_inc(maxima, 1)
                dve.wait_ge(powered, t + 1)
                v = rows[:, at:at + F].rearrange("p (h d) -> p h d", h=HEADS)
                dve.tensor_tensor(message[:, HEADS:ROW].rearrange("p (h d) -> p h d", h=HEADS), v,
                                  message[:, 0:HEADS].unsqueeze(2).to_broadcast([P, HEADS, HD]),
                                  ALU.mult).then_inc(messages, 1)
                dve.tensor_tensor(old[:, 0:HEADS], old[:, 0:HEADS], powers[:], ALU.mult)
                o = old[:, HEADS:ROW].rearrange("p (h d) -> p h d", h=HEADS)
                ch.link(dve.tensor_tensor(o, o, powers[:].unsqueeze(2).to_broadcast([P, HEADS, HD]), ALU.mult))
                dve.wait_ge(summed, t + 1)
                ch.link(dve.tensor_tensor(new[:, 0:ROW], p_sum[:, 0:ROW], old[:, 0:ROW], ALU.add))
                dve.sem_inc(updated, 1)
                ch.close()

        @block.tensor
        def _(pe):
            with pe.Fori(0, T) as t:
                pe.wait_ge(diag_ready, t + 1)
                nc.tensor.matmul(p_key[:, 0:P], k.ones[:], diag[:], start=True, stop=True).then_inc(key_spread, 1)
                pe.wait_ge(logits, t + 1)
                half = HEADS // 2
                for i in range(2):
                    last = nc.tensor.matmul(p_logit[i][:], k.ones[:], diags[:, i * half:(i + 1) * half, :],
                                            start=True, stop=True)
                last.then_inc(logits_spread, 1)
                pe.wait_ge(messages, t + 1)
                nc.tensor.matmul(p_sum[:, 0:ROW], same[:], message[:], start=True, stop=True).then_inc(summed, 1)

        @block.scalar
        def _(act):
            with act.Fori(0, T) as t:
                act.wait_ge(maxima, t + 1)
                nc.scalar.activation(powers[:], diffs[:, 0], ACT.Exp)
                nc.scalar.activation(message[:, 0:HEADS], diffs[:, 1], ACT.Exp).then_inc(powered, 1)

    finish(state)


def write_er(nc, k, layer, er_table):
    with ExitStack() as ctx:
        s = Scope(nc, ctx, f"er_rows{layer}")
        written = s.sem("written")
        block = ctx.enter_context(nc.Block())

        @block.sync
        def _(sp):
            sp.dma_start(er_table.rearrange("(b p) h -> p b h", p=P),
                         k.er[:].rearrange("p (b h) -> p b h", h=HEADS)).then_inc(written, 16)
            sp.wait_ge(written, 16)


def finish_nodes(nc, k, tag, state, kind, layer=0, table_out=None, x_in=None, x_out=None):
    with ExitStack() as ctx:
        s = Scope(nc, ctx, tag)
        st = s.sb("st", [P, STATE])
        total = s.sb("total", [P, HEADS])
        mean = s.sb("mean", [P, F])
        mean_t = s.sb("mean_t", [P, 2, P])
        x_row = s.sb("x_row", [P, F])
        out_row = s.sb("out_row", [P, ROW])
        p_mean = s.ps("p_mean", [P, 512])
        p_next = s.ps("p_next", [P, 512])
        loaded, x_loaded, x_cleared, chain, divided, turned, copied, product, made, stored = (s.sem(n) for n in (
            "loaded", "x_loaded", "x_cleared", "chain", "divided", "turned", "copied", "product", "made", "stored"))
        block = ctx.enter_context(nc.Block())
        full = N // P
        ends = [(full, N - full * P), (full + 1, 0)]
        out = table_out if kind == "table" else x_out
        width = ROW if kind == "table" else F
        padded = out.shape[0] == NP
        use_x = kind != "table"

        def each(eng, one):
            with eng.Fori(0, full) as b:
                one(b, P)
            for b, have in ends:
                one(b, have)

        @block.sync
        def _(sp):
            sp.wait_ge(x_cleared, 1)

            def one(b, have):
                sp.wait_ge(stored, b * 16)
                sp.dma_start(st[:], state[bass.ds(b * P, P), :]).then_inc(loaded, 16)
                if use_x and (have or x_in.shape[0] == NP):
                    n = P if x_in.shape[0] == NP else have
                    sp.dma_start(x_row[0:n, :], x_in[bass.ds(b * P, n), :]).then_inc(x_loaded, 16)
                elif use_x:
                    sp.sem_inc(x_loaded, 16)
                sp.wait_ge(made, b + 1)
                n = P if padded else have
                if n:
                    sp.dma_start(out[bass.ds(b * P, n), :], out_row[0:n, 0:width]).then_inc(stored, 16)
                    if not isinstance(b, int) or b < full + (1 if padded else 0):
                        return
                    sp.wait_ge(stored, (b + 1) * 16)
                else:
                    sp.sem_inc(stored, 16)

            each(sp, one)

        @block.vector
        def _(dve):
            dve.memset(x_row[:], 0.0).then_inc(x_cleared, 1)
            PER = {"table": 3, "sum": 4, "product": 3}[kind]

            def one(b, have):
                ch = Chain(dve, chain, per=PER, turn=b)
                dve.wait_ge(loaded, (b + 1) * 16)
                ch.link(dve.tensor_scalar(total[:], st[:, 0:HEADS], TINY, None, ALU.max))
                ch.link(dve.reciprocal(total[:], total[:]))
                ins = dve.tensor_tensor(mean[:].rearrange("p (h d) -> p h d", h=HEADS),
                                        st[:, HEADS:ROW].rearrange("p (h d) -> p h d", h=HEADS),
                                        total[:].unsqueeze(2).to_broadcast([P, HEADS, HD]), ALU.mult)
                ch.link(ins)
                dve.sem_inc(divided, 1)
                if use_x:
                    dve.wait_ge(x_loaded, (b + 1) * 16)
                if kind == "sum":
                    ch.link(dve.tensor_tensor(mean[:], mean[:], k.b2_row[:], ALU.add))
                    dve.tensor_tensor(out_row[:, 0:F], mean[:], x_row[:], ALU.add).then_inc(made, 1)
                if kind == "table":
                    dve.wait_ge(turned, (b + 1) * 2)
                    v = mean_t[:].rearrange("p c n -> p (c n)")
                    dve.scalar_tensor_tensor(out=v, in0=v, scalar=SLOPE_ACT, in1=v,
                                             op0=ALU.mult, op1=ALU.max).then_inc(copied, 1)
                if kind == "product":
                    dve.wait_ge(product, b + 1)
                    dve.tensor_tensor(out_row[:, 0:F], p_next[:, 0:F], x_row[:], ALU.add).then_inc(made, 1)
                ch.close()

            each(dve, one)

        @block.tensor
        def _(pe):
            def one(b, have):
                pe.wait_ge(divided, b + 1)
                for c in range(2):
                    last = nc.tensor.transpose(p_mean[:, c * P:(c + 1) * P], mean[:, c * P:(c + 1) * P], k.ident[:])
                last.then_inc(turned, 1)
                pe.wait_ge(copied, b + 1)
                w = k.w_gat[:, layer + 1] if kind == "table" else k.w_o
                cols = WCOLS if kind == "table" else F
                for c in range(2):
                    last = nc.tensor.matmul(p_next[:, 0:cols], mean_t[:, c, :], w[:, c, :],
                                            start=(c == 0), stop=(c == 1 and kind == "table"))
                if kind == "product":
                    last = nc.tensor.matmul(p_next[:, 0:cols], k.ones_b[0:3, :], k.bias_parts[:],
                                            start=False, stop=True)
                last.then_inc(product, 1)

            if kind != "sum":
                each(pe, one)

        @block.scalar
        def _(act):
            def one(b, have):
                if kind == "table":
                    act.wait_ge(turned, b * 2 + 1)
                    for c in range(2):
                        last = nc.scalar.activation(mean_t[:, c, :], p_mean[:, c * P:(c + 1) * P], ACT.Identity,
                                                    bias=k.b_col[:, layer, c:c + 1])
                    last.then_inc(turned, 1)
                    act.wait_ge(product, b + 1)
                    nc.scalar.copy(out_row[:], p_next[:, 0:ROW])
                    nc.scalar.copy(k.er[:, bass.ds(b * HEADS, HEADS)], p_next[:, ROW:WCOLS]).then_inc(made, 1)
                else:
                    act.wait_ge(turned, b + 1)
                    nc.scalar.copy(mean_t[:].rearrange("p c n -> p (c n)"), p_mean[:, 0:F]).then_inc(copied, 1)

            if kind != "sum":
                each(act, one)


FITS = 0


def gnn_kernel(nc, x, src, dst, W, al, ar, b, w_qkv, b_qkv, w_o, b_o, out):
    with ExitStack() as ctx:
        s = Scope(nc, ctx, "kept")
        k = Constants(s)
        k.w_gat = s.sb("w_gat", [P, 3, 2, WCOLS])
        k.b_col = s.sb("b_col", [P, 3, 2])
        k.b2_row = s.sb("b2_row", [P, F])
        k.w_qkv = s.sb("w_qkv", [P, 2, 3 * F])
        k.w_o = s.sb("w_o", [P, 2, F])
        k.b_qkv_row = s.sb("b_qkv_row", [P, 3 * F])
        k.bias_parts = s.sb("bias_parts", [3, F], BF16)
        k.er = s.sb("er", [P, NBK * HEADS])
        index = [s.sb(f"index{g}", [P, NBK * SLOTS], I32) for g in range(2)]
        local = [s.sb(f"local{g}", [P, NBK * SLOTS]) for g in range(2)]
        places = [nc.dram_tensor(f"places{g}", (SP_ROWS, 2), I32, kind="Internal").ap() for g in range(2)]
        tables = [nc.dram_tensor(f"table{i}", (NP, ROW), F32, kind="Internal").ap() for i in range(2)]
        x2 = nc.dram_tensor("x2", (NP, F), F32, kind="Internal").ap()
        er_table = nc.dram_tensor("er_table", (NP, HEADS), F32, kind="Internal").ap()
        q_table = nc.dram_tensor("q_table", (NP, F), F32, kind="Internal").ap()
        kv_table = nc.dram_tensor("kv_table", (NP, 2 * F), F32, kind="Internal").ap()

        make_constants(nc, k)
        load_weights(nc, k, W, al, ar, b, w_qkv, b_qkv, w_o, b_o)
        distribute(nc, k, [dst, src], [src, dst], places)
        sort_buckets(nc, k, places, index, local)
        by_dst, by_src = (Graph(index[g], local[g]) for g in range(2))
        project(nc, k, "first", x, [(tables[0], ROW, k.w_gat[:, 0], WCOLS, None)], k.er)

        crowded = nc.values_load(k.crowded[0:1, 0:1].bitcast(mybir.dt.uint32), min_val=0, max_val=1)
        dealt = list(k.pool_count)
        with nc.If(crowded == FITS):
            gat_layer(nc, k, by_dst, tables[0], 0, tables[1])
            gat_layer(nc, k, by_dst, tables[1], 1, tables[0])
            last_gat_layer(nc, k, by_dst, tables[0], x, x2)
        if_fit, k.pool_count = k.pool_count, dealt
        with nc.Else():
            for layer in range(3):
                write_er(nc, k, layer, er_table)
                kind = "sum" if layer == 2 else "table"
                any_degrees_layer(nc, k, f"any{layer}", dst, src, tables[layer % 2], er_table,
                                  lambda state: finish_nodes(nc, k, f"end{layer}", state, kind, layer,
                                                             tables[(layer + 1) % 2], x, x2))
        project(nc, k, "qkv", x2, [(q_table, F, k.w_qkv[:, :, 0:F], F, k.b_qkv_row[:, 0:F]),
                                   (kv_table, 2 * F, k.w_qkv[:, :, F:3 * F], 2 * F, k.b_qkv_row[:, F:3 * F])])
        if_crowded, k.pool_count = k.pool_count, if_fit
        with nc.If(crowded == FITS):
            dot_layer(nc, k, by_src, q_table, kv_table, x2, out)
        k.pool_count = if_crowded
        with nc.Else():
            any_degrees_layer(nc, k, "any3", src, dst, kv_table, q_table,
                              lambda state: finish_nodes(nc, k, "end3", state, "product", x_in=x2, x_out=out), SCALE)


def kernel(x, src, dst, L0_gnn_W, L0_gnn_al, L0_gnn_ar, L0_gnn_b, L1_gnn_Wq, L1_gnn_bq, L1_gnn_Wk, L1_gnn_bk,
           L1_gnn_Wv, L1_gnn_bv, L1_gnn_Wo, L1_gnn_bo):
    import numpy as np
    import concourse.bacc as bacc
    from concourse.bass_utils import run_bass_kernel_spmd

    def head_major(a):
        a = np.asarray(a)
        return a.reshape(a.shape[:-1] + (HD, HEADS)).swapaxes(-1, -2).reshape(a.shape)

    w_qkv = np.concatenate([head_major(np.asarray(w).T) for w in (L1_gnn_Wq, L1_gnn_Wk, L1_gnn_Wv)], axis=1)
    b_qkv = np.concatenate([head_major(b) for b in (L1_gnn_bq, L1_gnn_bk, L1_gnn_bv)])
    given = {
        "x": x, "src": src, "dst": dst, "W": L0_gnn_W, "al": L0_gnn_al, "ar": L0_gnn_ar, "b": L0_gnn_b,
        "w_qkv": w_qkv, "b_qkv": b_qkv, "w_o": head_major(L1_gnn_Wo).T, "b_o": L1_gnn_bo,
    }
    nc = bacc.Bacc("TRN2", target_bir_lowering=False, num_devices=1)
    arrays, args = {}, []
    for name, a in given.items():
        a = np.ascontiguousarray(a)
        arrays[f"in_{name}"] = a
        args.append(nc.dram_tensor(f"in_{name}", a.shape, mybir.dt.from_np(a.dtype), kind="ExternalInput").ap())
    out = nc.dram_tensor("out_0", (N, F), F32, kind="ExternalOutput").ap()
    gnn_kernel(nc, *args, out)
    return run_bass_kernel_spmd(nc, [arrays], core_ids=[0]).results[0]["out_0"]
```
